# Optimizing a Trainium2 kernel written in Bass

```python
import numpy as np
import jax
import jax.numpy as jnp

def _softmax(x, axis=-1):
    return jax.nn.softmax(x, axis=axis)

def _gelu(x):
    return jax.nn.gelu(x, approximate=True)

def _silu(x):
    return jax.nn.silu(x)

def _sigmoid(x):
    return jax.nn.sigmoid(x)

def _layernorm(x, axis=-1, eps=1e-05):
    m = jnp.mean(x, axis=axis, keepdims=True)
    v = jnp.var(x, axis=axis, keepdims=True)
    return (x - m) / jnp.sqrt(v + eps)

def _scatter_add(tgt, idx, src, axis=0):
    return tgt.at[idx].add(src)

def _segment_sum(src, seg, n):
    return jax.ops.segment_sum(src, seg, n)
kernel_name = 'mk_seq_preln_d1_jaxref_r4_0067f9'

def setup_inputs(seed: int=0):
    np.random.seed(seed)
    _w = jnp.asarray

    def _L0_attn_setup():
        import jax, jax.numpy as jnp
        import numpy as np
        D_MODEL = 256
        D_STATE = 16
        D_CONV = 4
        EXPAND = 2
        D_INNER = D_MODEL * EXPAND
        BATCH = 4
        SEQ_LEN = 1024

        def _silu(v):
            return v * jax.nn.sigmoid(v)
        key = jax.random.key(seed)
        ks = jax.random.split(key, 6)

        def rn(k, shape, scale):
            return jax.random.normal(k, shape, dtype=jnp.float32) * scale
        x = rn(ks[0], (BATCH, SEQ_LEN, D_MODEL), 1.0)
        in_proj_w = rn(ks[1], (2 * D_INNER, D_MODEL), D_MODEL ** (-0.5))
        conv_w = rn(ks[2], (D_INNER, 1, D_CONV), D_CONV ** (-0.5))
        conv_b = rn(ks[3], (D_INNER,), 0.02)
        x_proj_w = rn(ks[4], (2 * D_STATE + 1, D_INNER), D_INNER ** (-0.5))
        A_log = jnp.log(jnp.arange(1, D_STATE + 1, dtype=jnp.float32))
        D = jnp.ones((D_INNER,), jnp.float32)
        out_proj_w = rn(ks[5], (D_MODEL, D_INNER), D_INNER ** (-0.5))
        return dict(x=x, in_proj_w=in_proj_w, conv_w=conv_w, conv_b=conv_b, x_proj_w=x_proj_w, A_log=A_log, D=D, out_proj_w=out_proj_w)
    _L0_attn_in = _L0_attn_setup()

    def _L0_ffn_setup():
        import jax, jax.numpy as jnp
        import numpy as np
        D_MODEL = 256
        EXPANSION = 4
        D_HIDDEN = D_MODEL * EXPANSION
        NUM_STAGES = int(np.log2(D_HIDDEN))

        def butterfly(y, weights, dim):
            lead = y.shape[:-1]
            for stage in range(weights.shape[0]):
                s = 2 ** stage
                nb = dim // (2 * s)
                yr = y.reshape(*lead, nb, 2, s)
                a = yr[..., 0, :]
                b = yr[..., 1, :]
                w = weights[stage].reshape(nb, s, 2, 2)
                na = w[..., 0, 0] * a + w[..., 0, 1] * b
                nb2 = w[..., 1, 0] * a + w[..., 1, 1] * b
                y = jnp.stack([na, nb2], axis=-2).reshape(*lead, dim)
            return y
        key = jax.random.key(seed)
        ks = jax.random.split(key, 6)
        B, S = (4, 512)
        x = jax.random.normal(ks[0], (B, S, D_MODEL), jnp.float32)
        W_exp = jax.random.normal(ks[1], (D_MODEL, D_HIDDEN), jnp.float32) * 0.02
        b_exp = jnp.zeros((D_HIDDEN,), jnp.float32)
        up_weights = jax.random.normal(ks[2], (NUM_STAGES, D_HIDDEN // 2, 2, 2), jnp.float32) * 0.02
        up_bias = jnp.zeros((D_HIDDEN,), jnp.float32)
        down_weights = jax.random.normal(ks[3], (NUM_STAGES, D_HIDDEN // 2, 2, 2), jnp.float32) * 0.02
        W_con = jax.random.normal(ks[4], (D_HIDDEN, D_MODEL), jnp.float32) * 0.02
        b_con = jnp.zeros((D_MODEL,), jnp.float32)
        down_bias = jnp.zeros((D_MODEL,), jnp.float32)
        return dict(x=x, W_exp=W_exp, b_exp=b_exp, up_weights=up_weights, up_bias=up_bias, down_weights=down_weights, W_con=W_con, b_con=b_con, down_bias=down_bias)
    _L0_ffn_in = _L0_ffn_setup()
    _d = {'L0_attn_x': _L0_attn_in['x'], 'L0_attn_in_proj_w': _L0_attn_in['in_proj_w'], 'L0_attn_conv_w': _L0_attn_in['conv_w'], 'L0_attn_conv_b': _L0_attn_in['conv_b'], 'L0_attn_x_proj_w': _L0_attn_in['x_proj_w'], 'L0_attn_A_log': _L0_attn_in['A_log'], 'L0_attn_D': _L0_attn_in['D'], 'L0_attn_out_proj_w': _L0_attn_in['out_proj_w'], 'L0_ffn_W_exp': _L0_ffn_in['W_exp'], 'L0_ffn_b_exp': _L0_ffn_in['b_exp'], 'L0_ffn_up_weights': _L0_ffn_in['up_weights'], 'L0_ffn_up_bias': _L0_ffn_in['up_bias'], 'L0_ffn_down_weights': _L0_ffn_in['down_weights'], 'L0_ffn_W_con': _L0_ffn_in['W_con'], 'L0_ffn_b_con': _L0_ffn_in['b_con'], 'L0_ffn_down_bias': _L0_ffn_in['down_bias']}
    _x0 = _d['L0_attn_x']
    _d['L0_attn_x'] = jax.random.normal(jax.random.fold_in(jax.random.key(seed), 1), (2, 2048, 256), dtype=_x0.dtype)
    del _x0
    return _d

def reference(L0_attn_x, L0_attn_in_proj_w, L0_attn_conv_w, L0_attn_conv_b, L0_attn_x_proj_w, L0_attn_A_log, L0_attn_D, L0_attn_out_proj_w, L0_ffn_W_exp, L0_ffn_b_exp, L0_ffn_up_weights, L0_ffn_up_bias, L0_ffn_down_weights, L0_ffn_W_con, L0_ffn_b_con, L0_ffn_down_bias):

    def _L0_attn_ref(x, in_proj_w, conv_w, conv_b, x_proj_w, A_log, D, out_proj_w):
        import jax, jax.numpy as jnp
        import numpy as np
        D_MODEL = 256
        D_STATE = 16
        D_CONV = 4
        EXPAND = 2
        D_INNER = D_MODEL * EXPAND
        BATCH = 4
        SEQ_LEN = 1024

        def _silu(v):
            return v * jax.nn.sigmoid(v)
        b, l, _ = x.shape
        xz = jnp.einsum('bld,ed->ble', x, in_proj_w)
        x_inner, z = jnp.split(xz, 2, axis=-1)
        xc = jnp.transpose(x_inner, (0, 2, 1))
        xc = jax.lax.conv_general_dilated(xc, conv_w, window_strides=(1,), padding=[(D_CONV - 1, 0)], feature_group_count=D_INNER, dimension_numbers=('NCH', 'OIH', 'NCH'))
        xc = xc + conv_b[None, :, None]
        x_conv = _silu(jnp.transpose(xc, (0, 2, 1)))
        x_dbl = jnp.einsum('bld,ed->ble', x_conv, x_proj_w)
        delta = jax.nn.softplus(x_dbl[..., 0])
        B_ssm = x_dbl[..., 1:D_STATE + 1]
        C_ssm = x_dbl[..., D_STATE + 1:]
        A = -jnp.exp(A_log)

        def step(h, inp):
            x_t, d_t, B_t, C_t = inp
            dA = jnp.exp(d_t[:, None, None] * A)
            dB = d_t[:, None, None] * B_t[:, None, :]
            h = h * dA + x_t[:, :, None] * dB
            y_t = jnp.einsum('bdn,bn->bd', h, C_t)
            return (h, y_t)
        h0 = jnp.zeros((b, D_INNER, D_STATE), x.dtype)
        xs = (jnp.swapaxes(x_conv, 0, 1), jnp.swapaxes(delta, 0, 1), jnp.swapaxes(B_ssm, 0, 1), jnp.swapaxes(C_ssm, 0, 1))
        _, ys = jax.lax.scan(step, h0, xs)
        y = jnp.swapaxes(ys, 0, 1)
        y = y + x_conv * D
        y = y * _silu(z)
        return jnp.einsum('bld,od->blo', y, out_proj_w)

    def _L0_ffn_ref(x, W_exp, b_exp, up_weights, up_bias, down_weights, W_con, b_con, down_bias):
        import jax, jax.numpy as jnp
        import numpy as np
        D_MODEL = 256
        EXPANSION = 4
        D_HIDDEN = D_MODEL * EXPANSION
        NUM_STAGES = int(np.log2(D_HIDDEN))

        def butterfly(y, weights, dim):
            lead = y.shape[:-1]
            for stage in range(weights.shape[0]):
                s = 2 ** stage
                nb = dim // (2 * s)
                yr = y.reshape(*lead, nb, 2, s)
                a = yr[..., 0, :]
                b = yr[..., 1, :]
                w = weights[stage].reshape(nb, s, 2, 2)
                na = w[..., 0, 0] * a + w[..., 0, 1] * b
                nb2 = w[..., 1, 0] * a + w[..., 1, 1] * b
                y = jnp.stack([na, nb2], axis=-2).reshape(*lead, dim)
            return y
        h = jnp.einsum('bsd,dh->bsh', x, W_exp) + b_exp
        h = butterfly(h, up_weights, D_HIDDEN)
        h = jax.nn.gelu(h + up_bias, approximate=False)
        h = butterfly(h, down_weights, D_HIDDEN)
        y = jnp.einsum('bsh,hd->bsd', h, W_con) + b_con
        return y + down_bias
    x = L0_attn_x
    x = x + _L0_attn_ref(_layernorm(x, axis=-1), L0_attn_in_proj_w, L0_attn_conv_w, L0_attn_conv_b, L0_attn_x_proj_w, L0_attn_A_log, L0_attn_D, L0_attn_out_proj_w)
    x = x + _L0_ffn_ref(_layernorm(x, axis=-1), L0_ffn_W_exp, L0_ffn_b_exp, L0_ffn_up_weights, L0_ffn_up_bias, L0_ffn_down_weights, L0_ffn_W_con, L0_ffn_b_con, L0_ffn_down_bias)
    return x

_drawn_inputs = setup_inputs


def setup_inputs(seed=0):
    import zlib

    import numpy as np

    out = dict(_drawn_inputs(seed))
    spreads = {'L0_attn_D': (1.0, 0.2),
     'L0_ffn_b_exp': (0.0, 0.1),
     'L0_ffn_up_bias': (0.0, 0.1),
     'L0_ffn_b_con': (0.0, 0.1),
     'L0_ffn_down_bias': (0.0, 0.1)}
    factors = {'L0_attn_conv_b': 4.198}
    for name, (base, spread) in spreads.items():
        noise = np.random.default_rng([zlib.crc32(name.encode()), seed]).standard_normal(out[name].shape)
        drawn = base * np.exp(spread * noise) if base else spread * noise
        out[name] = jnp.asarray(drawn.astype(out[name].dtype))
    for name, factor in factors.items():
        out[name] = (out[name] * factor).astype(out[name].dtype)
    return out
```

```python
from contextlib import ExitStack

import concourse.bass as bass
from concourse import mybir

F32 = mybir.dt.float32
ALU = mybir.AluOpType
ACT = mybir.ActivationFunctionType
AXIS_X = mybir.AxisListType.X

P = 128
BATCH = 2
LENGTH = 2048
DM = 256
DI = 512
NS = 16
TAPS = 4
HID = 1024
TILE = 512
TILES = LENGTH // TILE
GR = TILE // P
MB = DM // P
CB = DI // P
HB = HID // P
BL = 16
NB = P // BL
HALO = TAPS - 1
XD = 1 + 2 * NS
SLOT = 32
LOW = 7
HIGH = 3
EPS = 1e-5
ATANH = [1 / 11, 1 / 9, 1 / 7, 1 / 5, 1 / 3]

WIDE_ORDER = (
    [("in", e, 0) for e in range(8)] + [("in", 0, 1), ("in", 1, 1), ("xp", 0, 0)]
    + [("in", e, 1) for e in range(2, 8)] + [("xp", 0, 1)]
    + [("y", g, 0) for g in range(CB)] + [("out", 0, 0), ("out", 1, 0)]
    + [("up", j, 0) for j in range(3)] + [("y", g, 1) for g in range(CB)]
    + [("up", j, 0) for j in range(3, 6)] + [("out", 0, 1), ("out", 1, 1)]
    + [("up", 6, 0), ("up", 7, 0)] + [("up", j, 1) for j in range(HB)]
)
SMALL_ORDER = (
    [("ln1T", m, 0) for m in range(MB)] + [("ln1T", m, 1) for m in range(MB)]
    + [("xtok", c, 0) for c in range(GR)] + [("xdtok", 0, 0), ("sums", 0, 0), ("gap", 0, 0), ("bd", 0, 0)]
    + [("ct", 0, 0), ("cbd", 0, 0), ("u", 0, 0), ("cb", 0, 0), ("cb", 1, 0)]
    + [("moff", 0, 0)]
    + [("xtok", c, 1) for c in range(GR)] + [("xdtok", 0, 1), ("sums", 0, 1), ("gap", 0, 1), ("bd", 0, 1)]
    + [("ct", 0, 1), ("cbd", 0, 1), ("u", 0, 1)]
    + [("ln2T", m, 0) for m in range(MB)] + [("cb", 0, 1), ("cb", 1, 1), ("moff", 0, 1)]
    + [("ln2T", m, 1) for m in range(MB)]
)
RING = 3
HRING = 4
VECTOR_STEPS = 58


class Signal:

    def __init__(self, handle, count):
        self.handle, self.count, self.total = handle, count, BATCH * count

    def value(self, k, b, n, ago=0):
        return k * self.total + (b - ago) * self.count + n


class Banks:

    def __init__(self, nc, ctx, name, tiles, order):
        self.tiles, self.order = tiles, order
        self.written = [ctx.enter_context(nc.semaphore(f"{name}{i}_written")) for i in range(len(tiles))]
        self.read = [ctx.enter_context(nc.semaphore(f"{name}{i}_read")) for i in range(len(tiles))]
        self.place, self.total = {}, [0] * len(tiles)
        for n, use in enumerate(order):
            self.total[n % len(tiles)] += 1
            self.place[use] = (n % len(tiles), self.total[n % len(tiles)])

    def value(self, k, use, ago):
        name, i, b = use
        bank, n = self.place[(name, i, (b - ago) % BATCH)]
        return bank, (k + (b - ago) // BATCH) * self.total[bank] + n


def bass_preln_ssm_butterfly_ffn(
    nc, x, in_proj_w, conv_w, conv_b, x_proj_w, A_log, D, out_proj_w,
    W_exp, b_exp, up_weights, up_bias, down_weights, W_con, b_con, down_bias, out,
):
    ctx = ExitStack()
    with ctx:
        def sb(name, shape, dt=F32):
            return ctx.enter_context(nc.sbuf_tensor(name, shape, dt))

        def sem(name):
            return ctx.enter_context(nc.semaphore(name))

        w_in = sb("w_in", [P, MB, 2 * DI])
        w_x = sb("w_x", [P, CB, XD])
        w_out = sb("w_out", [P, CB, DM])
        w_up = sb("w_up", [P, MB, HID])
        w_down = sb("w_down", [P, HB, DM])
        bias_up = sb("bias_up", [P, HB])
        bias_out = sb("bias_out", [P, DM])
        taps = sb("taps", [P, CB, TAPS])
        tap_bias = sb("tap_bias", [P, CB])
        skip = sb("skip", [P, CB])
        rates = sb("rates", [P, NS])

        ident = sb("ident", [P, P])
        after = sb("after", [P, P])
        upto = sb("upto", [P, P])
        in_block = sb("in_block", [P, P])
        block_upto = sb("block_upto", [P, P])
        row_in_block = sb("row_in_block", [P, BL])
        later_in_block = sb("later_in_block", [P, BL])
        before_block = sb("before_block", [P, NB])
        restart = sb("restart", [P, GR, BL])
        ones = sb("ones", [P, P])
        minus_half = sb("minus_half", [P, GR])
        rate_before = sb("rate_before", [P, NB, NS])
        perm = sb("perm", [P, LOW, P])

        x_in = [sb(f"x_in{b}", [P, GR, DM]) for b in range(BATCH)]
        xn1 = [sb(f"xn1_{b}", [P, GR, DM]) for b in range(BATCH)]
        xn1T = sb("xn1T", [P, MB, TILE])
        xi = [sb(f"xi{b}", [P, CB, HALO + TILE]) for b in range(BATCH)]
        xc = [sb(f"xc{b}", [P, CB, TILE]) for b in range(BATCH)]
        z = [sb(f"z{b}", [P, CB, TILE]) for b in range(BATCH)]
        x_tok = [sb(f"x_tok{b}", [P, GR, DI]) for b in range(BATCH)]
        state = [sb(f"state{b}", [P, DI]) for b in range(BATCH)]
        state_end = [sb(f"state_end{b}", [NS, DI]) for b in range(BATCH)]
        xdT = sb("xdT", [P, TILE])
        xd = sb("xd", [P, GR, XD])
        soft = sb("soft", [P, 10, GR])
        delta = sb("delta", [P, GR])
        dB = sb("dB", [P, GR, NS])
        dA = sb("dA", [P, GR, SLOT])
        d_place = sb("d_place", [P, GR, BL])
        gap_w = sb("gap_w", [P, GR, NB, NS])
        bd_tok = sb("bd_tok", [P, GR, NB, NS])
        c_place = sb("c_place", [P, GR, NS, BL])
        sums_A = sb("sums_A", [P, 3 * GR, NS])
        decays = sb("decays", [P, 3, GR, NS])
        group_sum = sb("group_sum", [P, 1])
        group_decay = sb("group_decay", [P, 1])
        d_block = sb("d_block", [P, GR, BL])
        gaps = sb("gaps", [P, GR, BL])
        diag = sb("diag", [P, GR, NS, BL])
        diag_sum = sb("diag_sum", [P, GR, BL])
        c_start = sb("c_start", [P, GR, P + SLOT])
        c_block = sb("c_block", [P, GR, NS])
        cbd_tok = sb("cbd_tok", [P, GR, NB, NS])
        b_end = sb("b_end", [P, GR, NS])
        b_hat = sb("b_hat", [P, TILE])
        c_hat = sb("c_hat", [P, TILE])
        c_startT = sb("c_startT", [P, TILE])
        m_mat = sb("m_mat", [P, TILE])
        yg = sb("yg", [P, CB, TILE])
        x1 = sb("x1", [P, GR, DM])
        x1b_xn2 = sb("x1b_xn2", [P, 2, GR, DM])
        x1b, xn2 = x1b_xn2[:, 0, :, :], x1b_xn2[:, 1, :, :]
        xn2T = sb("xn2T", [P, MB, TILE])
        hid = sb("hid", [P, HRING, TILE])
        y_out = sb("y_out", [P, GR, DM])
        stats = sb("stats", [P, GR, 6])
        carrier = sb("carrier", [P, 1])
        mean_var = sb("mean_var", [P, GR, 2])
        var_eps = sb("var_eps", [P, 2 * BATCH, GR])
        rstd = sb("rstd", [P, 2 * BATCH, GR])

        wide = [ctx.enter_context(nc.psum_tensor(f"wide{i}", [P, TILE], F32)) for i in range(RING)]
        small = [ctx.enter_context(nc.psum_tensor(f"small{i}", [P, TILE], F32)) for i in range(RING)]
        acc = ctx.enter_context(nc.psum_tensor("acc", [P, GR, DM], F32))
        WIDE = Banks(nc, ctx, "wide", wide, WIDE_ORDER)
        SMALL = Banks(nc, ctx, "small", small, SMALL_ORDER)
        ACC = Banks(nc, ctx, "acc", [acc], [("down", 0, 0), ("down", 0, 1)])
        where = {name: banks for banks in (WIDE, SMALL, ACC) for name, _, _ in banks.order}

        def tile_of(name, i, b):
            banks = where[name]
            return banks.tiles[banks.place[(name, i, b)][0]]

        def written(eng, k, name, i, b, ago=0):
            bank, value = where[name].value(k, (name, i, b), ago)
            eng.wait_ge(where[name].written[bank], value)

        def read(eng, k, name, i, b, ago=0):
            bank, value = where[name].value(k, (name, i, b), ago)
            eng.wait_ge(where[name].read[bank], value)

        def free(eng, k, name, i, b):
            banks = where[name]
            bank, value = banks.value(k, (name, i, b), 0)
            eng.wait_ge(banks.read[bank], value - 1)

        def mark_written(ins, name, i, b):
            ins.then_inc(where[name].written[where[name].place[(name, i, b)][0]], 1)

        def mark_read(ins, name, i, b):
            ins.then_inc(where[name].read[where[name].place[(name, i, b)][0]], 1)

        x_loaded = [sem(f"x_loaded{b}") for b in range(BATCH)]
        out_stored = Signal(sem("out_stored"), 16)
        var1 = Signal(sem("var1"), 1)
        rstd1 = Signal(sem("rstd1"), 1)
        norm1 = Signal(sem("norm1"), 1)
        var2 = Signal(sem("var2"), 1)
        rstd2 = Signal(sem("rstd2"), 1)
        norm2 = Signal(sem("norm2"), 1)
        halo_moved = Signal(sem("halo_moved"), 1)
        xi_copied = Signal(sem("xi_copied"), CB)
        convolved = Signal(sem("convolved"), CB)
        xc_ready = Signal(sem("xc_ready"), 1)
        z_ready = Signal(sem("z_ready"), 1)
        abs_ready = Signal(sem("abs_ready"), 1)
        exp_ready = Signal(sem("exp_ready"), 1)
        dB_ready = Signal(sem("dB_ready"), 1)
        delta_ready = Signal(sem("delta_ready"), 1)
        gap_w_ready = Signal(sem("gap_w_ready"), 1)
        c_placed = Signal(sem("c_placed"), 1)
        bd_ready = Signal(sem("bd_ready"), 1)
        sums_ready = Signal(sem("sums_ready"), 1)
        decays_ready = Signal(sem("decays_ready"), 1)
        group_decay_ready = Signal(sem("group_decay_ready"), 1)
        gaps_ready = Signal(sem("gaps_ready"), 1)
        diag_gaps = Signal(sem("diag_gaps"), 1)
        diag_exp = Signal(sem("diag_exp"), 1)
        diag_summed = Signal(sem("diag_summed"), 1)
        c_start_ready = Signal(sem("c_start_ready"), 1)
        cbd_ready = Signal(sem("cbd_ready"), 1)
        b_end_ready = Signal(sem("b_end_ready"), 1)
        first_state = Signal(sem("first_state"), 1)
        states_ready = Signal(sem("states_ready"), 1)
        gated = Signal(sem("gated"), CB)
        x1b_ready = Signal(sem("x1b_ready"), 1)
        down_steps = Signal(sem("down_steps"), HB - 1)
        vector_steps = Signal(sem("vector_steps"), VECTOR_STEPS // BATCH)

        by_vector = [var1, norm1, var2, norm2, convolved, abs_ready, dB_ready, delta_ready, gap_w_ready, sums_ready,
                     gaps_ready, diag_summed, c_start_ready, cbd_ready, b_end_ready, states_ready, gated]
        by_scalar = [halo_moved, xi_copied, xc_ready, z_ready, exp_ready, decays_ready, group_decay_ready, diag_exp,
                     first_state]
        by_pool = [rstd1, rstd2, c_placed, bd_ready, diag_gaps, x1b_ready]

        def start(eng, signals):
            for s in signals:
                eng.sem_inc(s.handle, s.total)

        w_loaded = [sem(f"w_loaded{i}") for i in range(4)]
        s_loaded = sem("s_loaded")
        low_loaded = sem("low_loaded")
        x_small = sem("x_small")
        masks_made = sem("masks_made")
        mask_steps = sem("mask_steps")
        perm_made = sem("perm_made")
        made = sem("made")
        taken = sem("taken")
        vector_setup = sem("vector_setup")
        prepared = sem("prepared")
        zeroed = sem("zeroed")
        rates_exp = sem("rates_exp")

        W1 = DM + 1
        flat = "p a b -> p (a b)"
        raw_in = xc[0][:, :, :].rearrange(flat).rearrange("p (e d) -> p e d", d=DM)
        raw_exp = xc[1][:, :, :].rearrange(flat).rearrange("p (m h) -> p m h", h=HID)
        raw_con = z[0][:, :, :].rearrange(flat).rearrange("p (g d) -> p g d", d=DM)
        raw_out = x1[:, :, :].rearrange(flat).rearrange("p (o d) -> p o d", d=DI)
        raw_x = yg[:, 0, :]
        wexpT = xi[0][:, :, :].rearrange(flat)[:, 0:HB * W1].rearrange("p (g m) -> p g m", m=W1)
        mixed = xi[1][:, :, :].rearrange(flat)[:, 0:HB * W1].rearrange("p (g m) -> p g m", m=W1)
        con_mixed = x_tok[0][:, :, :].rearrange(flat).rearrange("p (g d) -> p g d", d=DM)
        paths = [z[1][:, 2 * i:2 * i + 2, :].rearrange(flat) for i in range(2)]
        pathT = hid[:, 0:2, :].rearrange(flat).rearrange("p (g j) -> p g j", j=P)
        low_w = [x_tok[1][:, :, :].rearrange(flat), x1b_xn2[:, :, :, :].rearrange("p a b c -> p (a b c)")]
        high_w = [sb(f"high_w{i}", [P, HIGH, HB // 2, 4]) for i in range(2)]
        bias_raw = sb("bias_raw", [P, 2, DM])
        up_bias_sb = sb("up_bias_sb", [P, HB])
        SMALL_LOADS = 14

        low_at = [0]
        for s in range(LOW):
            low_at.append(low_at[-1] + HID // 2**s)

        products = (
            [("w_in", m, h) for m in range(MB) for h in range(2)] + [("w_x", 0, 0)]
            + [("w_out", h, 0) for h in range(2)] + [("wexpT", q, 0) for q in range(4)]
            + [("low", i, q) for i in range(2) for q in range(4)]
            + [("pathT", h, 0) for h in range(2)] + [("up_low", g, 0) for g in range(HB)]
            + [("w_up", m, h) for m in range(MB) for h in range(2)]
            + [("w_down", q, 0) for q in range(4)]
        )
        number = {product: n for n, product in enumerate(products)}
        banks6 = wide + small

        def bank_for(product):
            return banks6[number[product] % len(banks6)]

        block = ctx.enter_context(nc.Block())

        @block.sync
        def _(sp):
            for b in range(BATCH):
                sp.dma_start(x_in[b][:, :, :], x[b, 0:TILE, :].rearrange("(c p) d -> p c d", p=P)).then_inc(x_loaded[b], 16)
            sp.dma_start(raw_in, in_proj_w.rearrange("(e p) d -> p e d", p=P)).then_inc(w_loaded[0], 16)
            sp.dma_start(raw_x[0:XD, :], x_proj_w).then_inc(x_small, 16)
            sp.dma_start(raw_out, out_proj_w.rearrange("(o p) d -> p o d", p=P)).then_inc(w_loaded[1], 16)
            sp.dma_start(raw_exp, W_exp.rearrange("(m p) h -> p m h", p=P)).then_inc(w_loaded[2], 16)
            sp.dma_start(raw_con, W_con.rearrange("(g p) d -> p g d", p=P)).then_inc(w_loaded[3], 16)
            for i, weights in enumerate((up_weights, down_weights)):
                for s in range(HIGH):
                    sp.dma_start(high_w[i][:, s, :, :],
                                 weights[LOW + s].rearrange("(q p) o i -> p q (o i)", p=P)).then_inc(s_loaded, 16)
            for n, row in enumerate((b_con, down_bias)):
                sp.dma_start(bias_raw[:, n, :], row.partition_broadcast(P)).then_inc(s_loaded, 16)
            sp.dma_start(rates[:, :], A_log.partition_broadcast(P)).then_inc(s_loaded, 16)
            sp.dma_start(taps[:, :, :], conv_w.rearrange("(g p) o k -> p g (o k)", p=P)).then_inc(s_loaded, 16)
            sp.dma_start(tap_bias[:, :], conv_b.rearrange("(g p) -> p g", p=P), allow_slow_non_contiguous=True).then_inc(s_loaded, 16)
            sp.dma_start(skip[:, :], D.rearrange("(g p) -> p g", p=P), allow_slow_non_contiguous=True).then_inc(s_loaded, 16)
            sp.dma_start(up_bias_sb[:, :], up_bias.rearrange("(g p) -> p g", p=P), allow_slow_non_contiguous=True).then_inc(s_loaded, 16)
            sp.dma_start(wexpT[:, :, DM], b_exp.rearrange("(g p) -> p g", p=P), allow_slow_non_contiguous=True).then_inc(s_loaded, 16)
            start(sp, [out_stored])
            with sp.Fori(1, TILES + 1) as k:
                for b in range(BATCH):
                    read(sp, k, "out", 1, b)
                    nxt = k % TILES
                    sp.dma_start(x_in[b][:, :, :],
                                 x[b, bass.ds(nxt * TILE, TILE), :].rearrange("(c p) d -> p c d", p=P))\
                        .then_inc(x_loaded[b], 16)
                    if b == 0:
                        continue
                for b in range(BATCH):
                    read(sp, k, "down", 0, b)
                    sp.dma_start(out[b, bass.ds((k - 1) * TILE, TILE), :].rearrange("(c p) d -> p c d", p=P),
                                 y_out[:, :, :]).then_inc(out_stored.handle, 16)
            sp.wait_ge(out_stored.handle, out_stored.value(TILES, 1, 16))

        @block.gpsimd
        def _(pool):
            start(pool, by_pool)
            count = [0]

            def select(out_ap, in_ap, op, base, cm, pattern):
                pool.affine_select(out=out_ap, in_=in_ap, compare_op=op, fill=0.0, base=base, pattern=pattern,
                                   channel_multiplier=cm).then_inc(mask_steps, 1)
                count[0] += 1
                pool.wait_ge(mask_steps, count[0])

            pool.memset(ident[:, :], 0.0).then_inc(mask_steps, 1)
            pool.memset(ones[:, :], 1.0).then_inc(mask_steps, 1)
            pool.memset(restart[:, :, :], 1.0).then_inc(mask_steps, 1)
            pool.memset(minus_half[:, :], -0.5).then_inc(mask_steps, 1)
            count[0] = 4
            pool.wait_ge(mask_steps, count[0])
            pool.affine_select(out=ident[:, :], in_=ident[:, :], compare_op=ALU.not_equal, fill=1.0, base=0,
                               pattern=[[-1, P]], channel_multiplier=1).then_inc(masks_made, 1)
            for i, weights in enumerate((up_weights, down_weights)):
                for s in range(LOW):
                    half = 2**s
                    for o in range(2):
                        pool.dma_start(
                            low_w[i][o * half:(o + 1) * half, low_at[s]:low_at[s + 1]].rearrange("l (c i) -> l c i", i=2),
                            weights[s, :, o, :].rearrange("(c l) i -> l c i", l=half)).then_inc(low_loaded, 16)
            pool.memset(restart[:, :, 0], 0.0).then_inc(masks_made, 1)
            select(after[:, :], ones[:, :], ALU.is_gt, 0, 1, [[-1, P]])
            select(upto[:, :], ones[:, :], ALU.is_ge, 0, -1, [[1, P]])
            in_blocks = "p (j u) -> p j u"
            blk, blk_upto = (m[:, :].rearrange(in_blocks, u=BL) for m in (in_block, block_upto))
            select(blk, ones[:, :].rearrange(in_blocks, u=BL), ALU.is_ge, 0, 1, [[-BL, NB], [0, BL]])
            select(blk, blk, ALU.is_ge, BL - 1, -1, [[BL, NB], [0, BL]])
            select(blk_upto, blk, ALU.is_ge, 0, -1, [[BL, NB], [1, BL]])
            pool.affine_select(out=before_block[:, :], in_=ones[:, 0:NB], compare_op=ALU.is_gt, fill=0.0, base=0,
                               pattern=[[BL, NB]], channel_multiplier=-1).then_inc(masks_made, 1)

            def rstd_of(k, b, slot, var, ready):
                pool.wait_ge(var.handle, var.value(k, b, 1))
                pool.tensor_tensor(rstd[:, slot, :], var_eps[:, slot, :], minus_half[:, :], ALU.pow)\
                    .then_inc(ready.handle, 1)

            def place_c(k, b):
                read(pool, k, "xdtok", 0, b)
                written(pool, k, "cb", 1, b, ago=1)
                pool.tensor_tensor(c_place[:, :, :, :],
                                   xd[:, :, 1 + NS:XD].unsqueeze(3).to_broadcast([P, GR, NS, BL]),
                                   row_in_block[:, :].unsqueeze(1).unsqueeze(1).to_broadcast([P, GR, NS, BL]),
                                   ALU.mult).then_inc(c_placed.handle, 1)

            def mask_b(k, b):
                pool.wait_ge(dB_ready.handle, dB_ready.value(k, b, 1))
                written(pool, k, "bd", 0, b, ago=1)
                pool.tensor_tensor(bd_tok[:, :, :, :],
                                   dB[:, :, :].unsqueeze(2).to_broadcast([P, GR, NB, NS]),
                                   before_block[:, :].unsqueeze(1).unsqueeze(3).to_broadcast([P, GR, NB, NS]),
                                   ALU.mult).then_inc(bd_ready.handle, 1)

            def diagonal_gaps(k, b):
                pool.wait_ge(gaps_ready.handle, gaps_ready.value(k, b, 1))
                pool.wait_ge(diag_summed.handle, diag_summed.value(k, b, 1, ago=1))
                pool.tensor_tensor(diag[:, :, :, :],
                                   gaps[:, :, :].unsqueeze(2).to_broadcast([P, GR, NS, BL]),
                                   rates[:, :].unsqueeze(1).unsqueeze(3).to_broadcast([P, GR, NS, BL]),
                                   ALU.mult).then_inc(diag_gaps.handle, 1)

            def residual_with_bias(k, b):
                read(pool, k, "out", 1, b)
                read(pool, k, "down", 0, b, ago=1)
                pool.tensor_tensor(x1b, x1[:, :, :], bias_out[:, :].unsqueeze(1).to_broadcast([P, GR, DM]),
                                   ALU.add).then_inc(x1b_ready.handle, 1)

            for b in range(BATCH):
                rstd_of(1, b, b, var1, rstd1)
            with pool.Fori(1, TILES + 1) as k:
                place_c(k, 0)
                mask_b(k, 0)
                diagonal_gaps(k, 0)
                place_c(k, 1)
                mask_b(k, 1)
                residual_with_bias(k, 0)
                rstd_of(k, 0, BATCH, var2, rstd2)
                diagonal_gaps(k, 1)
                rstd_of(k, 1, BATCH + 1, var2, rstd2)
                residual_with_bias(k, 1)
                for b in range(BATCH):
                    rstd_of(k + 1, b, b, var1, rstd1)

        @block.tensor
        def _(pe):
            def begin(product):
                n = number[product]
                if n >= len(banks6):
                    pe.wait_ge(taken, n - len(banks6) + 1)
                return bank_for(product)

            pe.wait_ge(masks_made, 1)
            pe.wait_ge(w_loaded[0], 16)
            for m in range(MB):
                for h in range(2):
                    bank = begin(("w_in", m, h))
                    for q in range(4):
                        last = pe.transpose(bank[:, q * P:(q + 1) * P], raw_in[:, 4 * h + q, m * P:(m + 1) * P], ident[:, :])
                    last.then_inc(made, 1)
            pe.wait_ge(x_small, 16)
            bank = begin(("w_x", 0, 0))
            for g in range(CB):
                last = pe.transpose(bank[:, g * XD:(g + 1) * XD], raw_x[0:XD, g * P:(g + 1) * P], ident[0:XD, 0:XD])
            last.then_inc(made, 1)
            pe.wait_ge(w_loaded[1], 16)
            for h in range(2):
                bank = begin(("w_out", h, 0))
                for q in range(2):
                    for o in range(MB):
                        at = (q * MB + o) * P
                        last = pe.transpose(bank[:, at:at + P], raw_out[:, o, (2 * h + q) * P:(2 * h + q + 1) * P], ident[:, :])
                last.then_inc(made, 1)
            pe.wait_ge(w_loaded[2], 16)
            for q in range(4):
                bank = begin(("wexpT", q, 0))
                for g in range(2):
                    for m in range(MB):
                        at = (g * MB + m) * P
                        last = pe.transpose(bank[:, at:at + P], raw_exp[:, m, (2 * q + g) * P:(2 * q + g + 1) * P], ident[:, :])
                last.then_inc(made, 1)
            pe.wait_ge(perm_made, LOW)
            pe.wait_ge(low_loaded, 16 * 2 * 2 * LOW)
            for i in range(2):
                for q in range(4):
                    bank = begin(("low", i, q))
                    if q < 2:
                        parts = [(0, 512 * q, 512 * (q + 1), 0)]
                    elif q == 2:
                        parts = [(1, low_at[1], low_at[2], 0)]
                    else:
                        parts = [(s, low_at[s], low_at[s + 1], low_at[s] - low_at[2]) for s in range(2, LOW)]
                    for s, lo, hi, at in parts:
                        rows = 2**(s + 1)
                        last = pe.matmul(bank[:, at:at + hi - lo], perm[0:rows, s, :], low_w[i][0:rows, lo:hi],
                                         start=True, stop=True)
                    last.then_inc(made, 1)
            pe.wait_ge(prepared, 1)
            for h in range(2):
                bank = begin(("pathT", h, 0))
                for q in range(4):
                    g = 4 * h + q
                    last = pe.transpose(bank[:, q * P:(q + 1) * P], paths[0][:, g * P:(g + 1) * P], ident[:, :])
                last.then_inc(made, 1)
            pe.wait_ge(s_loaded, 16 * SMALL_LOADS)
            pe.wait_ge(taken, number[("pathT", 1, 0)] + 1)
            for g in range(HB):
                bank = begin(("up_low", g, 0))
                pe.matmul(bank[:, 0:W1], pathT[:, g, :], wexpT[:, g, :], start=True, stop=True).then_inc(made, 1)
            pe.wait_ge(prepared, 2)
            for m in range(MB):
                for h in range(2):
                    bank = begin(("w_up", m, h))
                    for q in range(4):
                        last = pe.transpose(bank[:, q * P:(q + 1) * P], wexpT[:, 4 * h + q, m * P:(m + 1) * P], ident[:, :])
                    last.then_inc(made, 1)
            pe.wait_ge(prepared, 3)
            for q in range(4):
                bank = begin(("w_down", q, 0))
                for g in range(2):
                    last = pe.matmul(bank[:, g * DM:(g + 1) * DM], paths[1][:, (2 * q + g) * P:(2 * q + g + 1) * P],
                                     con_mixed[:, 2 * q + g, :], start=True, stop=True)
                last.then_inc(made, 1)

            for banks in (WIDE, SMALL, ACC):
                for handle, total in zip(banks.written, banks.total):
                    pe.sem_inc(handle, total)
            start(pe, [down_steps])
            pe.wait_ge(zeroed, 1)
            pe.wait_ge(masks_made, 3)
            pe.wait_ge(taken, len(products))

            def transposes(k, name, b, source, ready):
                for m in range(MB):
                    bank = tile_of(name, m, b)
                    free(pe, k, name, m, b)
                    if m == 0:
                        pe.wait_ge(ready.handle, ready.value(k, b, 1))
                    for c in range(GR):
                        last = pe.transpose(bank[:, c * P:(c + 1) * P], source[:, c, m * P:(m + 1) * P], ident[:, :])
                    mark_written(last, name, m, b)

            def in_projection(k, b, e):
                bank = tile_of("in", e, b)
                free(pe, k, "in", e, b)
                if e == 0:
                    for m in range(MB):
                        read(pe, k, "ln1T", m, b)
                for m in range(MB):
                    last = pe.matmul(bank[:, :], w_in[:, m, e * P:(e + 1) * P], xn1T[:, m, :],
                                     start=m == 0, stop=m == MB - 1)
                mark_written(last, "in", e, b)

            def x_projection(k, b):
                bank = tile_of("xp", 0, b)
                free(pe, k, "xp", 0, b)
                pe.wait_ge(xc_ready.handle, xc_ready.value(k, b, 1))
                for g in range(CB):
                    last = pe.matmul(bank[0:XD, :], w_x[:, g, :], xc[b][:, g, :], start=g == 0, stop=g == CB - 1)
                mark_written(last, "xp", 0, b)

            def tokens_first(k, b):
                for c in range(GR):
                    bank = tile_of("xtok", c, b)
                    free(pe, k, "xtok", c, b)
                    for g in range(CB):
                        last = pe.transpose(bank[:, g * P:(g + 1) * P], xc[b][:, g, c * P:(c + 1) * P], ident[:, :])
                    mark_written(last, "xtok", c, b)

            def xd_tokens_first(k, b):
                bank = tile_of("xdtok", 0, b)
                free(pe, k, "xdtok", 0, b)
                read(pe, k, "xp", 0, b)
                for c in range(GR):
                    last = pe.transpose(bank[:, c * P:(c + 1) * P], xdT[:, c * P:(c + 1) * P], ident[:, :])
                mark_written(last, "xdtok", 0, b)

            def step_sums(k, b):
                bank = tile_of("sums", 0, b)
                free(pe, k, "sums", 0, b)
                pe.wait_ge(delta_ready.handle, delta_ready.value(k, b, 1))
                for n, mask in enumerate((upto, block_upto, after)):
                    pe.matmul(bank[:, n * GR:(n + 1) * GR], mask[:, :], delta[:, :], start=True, stop=True)
                pe.matmul(bank[:, 12:13], dA[:, :, :].rearrange(flat), ones[:, 0:1], start=True, stop=True)
                mark_written(pe.matmul(bank[:, 16:16 + GR * BL], in_block[:, :], d_place[:, :, :].rearrange(flat),
                                       start=True, stop=True), "sums", 0, b)

            def gap_products(k, b):
                bank = tile_of("gap", 0, b)
                free(pe, k, "gap", 0, b)
                pe.wait_ge(gap_w_ready.handle, gap_w_ready.value(k, b, 1))
                for c in range(GR):
                    last = pe.matmul(bank[:, c * P:(c + 1) * P], gap_w[:, c, :, :].rearrange(flat), after[:, :],
                                     start=True, stop=True)
                mark_written(last, "gap", 0, b)

            def transpose_groups(k, name, b, source, ready):
                bank = tile_of(name, 0, b)
                free(pe, k, name, 0, b)
                pe.wait_ge(ready.handle, ready.value(k, b, 1))
                for c in range(GR):
                    last = pe.transpose(bank[:, c * P:(c + 1) * P], source(c), ident[:, :])
                mark_written(last, name, 0, b)

            def state_inputs(k, b):
                bank = tile_of("u", 0, b)
                free(pe, k, "u", 0, b)
                pe.wait_ge(b_end_ready.handle, b_end_ready.value(k, b, 1))
                for c in range(GR):
                    read(pe, k, "xtok", c, b)
                for c in range(GR):
                    last = pe.matmul(bank[SLOT * c:SLOT * c + NS, :], b_end[:, c, :], x_tok[b][:, c, :],
                                     start=True, stop=True)
                mark_written(last, "u", 0, b)

            def spread_c(k, b):
                for h in range(2):
                    bank = tile_of("cb", h, b)
                    free(pe, k, "cb", h, b)
                    if h == 0:
                        pe.wait_ge(c_placed.handle, c_placed.value(k, b, 1))
                    mark_written(pe.matmul(bank[:, :], in_block[:, :],
                                           c_place[:, 2 * h:2 * h + 2, :, :].rearrange("p c n u -> p (c n u)"),
                                           start=True, stop=True), "cb", h, b)

            def off_diagonal(k, b):
                bank = tile_of("moff", 0, b)
                free(pe, k, "moff", 0, b)
                read(pe, k, "bd", 0, b)
                read(pe, k, "cbd", 0, b)
                for c in range(GR):
                    last = pe.matmul(bank[:, c * P:(c + 1) * P], b_hat[:, c * P:(c + 1) * P], c_hat[:, c * P:(c + 1) * P],
                                     start=True, stop=True)
                mark_written(last, "moff", 0, b)

            def ssm_output(k, b, g):
                bank = tile_of("y", g, b)
                free(pe, k, "y", g, b)
                if g == 0:
                    read(pe, k, "moff", 0, b)
                    read(pe, k, "ct", 0, b)
                    pe.wait_ge(first_state.handle, first_state.value(k, b, 1))
                    pe.wait_ge(states_ready.handle, states_ready.value(k, b, 1))
                for c in range(GR):
                    pe.matmul(bank[:, c * P:(c + 1) * P], x_tok[b][:, c, g * P:(g + 1) * P], m_mat[:, c * P:(c + 1) * P],
                              start=c == 0, stop=False, skip_group_check=True)
                mark_written(pe.matmul(bank[:, :], state[b][:, g * P:(g + 1) * P], c_startT[:, :],
                                       start=False, stop=True, skip_group_check=True), "y", g, b)

            def out_projection(k, b, h):
                bank = tile_of("out", h, b)
                free(pe, k, "out", h, b)
                if h == 0:
                    pe.wait_ge(gated.handle, gated.value(k, b, CB))
                for q in range(2):
                    c = 2 * h + q
                    for g in range(CB):
                        last = pe.matmul(bank[:, q * DM:(q + 1) * DM], yg[:, g, c * P:(c + 1) * P], w_out[:, g, :],
                                         start=g == 0, stop=g == CB - 1)
                mark_written(last, "out", h, b)

            def up(k, b, j):
                bank = tile_of("up", j, b)
                free(pe, k, "up", j, b)
                if j == 0:
                    for m in range(MB):
                        read(pe, k, "ln2T", m, b)
                for m in range(MB):
                    last = pe.matmul(bank[:, :], w_up[:, m, j * P:(j + 1) * P], xn2T[:, m, :],
                                     start=m == 0, stop=m == MB - 1)
                mark_written(last, "up", j, b)

            def down(k, b, j):
                if j == 0:
                    free(pe, k, "down", 0, b)
                read(pe, k, "up", j, b)
                for c in range(GR):
                    last = pe.matmul(acc[:, c, :], hid[:, j % HRING, c * P:(c + 1) * P], w_down[:, j, :],
                                     start=j == 0 and c % 2 == 0, stop=j == HB - 1, skip_group_check=True)
                if j == HB - 1:
                    mark_written(last, "down", 0, b)
                else:
                    last.then_inc(down_steps.handle, 1)

            def ssm_small(k, b, part):
                if part == 0:
                    transpose_groups(k, "ct", b, lambda c: c_start[:, c, 0:P] if c == 0 else
                                     c_start[:, :, :].rearrange(flat)[:, c * P:(c + 1) * P], c_start_ready)
                    transpose_groups(k, "cbd", b, lambda c: cbd_tok[:, c, :, :].rearrange(flat), cbd_ready)
                    state_inputs(k, b)

            with pe.Fori(1, TILES + 1) as k:
                transposes(k, "ln1T", 0, xn1[0], norm1)
                for e in range(8):
                    in_projection(k, 0, e)
                transposes(k, "ln1T", 1, xn1[1], norm1)
                in_projection(k, 1, 0)
                in_projection(k, 1, 1)
                x_projection(k, 0)
                tokens_first(k, 0)
                in_projection(k, 1, 2)
                in_projection(k, 1, 3)
                xd_tokens_first(k, 0)
                in_projection(k, 1, 4)
                in_projection(k, 1, 5)
                step_sums(k, 0)
                in_projection(k, 1, 6)
                gap_products(k, 0)
                transpose_groups(k, "bd", 0, lambda c: bd_tok[:, c, :, :].rearrange(flat), bd_ready)
                in_projection(k, 1, 7)
                ssm_small(k, 0, 0)
                x_projection(k, 1)
                spread_c(k, 0)
                off_diagonal(k, 0)
                tokens_first(k, 1)
                xd_tokens_first(k, 1)
                for g in range(CB):
                    ssm_output(k, 0, g)
                step_sums(k, 1)
                out_projection(k, 0, 0)
                out_projection(k, 0, 1)
                gap_products(k, 1)
                transpose_groups(k, "bd", 1, lambda c: bd_tok[:, c, :, :].rearrange(flat), bd_ready)
                ssm_small(k, 1, 0)
                transposes(k, "ln2T", 0, xn2, norm2)
                spread_c(k, 1)
                off_diagonal(k, 1)
                up(k, 0, 0)
                up(k, 0, 1)
                up(k, 0, 2)
                down(k, 0, 0)
                for g in range(CB):
                    ssm_output(k, 1, g)
                for j in range(3, 6):
                    up(k, 0, j)
                    down(k, 0, j - 2)
                out_projection(k, 1, 0)
                out_projection(k, 1, 1)
                for j in range(6, HB):
                    up(k, 0, j)
                    down(k, 0, j - 2)
                down(k, 0, HB - 2)
                down(k, 0, HB - 1)
                transposes(k, "ln2T", 1, xn2, norm2)
                up(k, 1, 0)
                up(k, 1, 1)
                for j in range(2, HB):
                    up(k, 1, j)
                    down(k, 1, j - 2)
                down(k, 1, HB - 2)
                down(k, 1, HB - 1)

        @block.scalar
        def _(act):
            act.wait_ge(s_loaded, 16 * SMALL_LOADS)
            act.activation(rates[:, :], rates[:, :], ACT.Exp).then_inc(rates_exp, 1)
            start(act, by_scalar)
            act.wait_ge(zeroed, 1)
            act.wait_ge(prepared, 4)

            def take(k, name, i, b, out_ap, in_ap, last=True, **how):
                written(act, k, name, i, b)
                how.setdefault("func", ACT.Copy)
                ins = act.activation(out_ap, in_ap, how.pop("func"), **how)
                if last:
                    mark_read(ins, name, i, b)
                return ins

            def normalised(k, name, b, target, last_use):
                last_use()
                for m in range(MB):
                    take(k, name, m, b, target[:, m, :], tile_of(name, m, b)[:, :])

            def move_halo(k, b):
                act.wait_ge(convolved.handle, convolved.value(k, b, CB, ago=2))
                act.wait_ge(xi_copied.handle, xi_copied.value(k, b, CB, ago=2))
                act.activation(xi[b][:, :, 0:HALO], xi[b][:, :, TILE:TILE + HALO], ACT.Copy)\
                    .then_inc(halo_moved.handle, 1)
                act.wait_ge(halo_moved.handle, halo_moved.value(k, b, 1))

            def first_tap(k, b, e):
                bank = tile_of("in", e, b)
                if e == 0:
                    act.wait_ge(gated.handle, gated.value(k, b, CB, ago=2))
                    written(act, k, "xtok", GR - 1, b, ago=2)
                take(k, "in", e, b, xi[b][:, e, HALO:], bank[:, :], last=False).then_inc(xi_copied.handle, 1)
                mark_read(act.activation(xc[b][:, e, :], bank[:, :], ACT.Identity, bias=tap_bias[:, e:e + 1],
                                         scale=taps[:, e, TAPS - 1:TAPS]), "in", e, b)

            def copy_z(k, b, e):
                take(k, "in", e, b, z[b][:, e - CB, :], tile_of("in", e, b)[:, :])

            def silu_x(k, b):
                act.wait_ge(convolved.handle, convolved.value(k, b, CB))
                act.activation(xc[b][:, :, :], xc[b][:, :, :], ACT.Silu).then_inc(xc_ready.handle, 1)

            def silu_z(k, b):
                read(act, k, "in", 7, b)
                act.activation(z[b][:, :, :], z[b][:, :, :], ACT.Silu).then_inc(z_ready.handle, 1)

            def take_xd(k, b):
                written(act, k, "xdtok", 0, b, ago=1)
                take(k, "xp", 0, b, xdT[0:XD, :], tile_of("xp", 0, b)[0:XD, :])

            def take_x_tok(k, b, c):
                if c == 0:
                    written(act, k, "y", CB - 1, b, ago=2)
                take(k, "xtok", c, b, x_tok[b][:, c, :], tile_of("xtok", c, b)[:, :])

            def exp_abs(k, b):
                act.wait_ge(abs_ready.handle, abs_ready.value(k, b, 1))
                act.activation(soft[:, 1, :], soft[:, 0, :], ACT.Exp, scale=-1.0).then_inc(exp_ready.handle, 1)

            def exp_sums(k, b):
                act.wait_ge(sums_ready.handle, sums_ready.value(k, b, 1))
                act.activation(decays[:, :, :, :].rearrange("p a c n -> p (a c n)"),
                               sums_A[:, :, :].rearrange(flat), ACT.Exp).then_inc(decays_ready.handle, 1)
                read(act, k, "u", 0, b, ago=1)
                act.activation(group_decay[:, :], group_sum[:, :], ACT.Exp).then_inc(group_decay_ready.handle, 1)

            def exp_gaps(k, b):
                written(act, k, "moff", 0, b, ago=1)
                take(k, "gap", 0, b, b_hat[:, :], tile_of("gap", 0, b)[:, :], func=ACT.Exp)

            def take_c(k, b):
                written(act, k, "y", CB - 1, b, ago=1)
                take(k, "ct", 0, b, c_startT[:, :], tile_of("ct", 0, b)[:, :])
                written(act, k, "moff", 0, b, ago=1)
                take(k, "cbd", 0, b, c_hat[:, :], tile_of("cbd", 0, b)[:, :])

            def copy_first_state(k, b):
                read(act, k, "u", 0, b, ago=2)
                written(act, k, "y", CB - 1, b, ago=2)
                act.activation(state[b][0:NS, :], state_end[b][:, :], ACT.Copy).then_inc(first_state.handle, 1)

            def exp_diagonal(k, b):
                act.wait_ge(diag_gaps.handle, diag_gaps.value(k, b, 1))
                whole = diag[:, :, :, :].rearrange("p c n u -> p (c n u)")
                act.activation(whole, whole, ACT.Exp).then_inc(diag_exp.handle, 1)

            def gelu(k, b, j):
                if j >= HRING:
                    act.wait_ge(down_steps.handle, down_steps.value(k, b, j - HRING + 1))
                elif j == HRING - 1:
                    written(act, k, "down", 0, b, ago=1)
                else:
                    act.wait_ge(down_steps.handle, down_steps.value(k, b, HB - 1 - (HRING - 2 - j), ago=1))
                take(k, "up", j, b, hid[:, j % HRING, :], tile_of("up", j, b)[:, :], func=ACT.Gelu,
                     bias=bias_up[:, j:j + 1])

            with act.Fori(1, TILES + 1) as k:
                move_halo(k, 0)
                normalised(k, "ln1T", 0, xn1T, lambda: written(act, k, "in", 7, 0, ago=1))
                for e in range(CB):
                    first_tap(k, 0, e)
                copy_z(k, 0, 4)
                copy_z(k, 0, 5)
                silu_x(k, 0)
                copy_z(k, 0, 6)
                copy_z(k, 0, 7)
                silu_z(k, 0)
                move_halo(k, 1)
                normalised(k, "ln1T", 1, xn1T, lambda: written(act, k, "in", 7, 1, ago=1))
                first_tap(k, 1, 0)
                first_tap(k, 1, 1)
                take_xd(k, 0)
                take_x_tok(k, 0, 0)
                take_x_tok(k, 0, 1)
                first_tap(k, 1, 2)
                first_tap(k, 1, 3)
                exp_abs(k, 0)
                copy_z(k, 1, 4)
                copy_z(k, 1, 5)
                exp_sums(k, 0)
                copy_z(k, 1, 6)
                exp_gaps(k, 0)
                copy_z(k, 1, 7)
                take_c(k, 0)
                copy_first_state(k, 0)
                exp_diagonal(k, 0)
                silu_x(k, 1)
                silu_z(k, 1)
                take_xd(k, 1)
                take_x_tok(k, 1, 0)
                take_x_tok(k, 1, 1)
                exp_abs(k, 1)
                exp_sums(k, 1)
                exp_gaps(k, 1)
                take_c(k, 1)
                copy_first_state(k, 1)
                normalised(k, "ln2T", 0, xn2T, lambda: written(act, k, "up", 7, 0, ago=1))
                exp_diagonal(k, 1)
                for j in range(HB):
                    gelu(k, 0, j)
                normalised(k, "ln2T", 1, xn2T, lambda: written(act, k, "up", 7, 1, ago=1))
                for j in range(HB):
                    gelu(k, 1, j)

        @block.vector
        def _(dve):
            done = [0]

            def link(ins):
                done[0] += 1
                ins.then_inc(vector_setup, 1)
                dve.wait_ge(vector_setup, done[0])

            def norm_stats(k, b, slot, source, var, link):
                for c in range(GR):
                    ins = dve.bn_stats(stats[:, c, :], source[:, c, :])
                link(ins)
                dve.memset(carrier[:, :], 0.0)
                for c in range(GR):
                    ins = dve.bn_aggr(mean_var[:, c, :], stats[:, c, :])
                link(ins)
                dve.tensor_scalar(var_eps[:, slot, :], mean_var[:, :, 1], EPS, None, ALU.add).then_inc(var.handle, 1)

            def normalise(k, b, slot, source, target, ready, normed):
                dve.wait_ge(ready.handle, ready.value(k, b, 1))
                for c in range(GR):
                    ins = dve.tensor_scalar(target[:, c, :], source[:, c, :], mean_var[:, c, 0:1],
                                            rstd[:, slot, c:c + 1], ALU.subtract, ALU.mult)
                ins.then_inc(normed.handle, 1)

            start(dve, by_vector)
            for banks in (WIDE, SMALL, ACC):
                for handle, total in zip(banks.read, banks.total):
                    dve.sem_inc(handle, total)
            dve.wait_ge(masks_made, 1)
            for s in range(LOW):
                rows = 2**(s + 1)
                dve.tensor_copy(perm[0:rows, s, :].rearrange("q (r w) -> q r w", w=rows),
                                ident[0:rows, 0:rows].unsqueeze(1).to_broadcast([rows, P // rows, rows]))\
                    .then_inc(perm_made, 1)
            for b in range(BATCH):
                dve.wait_ge(x_loaded[b], 16)
                norm_stats(1, b, b, x_in[b], var1, link)
                normalise(1, b, b, x_in[b], xn1[b], rstd1, norm1)
                dve.wait_ge(norm1.handle, norm1.value(1, b, 1))
            dve.wait_ge(masks_made, 3)
            dve.wait_ge(rates_exp, 1)
            dve.tensor_reduce(row_in_block[:, :], ident[:, :].rearrange("p (j u) -> p u j", u=BL), AXIS_X, ALU.add)
            dve.tensor_tensor(m_mat[:, 0:P], block_upto[:, :], ident[:, :], ALU.subtract)
            link(dve.tensor_scalar(rates[:, :], rates[:, :], -1.0, None, ALU.mult))
            dve.tensor_reduce(later_in_block[:, :], m_mat[:, 0:P].rearrange("p (j u) -> p u j", u=BL), AXIS_X, ALU.add)
            dve.tensor_tensor(rate_before[:, :, :], before_block[:, :].unsqueeze(2).to_broadcast([P, NB, NS]),
                              rates[:, :].unsqueeze(1).to_broadcast([P, NB, NS]), ALU.mult)
            dve.tensor_tensor(bias_out[:, :], bias_raw[:, 0, :], bias_raw[:, 1, :], ALU.add)

            def receive(product, target, source, op=None, other=None):
                dve.wait_ge(made, number[product] + 1)
                if op is None:
                    ins = dve.tensor_copy(target, source)
                else:
                    ins = dve.tensor_tensor(target, other, source, op)
                ins.then_inc(taken, 1)
                dve.wait_ge(taken, number[product] + 1)

            for m in range(MB):
                for h in range(2):
                    receive(("w_in", m, h), w_in[:, m, h * 512:(h + 1) * 512], bank_for(("w_in", m, h))[:, :])
            receive(("w_x", 0, 0), w_x[:, :, :].rearrange(flat), bank_for(("w_x", 0, 0))[:, 0:CB * XD])
            for h in range(2):
                receive(("w_out", h, 0), w_out[:, 2 * h:2 * h + 2, :].rearrange(flat), bank_for(("w_out", h, 0))[:, :])
            for q in range(4):
                receive(("wexpT", q, 0), wexpT[:, 2 * q:2 * q + 2, 0:DM],
                        bank_for(("wexpT", q, 0))[:, :].rearrange("p (g m) -> p g m", m=DM))
            for i in range(2):
                path = paths[i]
                for q in range(2):
                    receive(("low", i, q), path[:, 512 * q:512 * (q + 1)], bank_for(("low", i, q))[:, :])
                for s in range(1, LOW):
                    wide_as = path.rearrange("p (m w) -> p m w", w=2**s)
                    cols = HID // 2**s
                    bank = bank_for(("low", i, 2 if s == 1 else 3))
                    at = 0 if s == 1 else low_at[s] - low_at[2]
                    weights = bank[:, at:at + cols].unsqueeze(2).to_broadcast([P, cols, 2**s])
                    if s == 1:
                        receive(("low", i, 2), wide_as, weights, ALU.mult, wide_as)
                    elif s < LOW - 1:
                        if s == 2:
                            dve.wait_ge(made, number[("low", i, 3)] + 1)
                        link(dve.tensor_tensor(wide_as, wide_as, weights, ALU.mult))
                    else:
                        receive(("low", i, 3), wide_as, weights, ALU.mult, wide_as)
                if i == 0:
                    dve.sem_inc(prepared, 1)
            for h in range(2):
                receive(("pathT", h, 0), pathT[:, 4 * h:4 * h + 4, :].rearrange(flat), bank_for(("pathT", h, 0))[:, :])
            for g in range(HB):
                receive(("up_low", g, 0), mixed[:, g, :], bank_for(("up_low", g, 0))[:, 0:W1])

            def mix(weights, stage, source, target, transposed):
                span = 2**stage
                weight = lambda q, o, i: weights[:, stage, q, (2 * i + o if transposed else 2 * o + i):][:, 0:1]
                pairs = [(g // span % 2, g) for g in range(HB)]
                for o, g in pairs:
                    low = g - o * span
                    q = (low // (2 * span)) * span + low % span
                    ins = dve.tensor_scalar(target[:, g, :], source[:, low, :], weight(q, o, 0), None, ALU.mult)
                link(ins)
                for o, g in pairs:
                    low = g - o * span
                    q = (low // (2 * span)) * span + low % span
                    ins = dve.scalar_tensor_tensor(target[:, g, :], source[:, low + span, :], weight(q, o, 1),
                                                   target[:, g, :], ALU.mult, ALU.add)
                link(ins)

            dve.wait_ge(made, number[("up_low", HB - 1, 0)] + 1)
            mix(high_w[0], 0, mixed, wexpT, False)
            mix(high_w[0], 1, wexpT, mixed, False)
            mix(high_w[0], 2, mixed, wexpT, False)
            dve.tensor_tensor(bias_up[:, :], wexpT[:, :, DM], up_bias_sb[:, :], ALU.add).then_inc(prepared, 1)
            dve.wait_ge(w_loaded[3], 16)
            mix(high_w[1], 2, raw_con, con_mixed, True)
            mix(high_w[1], 1, con_mixed, raw_con, True)
            mix(high_w[1], 0, raw_con, con_mixed, True)
            dve.sem_inc(prepared, 1)
            for m in range(MB):
                for h in range(2):
                    receive(("w_up", m, h), w_up[:, m, h * 512:(h + 1) * 512], bank_for(("w_up", m, h))[:, :])
            for q in range(4):
                receive(("w_down", q, 0), w_down[:, 2 * q:2 * q + 2, :].rearrange(flat), bank_for(("w_down", q, 0))[:, :])
            dve.sem_inc(prepared, 1)
            dve.memset(xdT[:, :], 0.0)
            dve.memset(dA[:, :, :], 0.0)
            dve.memset(c_start[:, :, :], 0.0)
            for b in range(BATCH):
                dve.memset(state[b][:, :], 0.0)
                dve.memset(state_end[b][:, :], 0.0)
                ins = dve.memset(xi[b][:, :, TILE:], 0.0)
            ins.then_inc(zeroed, 1)
            dve.wait_ge(zeroed, 1)
            start(dve, [vector_steps])

            def convolve(k, b, e):
                read(dve, k, "in", e, b)
                for tap in range(TAPS - 2, -1, -1):
                    ins = dve.scalar_tensor_tensor(xc[b][:, e, :], xi[b][:, e, tap:tap + TILE], taps[:, e, tap:tap + 1],
                                                   xc[b][:, e, :], ALU.mult, ALU.add)
                    if tap:
                        link(ins)
                ins.then_inc(convolved.handle, 1)

            def take_x_tok(k, b, c):
                written(dve, k, "xtok", c, b)
                mark_read(dve.tensor_copy(x_tok[b][:, c, :], tile_of("xtok", c, b)[:, :]), "xtok", c, b)

            def take_xd(k, b):
                dve.wait_ge(c_placed.handle, c_placed.value(k, b, 1, ago=1))
                written(dve, k, "xdtok", 0, b)
                mark_read(dve.tensor_copy(xd[:, :, :], tile_of("xdtok", 0, b)[:, :]
                                          .rearrange("p (c w) -> p c w", w=P)[:, :, 0:XD]), "xdtok", 0, b)
                read(dve, k, "xdtok", 0, b)
                dve.scalar_tensor_tensor(soft[:, 0, :], xd[:, :, 0], -1.0, xd[:, :, 0], ALU.mult, ALU.max)\
                    .then_inc(abs_ready.handle, 1)

            def softplus(k, b):
                den, inv, q, sq, p, log_half, relu = (soft[:, n, :] for n in range(2, 9))
                dve.wait_ge(exp_ready.handle, exp_ready.value(k, b, 1))
                link(dve.tensor_scalar(den, soft[:, 1, :], 2.0, None, ALU.add))
                link(dve.reciprocal(inv, den))
                link(dve.tensor_tensor(q, soft[:, 1, :], inv, ALU.mult))
                link(dve.tensor_tensor(sq, q, q, ALU.mult))
                link(dve.tensor_scalar(p, sq, 1 / 13, None, ALU.mult))
                for c in ATANH:
                    link(dve.scalar_tensor_tensor(p, p, c, sq, ALU.add, ALU.mult))
                dve.tensor_scalar(relu, xd[:, :, 0], 0.0, None, ALU.max)
                link(dve.scalar_tensor_tensor(log_half, p, 1.0, q, ALU.add, ALU.mult))
                written(dve, k, "sums", 0, b, ago=1)
                link(dve.scalar_tensor_tensor(delta[:, :], log_half, 2.0, relu, ALU.mult, ALU.add))
                dve.wait_ge(bd_ready.handle, bd_ready.value(k, b, 1, ago=1))
                dve.tensor_tensor(dB[:, :, :], xd[:, :, 1:1 + NS], delta[:, :].unsqueeze(2).to_broadcast([P, GR, NS]),
                                  ALU.mult).then_inc(dB_ready.handle, 1)
                dve.tensor_tensor(dA[:, :, 0:NS], rates[:, :].unsqueeze(1).to_broadcast([P, GR, NS]),
                                  delta[:, :].unsqueeze(2).to_broadcast([P, GR, NS]), ALU.mult)
                dve.tensor_tensor(d_place[:, :, :], row_in_block[:, :].unsqueeze(1).to_broadcast([P, GR, BL]),
                                  delta[:, :].unsqueeze(2).to_broadcast([P, GR, BL]), ALU.mult)\
                    .then_inc(delta_ready.handle, 1)
                written(dve, k, "gap", 0, b, ago=1)
                dve.tensor_tensor(gap_w[:, :, :, :].rearrange("p c j n -> p c (j n)"),
                                  rate_before[:, :, :].rearrange(flat).unsqueeze(1).to_broadcast([P, GR, P]),
                                  delta[:, :].unsqueeze(2).to_broadcast([P, GR, P]), ALU.mult)\
                    .then_inc(gap_w_ready.handle, 1)

            def take_sums(k, b):
                bank = tile_of("sums", 0, b)
                written(dve, k, "sums", 0, b)
                dve.wait_ge(group_decay_ready.handle, group_decay_ready.value(k, b, 1, ago=1))
                dve.tensor_copy(group_sum[:, :], bank[:, 12:13])
                dve.tensor_tensor(sums_A[:, :, :], bank[:, 0:3 * GR].unsqueeze(2).to_broadcast([P, 3 * GR, NS]),
                                  rates[:, :].unsqueeze(1).to_broadcast([P, 3 * GR, NS]), ALU.mult)\
                    .then_inc(sums_ready.handle, 1)
                mark_read(dve.tensor_tensor(d_block[:, :, :], bank[:, 16:16 + GR * BL].rearrange("p (c u) -> p c u", u=BL),
                                            later_in_block[:, :].unsqueeze(1).to_broadcast([P, GR, BL]), ALU.mult),
                          "sums", 0, b)
                read(dve, k, "sums", 0, b)
                dve.wait_ge(diag_gaps.handle, diag_gaps.value(k, b, 1, ago=1))
                dve.tensor_tensor_scan(gaps[:, :, :].rearrange(flat), restart[:, :, :].rearrange(flat),
                                       d_block[:, :, :].rearrange(flat), 0.0, ALU.mult, ALU.add)\
                    .then_inc(gaps_ready.handle, 1)

            def weigh(k, b):
                dve.wait_ge(decays_ready.handle, decays_ready.value(k, b, 1))
                c_tok = xd[:, :, 1 + NS:XD]
                written(dve, k, "ct", 0, b, ago=1)
                dve.tensor_tensor(c_start[:, :, 0:NS], c_tok, decays[:, 0, :, :], ALU.mult)\
                    .then_inc(c_start_ready.handle, 1)
                link(dve.tensor_tensor(c_block[:, :, :], c_tok, decays[:, 1, :, :], ALU.mult))
                written(dve, k, "cbd", 0, b, ago=1)
                dve.tensor_tensor(cbd_tok[:, :, :, :], c_block[:, :, :].unsqueeze(2).to_broadcast([P, GR, NB, NS]),
                                  in_block[:, :].rearrange("p (j u) -> p j u", u=BL)[:, :, 0:1].unsqueeze(1)
                                  .to_broadcast([P, GR, NB, NS]), ALU.mult).then_inc(cbd_ready.handle, 1)
                written(dve, k, "u", 0, b, ago=1)
                dve.tensor_tensor(b_end[:, :, :], dB[:, :, :], decays[:, 2, :, :], ALU.mult)\
                    .then_inc(b_end_ready.handle, 1)

            def weigh_b(k, b):
                written(dve, k, "bd", 0, b)
                read(dve, k, "gap", 0, b)
                mark_read(dve.tensor_tensor(b_hat[:, :], b_hat[:, :], tile_of("bd", 0, b)[:, :], ALU.mult), "bd", 0, b)

            def advance_state(k, b):
                bank = tile_of("u", 0, b)
                dve.wait_ge(group_decay_ready.handle, group_decay_ready.value(k, b, 1))
                written(dve, k, "u", 0, b)
                written(dve, k, "y", CB - 1, b, ago=2)
                dve.wait_ge(first_state.handle, first_state.value(k, b, 1))
                for c in range(GR):
                    at = SLOT * c
                    before = state_end[b][:, :] if c == 0 else state[b][at:at + NS, :]
                    to = state_end[b][:, :] if c == GR - 1 else state[b][at + SLOT:at + SLOT + NS, :]
                    ins = dve.scalar_tensor_tensor(to, before, group_decay[at:at + NS, :], bank[at:at + NS, :],
                                                   ALU.mult, ALU.add)
                    if c == GR - 1:
                        mark_read(ins, "u", 0, b)
                    elif c == GR - 2:
                        ins.then_inc(states_ready.handle, 1)
                        dve.wait_ge(states_ready.handle, states_ready.value(k, b, 1))
                    else:
                        link(ins)

            def weigh_diagonal(k, b):
                dve.wait_ge(diag_exp.handle, diag_exp.value(k, b, 1))
                link(dve.tensor_tensor(diag[:, :, :, :], diag[:, :, :, :],
                                       dB[:, :, :].unsqueeze(3).to_broadcast([P, GR, NS, BL]), ALU.mult))
                for h in range(2):
                    written(dve, k, "cb", h, b)
                    part = diag[:, 2 * h:2 * h + 2, :, :].rearrange("p c n u -> p (c n u)")
                    mark_read(dve.tensor_tensor(part, part, tile_of("cb", h, b)[:, :], ALU.mult), "cb", h, b)
                    read(dve, k, "cb", h, b)
                dve.tensor_reduce(diag_sum[:, :, :], diag[:, :, :, :].rearrange("p c n u -> p c u n"), AXIS_X, ALU.add)\
                    .then_inc(diag_summed.handle, 1)
                dve.wait_ge(diag_summed.handle, diag_summed.value(k, b, 1))

            def assemble(k, b):
                written(dve, k, "y", CB - 1, b, ago=1)
                link(dve.tensor_tensor(m_mat[:, :].rearrange("p (c j u) -> p c j u", j=NB, u=BL),
                                       diag_sum[:, :, :].unsqueeze(2).to_broadcast([P, GR, NB, BL]),
                                       block_upto[:, :].rearrange("p (j u) -> p j u", u=BL).unsqueeze(1)
                                       .to_broadcast([P, GR, NB, BL]), ALU.mult))
                written(dve, k, "moff", 0, b)
                mark_read(dve.tensor_tensor(m_mat[:, :], m_mat[:, :], tile_of("moff", 0, b)[:, :], ALU.add), "moff", 0, b)

            def gate(k, b, g):
                if g == 0:
                    written(dve, k, "out", 1, b, ago=1)
                    dve.wait_ge(z_ready.handle, z_ready.value(k, b, 1))
                written(dve, k, "y", g, b)
                mark_read(dve.scalar_tensor_tensor(yg[:, g, :], xc[b][:, g, :], skip[:, g:g + 1],
                                                   tile_of("y", g, b)[:, :], ALU.mult, ALU.add), "y", g, b)
                read(dve, k, "y", g, b)
                dve.tensor_tensor(yg[:, g, :], yg[:, g, :], z[b][:, g, :], ALU.mult).then_inc(gated.handle, 1)

            def first_residual(k, b):
                dve.wait_ge(x1b_ready.handle, x1b_ready.value(k, b, 1, ago=1))
                for h in range(2):
                    written(dve, k, "out", h, b)
                    mark_read(dve.tensor_tensor(x1[:, 2 * h:2 * h + 2, :],
                                                tile_of("out", h, b)[:, :].rearrange("p (c d) -> p c d", d=DM),
                                                x_in[b][:, 2 * h:2 * h + 2, :], ALU.add), "out", h, b)
                    read(dve, k, "out", h, b)

            def second_norm(k, b):
                norm_stats(k, b, BATCH + b, x1, var2, link)
                written(dve, k, "ln2T", MB - 1, b, ago=1)
                normalise(k, b, BATCH + b, x1, xn2, rstd2, norm2)

            def first_norm(k, b, loaded):
                dve.wait_ge(x_loaded[b], loaded)
                dve.wait_ge(norm2.handle, norm2.value(k, 1, 1))
                dve.wait_ge(norm1.handle, norm1.value(k + 1, b, 0))
                norm_stats(k + 1, b, b, x_in[b], var1, link)
                written(dve, k, "ln1T", MB - 1, b)
                normalise(k + 1, b, b, x_in[b], xn1[b], rstd1, norm1)

            def final(k, b):
                dve.wait_ge(x1b_ready.handle, x1b_ready.value(k, b, 1))
                dve.wait_ge(out_stored.handle, out_stored.value(k, b, 16, ago=1))
                written(dve, k, "down", 0, b)
                mark_read(dve.tensor_tensor(y_out[:, :, :], acc[:, :, :], x1b, ALU.add), "down", 0, b)

            with dve.Fori(1, TILES + 1) as k:
                done = [0]

                def link(ins):
                    done[0] += 1
                    ins.then_inc(vector_steps.handle, 1)
                    dve.wait_ge(vector_steps.handle, vector_steps.value(k, 0, done[0]))

                for e in range(CB):
                    convolve(k, 0, e)
                take_x_tok(k, 0, 2)
                take_x_tok(k, 0, 3)
                convolve(k, 1, 0)
                take_xd(k, 0)
                convolve(k, 1, 1)
                softplus(k, 0)
                convolve(k, 1, 2)
                take_sums(k, 0)
                convolve(k, 1, 3)
                weigh(k, 0)
                weigh_b(k, 0)
                advance_state(k, 0)
                weigh_diagonal(k, 0)
                assemble(k, 0)
                take_x_tok(k, 1, 2)
                take_x_tok(k, 1, 3)
                take_xd(k, 1)
                for g in range(CB):
                    gate(k, 0, g)
                softplus(k, 1)
                first_residual(k, 0)
                second_norm(k, 0)
                take_sums(k, 1)
                weigh(k, 1)
                weigh_b(k, 1)
                advance_state(k, 1)
                weigh_diagonal(k, 1)
                assemble(k, 1)
                for g in range(CB):
                    gate(k, 1, g)
                first_residual(k, 1)
                second_norm(k, 1)
                final(k, 0)
                for b in range(BATCH):
                    first_norm(k, b, k * 16 + 16)
                final(k, 1)
                assert done[0] == VECTOR_STEPS, done[0]


_INS = ["L0_attn_x", "L0_attn_in_proj_w", "L0_attn_conv_w", "L0_attn_conv_b", "L0_attn_x_proj_w", "L0_attn_A_log",
        "L0_attn_D", "L0_attn_out_proj_w", "L0_ffn_W_exp", "L0_ffn_b_exp", "L0_ffn_up_weights", "L0_ffn_up_bias",
        "L0_ffn_down_weights", "L0_ffn_W_con", "L0_ffn_b_con", "L0_ffn_down_bias"]
_OUT = ((BATCH, LENGTH, DM), "float32")


def kernel(**inputs):
    import numpy as _np
    import concourse.bacc as _bacc
    from concourse import mybir as _mybir
    from concourse.bass_utils import run_bass_kernel_spmd as _run

    nc = _bacc.Bacc("TRN2", target_bir_lowering=False, num_devices=1)
    arrays, args = {}, []
    for name in _INS:
        a = _np.ascontiguousarray(inputs[name])
        arrays[f"in_{name}_dram"] = a
        args.append(nc.dram_tensor(f"in_{name}_dram", a.shape, _mybir.dt.from_np(a.dtype), kind="ExternalInput").ap())
    shape, dtype = _OUT
    args.append(nc.dram_tensor("out_dram", shape, _mybir.dt.from_np(_np.dtype(dtype)), kind="ExternalOutput").ap())
    bass_preln_ssm_butterfly_ffn(nc, *args)
    r = _run(nc, [arrays], core_ids=[0])
    return r.results[0]["out_dram"]
```

```python
from contextlib import ExitStack

import concourse.bass as bass
from concourse import mybir

F32 = mybir.dt.float32
F32R = mybir.dt.float32r
PARTS = ("high", "low")
PASSES = ((0, 0), (0, 1), (1, 0))
ALU = mybir.AluOpType
ACT = mybir.ActivationFunctionType
AXIS_X = mybir.AxisListType.X

P = 128
BATCH = 2
LENGTH = 2048
DM = 256
DI = 512
NS = 16
TAPS = 4
HID = 1024
TILE = 512
TILES = LENGTH // TILE
GR = TILE // P
MB = DM // P
CB = DI // P
HB = HID // P
BL = 16
NB = P // BL
HALO = TAPS - 1
XD = 1 + 2 * NS
SLOT = 32
LOW = 7
HIGH = 3
EPS = 1e-5
ATANH = [1 / 11, 1 / 9, 1 / 7, 1 / 5, 1 / 3]

WIDE_ORDER = (
    [("in", e, 0) for e in range(8)] + [("xp", 0, 0)] + [("in", e, 1) for e in range(8)] + [("xp", 0, 1)]
    + [("y", g, 0) for g in range(CB)] + [("out", 0, 0), ("out", 1, 0)]
    + [("up", j, 0) for j in range(4)] + [("y", g, 1) for g in range(CB)]
    + [("up", j, 0) for j in range(4, 6)] + [("out", 0, 1), ("out", 1, 1)]
    + [("up", 6, 0), ("up", 7, 0)] + [("up", j, 1) for j in range(HB)]
)
SMALL_ORDER = (
    [("ln1T", m, b) for b in range(BATCH) for m in range(MB)]
    + [("xtok", c, 0) for c in range(GR)] + [(name, 0, 0) for name in ("xdtok", "sums", "gap", "bd", "ct", "cbd", "u")]
    + [("cb", 0, 0), ("cb", 1, 0), ("moff", 0, 0)]
    + [("xtok", c, 1) for c in range(GR)] + [(name, 0, 1) for name in ("xdtok", "sums", "gap", "bd", "ct", "cbd", "u")]
    + [("ln2T", m, 0) for m in range(MB)] + [("cb", 0, 1), ("cb", 1, 1), ("moff", 0, 1)]
    + [("ln2T", m, 1) for m in range(MB)]
)
TAKES = {"ln1T": 2, "ln2T": 2}
RING = 3
HRING = 2
FIRST_HALF_STEPS, VECTOR_STEPS = 50, 58


class Signal:

    def __init__(self, handle, count):
        self.handle, self.count, self.total = handle, count, BATCH * count

    def value(self, k, b, n, ago=0):
        return k * self.total + (b - ago) * self.count + n


class Banks:

    def __init__(self, nc, ctx, name, tiles, order):
        self.tiles, self.order = tiles, order
        self.written = [ctx.enter_context(nc.semaphore(f"{name}{i}_written")) for i in range(len(tiles))]
        self.read = [ctx.enter_context(nc.semaphore(f"{name}{i}_read")) for i in range(len(tiles))]
        self.place, self.products, self.takes = {}, [0] * len(tiles), [0] * len(tiles)
        for n, use in enumerate(order):
            bank = n % len(tiles)
            before = self.takes[bank]
            self.products[bank] += 1
            self.takes[bank] += TAKES.get(use[0], 1)
            self.place[use] = (bank, self.products[bank], before, self.takes[bank])

    def bank(self, use):
        return self.place[use][0]

    def value(self, k, use, ago, of):
        name, i, b = use
        place = self.place[(name, i, (b - ago) % BATCH)]
        total = (self.products if of == "written" else self.takes)[place[0]]
        n = place[{"written": 1, "free": 2, "read": 3}[of]]
        return place[0], (k + (b - ago) // BATCH) * total + n


def bass_preln_ssm_butterfly_ffn(
    nc, x, in_proj_w, conv_w, conv_b, x_proj_w, A_log, D, out_proj_w,
    W_exp, b_exp, up_weights, up_bias, down_weights, W_con, b_con, down_bias, out,
):
    ctx = ExitStack()
    with ctx:
        def sb(name, shape, dt=F32):
            return ctx.enter_context(nc.sbuf_tensor(name, shape, dt))

        def sem(name):
            return ctx.enter_context(nc.semaphore(name))

        w_in = [sb(f"w_in_{part}", [P, MB, 2 * DI], F32R) for part in PARTS]
        w_x = sb("w_x", [P, CB, XD])
        w_out = sb("w_out", [P, CB, DM])
        w_up = [sb(f"w_up_{part}", [P, MB, HID], F32R) for part in PARTS]
        w_down = [sb(f"w_down_{part}", [P, HB, DM], F32R) for part in PARTS]
        bias_up = sb("bias_up", [P, HB])
        bias_out = sb("bias_out", [P, DM])
        taps = sb("taps", [P, CB, TAPS])
        tap_bias = sb("tap_bias", [P, CB])
        skip = sb("skip", [P, CB])
        rates = sb("rates", [P, NS])

        ident = sb("ident", [P, P])
        after = sb("after", [P, P])
        upto = sb("upto", [P, P])
        in_block = sb("in_block", [P, P])
        block_upto = sb("block_upto", [P, P])
        row_in_block = sb("row_in_block", [P, BL])
        later_in_block = sb("later_in_block", [P, BL])
        before_block = sb("before_block", [P, NB])
        restart = sb("restart", [P, GR, BL])
        ones = sb("ones", [P, P])
        minus_half = sb("minus_half", [P, GR])
        rate_before = sb("rate_before", [P, NB, NS])

        x_in = [sb(f"x_in{b}", [P, GR, DM]) for b in range(BATCH)]
        xn1 = [sb(f"xn1_{b}", [P, GR, DM]) for b in range(BATCH)]
        xnT = [sb(f"xnT_{part}", [P, MB, TILE], F32R) for part in PARTS]
        xi = sb("xi", [P, CB, HALO + TILE])
        halo = [sb(f"halo{b}", [P, CB, HALO]) for b in range(BATCH)]
        xc = [sb(f"xc{b}", [P, CB, TILE]) for b in range(BATCH)]
        z = [sb(f"z{b}", [P, CB, TILE]) for b in range(BATCH)]
        x_tok = sb("x_tok", [P, GR, DI])
        state = [sb(f"state{b}", [P, DI]) for b in range(BATCH)]
        state_end = [sb(f"state_end{b}", [NS, DI]) for b in range(BATCH)]
        xdT = sb("xdT", [P, TILE])
        xd = sb("xd", [P, GR, XD])
        soft = sb("soft", [P, 10, GR])
        delta = sb("delta", [P, GR])
        dB = sb("dB", [P, GR, NS])
        dA = sb("dA", [P, GR, SLOT])
        d_place = sb("d_place", [P, GR, BL])
        gap_w = sb("gap_w", [P, GR, NB, NS])
        bd_tok = sb("bd_tok", [P, GR, NB, NS])
        work = sb("work", [P, 2 * GR * NS * BL + HB])
        c_place, diag = (work[:, n * GR * NS * BL:(n + 1) * GR * NS * BL].rearrange("p (c n u) -> p c n u", c=GR, n=NS)
                         for n in range(2))
        sums_A = sb("sums_A", [P, 3 * GR, NS])
        decays = sb("decays", [P, 3, GR, NS])
        group_sum = sb("group_sum", [P, 1])
        group_decay = sb("group_decay", [P, 1])
        d_block = sb("d_block", [P, GR, BL])
        gaps = sb("gaps", [P, GR, BL])
        diag_sum = sb("diag_sum", [P, GR, BL])
        c_start = sb("c_start", [P, GR, P + SLOT])
        c_block = sb("c_block", [P, GR, NS])
        cbd_tok = sb("cbd_tok", [P, GR, NB, NS])
        b_end = sb("b_end", [P, GR, NS])
        b_hat = sb("b_hat", [P, TILE])
        c_hat = sb("c_hat", [P, TILE])
        c_startT = sb("c_startT", [P, TILE])
        m_mat = sb("m_mat", [P, TILE])
        yg = sb("yg", [P, CB, TILE])
        x1 = sb("x1", [P, GR, DM])
        x1b_xn2 = sb("x1b_xn2", [P, 2, GR, DM])
        x1b, xn2 = x1b_xn2[:, 0, :, :], x1b_xn2[:, 1, :, :]
        hid_f32 = sb("hid_f32", [P, HRING, TILE])
        hid = [sb(f"hid_{part}", [P, HRING, TILE], F32R) for part in PARTS]
        stats = sb("stats", [P, GR, 6])
        carrier = sb("carrier", [P, 1])
        mean_var = sb("mean_var", [P, GR, 2])
        var_eps = sb("var_eps", [P, 2 * BATCH, GR])
        rstd = sb("rstd", [P, 2 * BATCH, GR])

        wide = [ctx.enter_context(nc.psum_tensor(f"wide{i}", [P, TILE], F32)) for i in range(RING)]
        small = [ctx.enter_context(nc.psum_tensor(f"small{i}", [P, TILE], F32)) for i in range(RING)]
        acc = ctx.enter_context(nc.psum_tensor("acc", [P, GR, DM], F32))
        WIDE = Banks(nc, ctx, "wide", wide, WIDE_ORDER)
        SMALL = Banks(nc, ctx, "small", small, SMALL_ORDER)
        ACC = Banks(nc, ctx, "acc", [acc], [("down", 0, 0), ("down", 0, 1)])
        where = {name: banks for banks in (WIDE, SMALL, ACC) for name, _, _ in banks.order}

        def tile_of(name, i, b):
            return where[name].tiles[where[name].bank((name, i, b))]

        def written(eng, k, name, i, b, ago=0):
            bank, value = where[name].value(k, (name, i, b), ago, "written")
            eng.wait_ge(where[name].written[bank], value)

        def read(eng, k, name, i, b, ago=0, takes=None):
            bank, value = where[name].value(k, (name, i, b), ago, "read" if takes is None else "free")
            eng.wait_ge(where[name].read[bank], value + (takes or 0))

        def free(eng, k, name, i, b):
            bank, value = where[name].value(k, (name, i, b), 0, "free")
            eng.wait_ge(where[name].read[bank], value)

        def mark_written(ins, name, i, b):
            ins.then_inc(where[name].written[where[name].bank((name, i, b))], 1)

        def mark_read(ins, name, i, b):
            ins.then_inc(where[name].read[where[name].bank((name, i, b))], 1)

        x_loaded = [sem(f"x_loaded{b}") for b in range(BATCH)]
        out_stored = Signal(sem("out_stored"), 16)
        var1 = Signal(sem("var1"), 1)
        rstd1 = Signal(sem("rstd1"), 1)
        norm1 = Signal(sem("norm1"), 1)
        var2 = Signal(sem("var2"), 1)
        rstd2 = Signal(sem("rstd2"), 1)
        norm2 = Signal(sem("norm2"), 1)
        halo_moved = Signal(sem("halo_moved"), 1)
        halo_saved = Signal(sem("halo_saved"), 1)
        xi_copied = Signal(sem("xi_copied"), CB)
        convolved = Signal(sem("convolved"), CB)
        xc_ready = Signal(sem("xc_ready"), 1)
        z_ready = Signal(sem("z_ready"), 1)
        abs_ready = Signal(sem("abs_ready"), 1)
        exp_ready = Signal(sem("exp_ready"), 1)
        dB_ready = Signal(sem("dB_ready"), 1)
        delta_ready = Signal(sem("delta_ready"), 1)
        gap_w_ready = Signal(sem("gap_w_ready"), 1)
        c_placed = Signal(sem("c_placed"), 1)
        bd_ready = Signal(sem("bd_ready"), 1)
        sums_ready = Signal(sem("sums_ready"), 1)
        decays_ready = Signal(sem("decays_ready"), 1)
        group_decay_ready = Signal(sem("group_decay_ready"), 1)
        gaps_ready = Signal(sem("gaps_ready"), 1)
        diag_gaps = Signal(sem("diag_gaps"), 1)
        diag_exp = Signal(sem("diag_exp"), 1)
        diag_summed = Signal(sem("diag_summed"), 1)
        c_start_ready = Signal(sem("c_start_ready"), 1)
        cbd_ready = Signal(sem("cbd_ready"), 1)
        b_end_ready = Signal(sem("b_end_ready"), 1)
        first_state = Signal(sem("first_state"), 1)
        states_ready = Signal(sem("states_ready"), 1)
        gated = Signal(sem("gated"), CB)
        x1b_ready = Signal(sem("x1b_ready"), 1)
        hid_high = Signal(sem("hid_high"), HB)
        hid_ready = Signal(sem("hid_ready"), HB)
        down_steps = Signal(sem("down_steps"), HB - 1)
        vector_steps = Signal(sem("vector_steps"), VECTOR_STEPS // BATCH)

        by_vector = [var1, norm1, var2, norm2, convolved, abs_ready, dB_ready, delta_ready, gap_w_ready, sums_ready,
                     gaps_ready, diag_summed, c_start_ready, cbd_ready, b_end_ready, states_ready, gated, hid_ready]
        by_scalar = [halo_moved, xi_copied, xc_ready, z_ready, exp_ready, decays_ready, group_decay_ready, diag_exp,
                     first_state, halo_saved, hid_high]
        by_pool = [rstd1, rstd2, c_placed, bd_ready, diag_gaps, x1b_ready]

        def start(eng, signals):
            for s in signals:
                eng.sem_inc(s.handle, s.total)

        w_loaded = [sem(f"w_loaded{i}") for i in range(4)]
        s_loaded = sem("s_loaded")
        low_loaded = sem("low_loaded")
        x_small = sem("x_small")
        masks_made = sem("masks_made")
        mask_steps = sem("mask_steps")
        perm_made = sem("perm_made")
        made = sem("made")
        taken = sem("taken")
        highs = sem("highs")
        vector_setup = sem("vector_setup")
        prepared = sem("prepared")
        zeroed = sem("zeroed")
        rates_exp = sem("rates_exp")

        perm = x1[:, :, :].rearrange("p a b -> p (a b)")[:, 0:LOW * P].rearrange("p (s q) -> p s q", q=P)
        W1 = DM + 1
        flat = "p a b -> p (a b)"
        raw_in = xc[0][:, :, :].rearrange(flat).rearrange("p (e d) -> p e d", d=DM)
        raw_exp = xc[1][:, :, :].rearrange(flat).rearrange("p (m h) -> p m h", h=HID)
        raw_con = z[0][:, :, :].rearrange(flat).rearrange("p (g d) -> p g d", d=DM)
        raw_out = yg[:, 0:2, :]
        raw_x = yg[:, 2, :]
        wexpT = xi[:, :, :].rearrange(flat)[:, 0:HB * W1].rearrange("p (g m) -> p g m", m=W1)
        mixed = work[:, :].rearrange("p (g m) -> p g m", m=W1)
        con_mixed = x_tok[:, :, :].rearrange(flat).rearrange("p (g d) -> p g d", d=DM)
        paths = [z[1][:, 2 * i:2 * i + 2, :].rearrange(flat) for i in range(2)]
        pathT = hid_f32[:, :, :].rearrange(flat).rearrange("p (g j) -> p g j", j=P)
        low_w = [x_tok[:, :, :].rearrange(flat), x1b_xn2[:, :, :, :].rearrange("p a b c -> p (a b c)")]
        high_w = [sb(f"high_w{i}", [P, HIGH, HB // 2, 4]) for i in range(2)]
        bias_raw = sb("bias_raw", [P, 2, DM])
        up_bias_sb = sb("up_bias_sb", [P, HB])
        SMALL_LOADS = 14

        low_at = [0]
        for s in range(LOW):
            low_at.append(low_at[-1] + HID // 2**s)

        products = (
            [("w_in", m, h) for m in range(MB) for h in range(2)] + [("w_x", 0, 0)]
            + [("w_out", h, 0) for h in range(2)] + [("wexpT", q, 0) for q in range(4)]
            + [("low", i, q) for i in range(2) for q in range(4)]
            + [("pathT", h, 0) for h in range(2)] + [("up_low", g, 0) for g in range(HB)]
            + [("w_up", m, h) for m in range(MB) for h in range(2)]
            + [("w_down", q, 0) for q in range(4)]
        )
        number = {product: n for n, product in enumerate(products)}
        banks6 = wide + small

        def bank_for(product):
            return banks6[number[product] % len(banks6)]

        block = ctx.enter_context(nc.Block())

        @block.sync
        def _(sp):
            for b in range(BATCH):
                sp.dma_start(x_in[b][:, :, :], x[b, 0:TILE, :].rearrange("(c p) d -> p c d", p=P)).then_inc(x_loaded[b], 16)
            sp.dma_start(raw_in, in_proj_w.rearrange("(e p) d -> p e d", p=P)).then_inc(w_loaded[0], 16)
            sp.dma_start(raw_x[0:XD, :], x_proj_w).then_inc(x_small, 16)
            sp.dma_start(raw_out, out_proj_w.rearrange("(o p) d -> p o d", p=P)).then_inc(w_loaded[1], 16)
            sp.dma_start(raw_exp, W_exp.rearrange("(m p) h -> p m h", p=P)).then_inc(w_loaded[2], 16)
            sp.dma_start(raw_con, W_con.rearrange("(g p) d -> p g d", p=P)).then_inc(w_loaded[3], 16)
            for i, weights in enumerate((up_weights, down_weights)):
                for s in range(HIGH):
                    sp.dma_start(high_w[i][:, s, :, :],
                                 weights[LOW + s].rearrange("(q p) o i -> p q (o i)", p=P)).then_inc(s_loaded, 16)
            for n, row in enumerate((b_con, down_bias)):
                sp.dma_start(bias_raw[:, n, :], row.partition_broadcast(P)).then_inc(s_loaded, 16)
            sp.dma_start(rates[:, :], A_log.partition_broadcast(P)).then_inc(s_loaded, 16)
            sp.dma_start(taps[:, :, :], conv_w.rearrange("(g p) o k -> p g (o k)", p=P)).then_inc(s_loaded, 16)
            sp.dma_start(tap_bias[:, :], conv_b.rearrange("(g p) -> p g", p=P), allow_slow_non_contiguous=True).then_inc(s_loaded, 16)
            sp.dma_start(skip[:, :], D.rearrange("(g p) -> p g", p=P), allow_slow_non_contiguous=True).then_inc(s_loaded, 16)
            sp.dma_start(up_bias_sb[:, :], up_bias.rearrange("(g p) -> p g", p=P), allow_slow_non_contiguous=True).then_inc(s_loaded, 16)
            sp.dma_start(wexpT[:, :, DM], b_exp.rearrange("(g p) -> p g", p=P), allow_slow_non_contiguous=True).then_inc(s_loaded, 16)
            start(sp, [out_stored])

            def load(k, b):
                read(sp, k, "out", 1, b)
                sp.dma_start(x_in[b][:, :, :], x[b, bass.ds(k * TILE, TILE), :].rearrange("(c p) d -> p c d", p=P))\
                    .then_inc(x_loaded[b], 16)

            def store(k, b):
                read(sp, k, "down", 0, b)
                sp.dma_start(out[b, bass.ds((k - 1) * TILE, TILE), :].rearrange("(c p) d -> p c d", p=P),
                             x1b).then_inc(out_stored.handle, 16)

            with sp.Fori(1, TILES) as k:
                for b in range(BATCH):
                    load(k, b)
                for b in range(BATCH):
                    store(k, b)
            for b in range(BATCH):
                store(TILES, b)
            sp.wait_ge(out_stored.handle, out_stored.value(TILES, 1, 16))

        @block.gpsimd
        def _(pool):
            start(pool, by_pool)
            count = [0]

            def select(out_ap, in_ap, op, base, cm, pattern):
                pool.affine_select(out=out_ap, in_=in_ap, compare_op=op, fill=0.0, base=base, pattern=pattern,
                                   channel_multiplier=cm).then_inc(mask_steps, 1)
                count[0] += 1
                pool.wait_ge(mask_steps, count[0])

            pool.memset(ident[:, :], 0.0).then_inc(mask_steps, 1)
            pool.memset(ones[:, :], 1.0).then_inc(mask_steps, 1)
            pool.memset(restart[:, :, :], 1.0).then_inc(mask_steps, 1)
            pool.memset(minus_half[:, :], -0.5).then_inc(mask_steps, 1)
            count[0] = 4
            pool.wait_ge(mask_steps, count[0])
            pool.affine_select(out=ident[:, :], in_=ident[:, :], compare_op=ALU.not_equal, fill=1.0, base=0,
                               pattern=[[-1, P]], channel_multiplier=1).then_inc(masks_made, 1)
            for i, weights in enumerate((up_weights, down_weights)):
                for s in range(LOW):
                    half = 2**s
                    for o in range(2):
                        pool.dma_start(
                            low_w[i][o * half:(o + 1) * half, low_at[s]:low_at[s + 1]].rearrange("l (c i) -> l c i", i=2),
                            weights[s, :, o, :].rearrange("(c l) i -> l c i", l=half)).then_inc(low_loaded, 16)
            pool.memset(restart[:, :, 0], 0.0).then_inc(masks_made, 1)
            select(after[:, :], ones[:, :], ALU.is_gt, 0, 1, [[-1, P]])
            select(upto[:, :], ones[:, :], ALU.is_ge, 0, -1, [[1, P]])
            in_blocks = "p (j u) -> p j u"
            blk, blk_upto = (m[:, :].rearrange(in_blocks, u=BL) for m in (in_block, block_upto))
            select(blk, ones[:, :].rearrange(in_blocks, u=BL), ALU.is_ge, 0, 1, [[-BL, NB], [0, BL]])
            select(blk, blk, ALU.is_ge, BL - 1, -1, [[BL, NB], [0, BL]])
            select(blk_upto, blk, ALU.is_ge, 0, -1, [[BL, NB], [1, BL]])
            pool.affine_select(out=before_block[:, :], in_=ones[:, 0:NB], compare_op=ALU.is_gt, fill=0.0, base=0,
                               pattern=[[BL, NB]], channel_multiplier=-1).then_inc(masks_made, 1)

            def rstd_of(k, b, slot, var, ready):
                pool.wait_ge(var.handle, var.value(k, b, 1))
                pool.tensor_tensor(rstd[:, slot, :], var_eps[:, slot, :], minus_half[:, :], ALU.pow)\
                    .then_inc(ready.handle, 1)

            def place_c(k, b):
                read(pool, k, "xdtok", 0, b)
                written(pool, k, "cb", 1, b, ago=1)
                pool.tensor_tensor(c_place[:, :, :, :],
                                   xd[:, :, 1 + NS:XD].unsqueeze(3).to_broadcast([P, GR, NS, BL]),
                                   row_in_block[:, :].unsqueeze(1).unsqueeze(1).to_broadcast([P, GR, NS, BL]),
                                   ALU.mult).then_inc(c_placed.handle, 1)

            def mask_b(k, b):
                pool.wait_ge(dB_ready.handle, dB_ready.value(k, b, 1))
                written(pool, k, "bd", 0, b, ago=1)
                pool.tensor_tensor(bd_tok[:, :, :, :],
                                   dB[:, :, :].unsqueeze(2).to_broadcast([P, GR, NB, NS]),
                                   before_block[:, :].unsqueeze(1).unsqueeze(3).to_broadcast([P, GR, NB, NS]),
                                   ALU.mult).then_inc(bd_ready.handle, 1)

            def diagonal_gaps(k, b):
                pool.wait_ge(gaps_ready.handle, gaps_ready.value(k, b, 1))
                pool.wait_ge(diag_summed.handle, diag_summed.value(k, b, 1, ago=1))
                pool.tensor_tensor(diag[:, :, :, :],
                                   gaps[:, :, :].unsqueeze(2).to_broadcast([P, GR, NS, BL]),
                                   rates[:, :].unsqueeze(1).unsqueeze(3).to_broadcast([P, GR, NS, BL]),
                                   ALU.mult).then_inc(diag_gaps.handle, 1)

            def residual_with_bias(k, b):
                read(pool, k, "out", 1, b)
                pool.wait_ge(out_stored.handle, out_stored.value(k, b, 16, ago=1))
                pool.tensor_tensor(x1b, x1[:, :, :], bias_out[:, :].unsqueeze(1).to_broadcast([P, GR, DM]),
                                   ALU.add).then_inc(x1b_ready.handle, 1)

            def first_half(k):
                for b in range(BATCH):
                    place_c(k, b)
                    mask_b(k, b)
                    if b == 0:
                        diagonal_gaps(k, 0)
                rstd_of(k, 0, BATCH, var2, rstd2)

            def second_half(k, last=False):
                residual_with_bias(k, 0)
                diagonal_gaps(k, 1)
                rstd_of(k, 1, BATCH + 1, var2, rstd2)
                residual_with_bias(k, 1)
                if not last:
                    for b in range(BATCH):
                        rstd_of(k + 1, b, b, var1, rstd1)

            for b in range(BATCH):
                rstd_of(1, b, b, var1, rstd1)
            first_half(1)
            with pool.Fori(1, TILES) as k:
                second_half(k)
                first_half(k + 1)
            second_half(TILES, last=True)

        @block.tensor
        def _(pe):
            def begin(product):
                n = number[product]
                if n >= len(banks6):
                    pe.wait_ge(taken, n - len(banks6) + 1)
                return bank_for(product)

            pe.wait_ge(masks_made, 1)
            pe.wait_ge(w_loaded[0], 16)
            for m in range(MB):
                for h in range(2):
                    bank = begin(("w_in", m, h))
                    for q in range(4):
                        last = pe.transpose(bank[:, q * P:(q + 1) * P], raw_in[:, 4 * h + q, m * P:(m + 1) * P], ident[:, :])
                    last.then_inc(made, 1)
            pe.wait_ge(x_small, 16)
            bank = begin(("w_x", 0, 0))
            for g in range(CB):
                last = pe.transpose(bank[:, g * XD:(g + 1) * XD], raw_x[0:XD, g * P:(g + 1) * P], ident[0:XD, 0:XD])
            last.then_inc(made, 1)
            pe.wait_ge(w_loaded[1], 16)
            for h in range(2):
                bank = begin(("w_out", h, 0))
                for q in range(2):
                    for o in range(MB):
                        at = (q * MB + o) * P
                        last = pe.transpose(bank[:, at:at + P], raw_out[:, o, (2 * h + q) * P:(2 * h + q + 1) * P], ident[:, :])
                last.then_inc(made, 1)
            pe.wait_ge(w_loaded[2], 16)
            for q in range(4):
                bank = begin(("wexpT", q, 0))
                for g in range(2):
                    for m in range(MB):
                        at = (g * MB + m) * P
                        last = pe.transpose(bank[:, at:at + P], raw_exp[:, m, (2 * q + g) * P:(2 * q + g + 1) * P], ident[:, :])
                last.then_inc(made, 1)
            pe.wait_ge(perm_made, LOW)
            pe.wait_ge(low_loaded, 16 * 2 * 2 * LOW)
            for i in range(2):
                for q in range(4):
                    bank = begin(("low", i, q))
                    if q < 2:
                        parts = [(0, 512 * q, 512 * (q + 1), 0)]
                    elif q == 2:
                        parts = [(1, low_at[1], low_at[2], 0)]
                    else:
                        parts = [(s, low_at[s], low_at[s + 1], low_at[s] - low_at[2]) for s in range(2, LOW)]
                    for s, lo, hi, at in parts:
                        rows = 2**(s + 1)
                        last = pe.matmul(bank[:, at:at + hi - lo], perm[0:rows, s, :], low_w[i][0:rows, lo:hi],
                                         start=True, stop=True)
                    last.then_inc(made, 1)
            pe.wait_ge(prepared, 1)
            for h in range(2):
                bank = begin(("pathT", h, 0))
                for q in range(4):
                    g = 4 * h + q
                    last = pe.transpose(bank[:, q * P:(q + 1) * P], paths[0][:, g * P:(g + 1) * P], ident[:, :])
                last.then_inc(made, 1)
            pe.wait_ge(s_loaded, 16 * SMALL_LOADS)
            pe.wait_ge(taken, number[("pathT", 1, 0)] + 1)
            for g in range(HB):
                bank = begin(("up_low", g, 0))
                pe.matmul(bank[:, 0:W1], pathT[:, g, :], wexpT[:, g, :], start=True, stop=True).then_inc(made, 1)
            pe.wait_ge(prepared, 2)
            for m in range(MB):
                for h in range(2):
                    bank = begin(("w_up", m, h))
                    for q in range(4):
                        last = pe.transpose(bank[:, q * P:(q + 1) * P], wexpT[:, 4 * h + q, m * P:(m + 1) * P], ident[:, :])
                    last.then_inc(made, 1)
            pe.wait_ge(prepared, 3)
            for q in range(4):
                bank = begin(("w_down", q, 0))
                for g in range(2):
                    last = pe.matmul(bank[:, g * DM:(g + 1) * DM], paths[1][:, (2 * q + g) * P:(2 * q + g + 1) * P],
                                     con_mixed[:, 2 * q + g, :], start=True, stop=True)
                last.then_inc(made, 1)

            for banks in (WIDE, SMALL, ACC):
                for handle, total in zip(banks.written, banks.products):
                    pe.sem_inc(handle, total)
            start(pe, [down_steps])
            pe.wait_ge(zeroed, 1)
            pe.wait_ge(masks_made, 3)
            pe.wait_ge(taken, len(products))

            def transposes(k, name, b, source, ready):
                for m in range(MB):
                    bank = tile_of(name, m, b)
                    free(pe, k, name, m, b)
                    if m == 0:
                        pe.wait_ge(ready.handle, ready.value(k, b, 1))
                    for c in range(GR):
                        last = pe.transpose(bank[:, c * P:(c + 1) * P], source[:, c, m * P:(m + 1) * P], ident[:, :])
                    mark_written(last, name, m, b)

            def in_projection(k, b, e):
                bank = tile_of("in", e, b)
                free(pe, k, "in", e, b)
                if e == 0:
                    for m in range(MB):
                        read(pe, k, "ln1T", m, b)
                for n, (m, w, x) in enumerate((m, w, x) for m in range(MB) for w, x in PASSES):
                    last = pe.matmul(bank[:, :], w_in[w][:, m, e * P:(e + 1) * P], xnT[x][:, m, :],
                                     start=n == 0, stop=n == MB * len(PASSES) - 1)
                mark_written(last, "in", e, b)

            def x_projection(k, b):
                bank = tile_of("xp", 0, b)
                free(pe, k, "xp", 0, b)
                pe.wait_ge(xc_ready.handle, xc_ready.value(k, b, 1))
                for g in range(CB):
                    last = pe.matmul(bank[0:XD, :], w_x[:, g, :], xc[b][:, g, :], start=g == 0, stop=g == CB - 1)
                mark_written(last, "xp", 0, b)

            def tokens_first(k, b):
                for c in range(GR):
                    bank = tile_of("xtok", c, b)
                    free(pe, k, "xtok", c, b)
                    for g in range(CB):
                        last = pe.transpose(bank[:, g * P:(g + 1) * P], xc[b][:, g, c * P:(c + 1) * P], ident[:, :])
                    mark_written(last, "xtok", c, b)

            def xd_tokens_first(k, b):
                bank = tile_of("xdtok", 0, b)
                free(pe, k, "xdtok", 0, b)
                read(pe, k, "xp", 0, b)
                for c in range(GR):
                    last = pe.transpose(bank[:, c * P:(c + 1) * P], xdT[:, c * P:(c + 1) * P], ident[:, :])
                mark_written(last, "xdtok", 0, b)

            def step_sums(k, b):
                bank = tile_of("sums", 0, b)
                free(pe, k, "sums", 0, b)
                pe.wait_ge(delta_ready.handle, delta_ready.value(k, b, 1))
                for n, mask in enumerate((upto, block_upto, after)):
                    pe.matmul(bank[:, n * GR:(n + 1) * GR], mask[:, :], delta[:, :], start=True, stop=True)
                pe.matmul(bank[:, 12:13], dA[:, :, :].rearrange(flat), ones[:, 0:1], start=True, stop=True)
                mark_written(pe.matmul(bank[:, 16:16 + GR * BL], in_block[:, :], d_place[:, :, :].rearrange(flat),
                                       start=True, stop=True), "sums", 0, b)

            def gap_products(k, b):
                bank = tile_of("gap", 0, b)
                free(pe, k, "gap", 0, b)
                pe.wait_ge(gap_w_ready.handle, gap_w_ready.value(k, b, 1))
                for c in range(GR):
                    last = pe.matmul(bank[:, c * P:(c + 1) * P], gap_w[:, c, :, :].rearrange(flat), after[:, :],
                                     start=True, stop=True)
                mark_written(last, "gap", 0, b)

            def transpose_groups(k, name, b, source, ready):
                bank = tile_of(name, 0, b)
                free(pe, k, name, 0, b)
                pe.wait_ge(ready.handle, ready.value(k, b, 1))
                for c in range(GR):
                    last = pe.transpose(bank[:, c * P:(c + 1) * P], source(c), ident[:, :])
                mark_written(last, name, 0, b)

            def state_inputs(k, b):
                bank = tile_of("u", 0, b)
                free(pe, k, "u", 0, b)
                pe.wait_ge(b_end_ready.handle, b_end_ready.value(k, b, 1))
                for c in range(GR):
                    read(pe, k, "xtok", c, b)
                for c in range(GR):
                    last = pe.matmul(bank[SLOT * c:SLOT * c + NS, :], b_end[:, c, :], x_tok[:, c, :],
                                     start=True, stop=True)
                mark_written(last, "u", 0, b)

            def spread_c(k, b):
                for h in range(2):
                    bank = tile_of("cb", h, b)
                    free(pe, k, "cb", h, b)
                    if h == 0:
                        pe.wait_ge(c_placed.handle, c_placed.value(k, b, 1))
                    mark_written(pe.matmul(bank[:, :], in_block[:, :],
                                           c_place[:, 2 * h:2 * h + 2, :, :].rearrange("p c n u -> p (c n u)"),
                                           start=True, stop=True), "cb", h, b)

            def off_diagonal(k, b):
                bank = tile_of("moff", 0, b)
                free(pe, k, "moff", 0, b)
                read(pe, k, "bd", 0, b)
                read(pe, k, "cbd", 0, b)
                for c in range(GR):
                    last = pe.matmul(bank[:, c * P:(c + 1) * P], b_hat[:, c * P:(c + 1) * P], c_hat[:, c * P:(c + 1) * P],
                                     start=True, stop=True)
                mark_written(last, "moff", 0, b)

            def ssm_output(k, b, g):
                bank = tile_of("y", g, b)
                free(pe, k, "y", g, b)
                if g == 0:
                    read(pe, k, "moff", 0, b)
                    read(pe, k, "ct", 0, b)
                    pe.wait_ge(first_state.handle, first_state.value(k, b, 1))
                    pe.wait_ge(states_ready.handle, states_ready.value(k, b, 1))
                for c in range(GR):
                    pe.matmul(bank[:, c * P:(c + 1) * P], x_tok[:, c, g * P:(g + 1) * P], m_mat[:, c * P:(c + 1) * P],
                              start=c == 0, stop=False, skip_group_check=True)
                mark_written(pe.matmul(bank[:, :], state[b][:, g * P:(g + 1) * P], c_startT[:, :],
                                       start=False, stop=True, skip_group_check=True), "y", g, b)

            def out_projection(k, b, h):
                bank = tile_of("out", h, b)
                free(pe, k, "out", h, b)
                if h == 0:
                    pe.wait_ge(gated.handle, gated.value(k, b, CB))
                for q in range(2):
                    c = 2 * h + q
                    for g in range(CB):
                        last = pe.matmul(bank[:, q * DM:(q + 1) * DM], yg[:, g, c * P:(c + 1) * P], w_out[:, g, :],
                                         start=g == 0, stop=g == CB - 1)
                mark_written(last, "out", h, b)

            def up(k, b, j):
                bank = tile_of("up", j, b)
                free(pe, k, "up", j, b)
                if j == 0:
                    for m in range(MB):
                        read(pe, k, "ln2T", m, b)
                for n, (m, w, x) in enumerate((m, w, x) for m in range(MB) for w, x in PASSES):
                    last = pe.matmul(bank[:, :], w_up[w][:, m, j * P:(j + 1) * P], xnT[x][:, m, :],
                                     start=n == 0, stop=n == MB * len(PASSES) - 1)
                mark_written(last, "up", j, b)

            def down(k, b, j):
                if j == 0:
                    free(pe, k, "down", 0, b)
                pe.wait_ge(hid_ready.handle, hid_ready.value(k, b, j + 1))
                for c in range(GR):
                    for n, (h, w) in enumerate(PASSES):
                        last = pe.matmul(acc[:, c, :], hid[h][:, j % HRING, c * P:(c + 1) * P], w_down[w][:, j, :],
                                         start=j == 0 and c % 2 == 0 and n == 0,
                                         stop=j == HB - 1 and n == len(PASSES) - 1, skip_group_check=True)
                if j == HB - 1:
                    mark_written(last, "down", 0, b)
                else:
                    last.then_inc(down_steps.handle, 1)

            def decayed_b(k, b):
                gap_products(k, b)
                transpose_groups(k, "bd", b, lambda c: bd_tok[:, c, :, :].rearrange(flat), bd_ready)

            def decayed_c_and_states(k, b):
                transpose_groups(k, "ct", b, lambda c: c_start[:, :, :].rearrange(flat)[:, c * P:(c + 1) * P], c_start_ready)
                transpose_groups(k, "cbd", b, lambda c: cbd_tok[:, c, :, :].rearrange(flat), cbd_ready)
                state_inputs(k, b)

            def ffn(k, b, first, last):
                for j in range(first, last):
                    up(k, b, j)
                    if j >= HRING:
                        down(k, b, j - HRING)

            def first_half(k):
                for e in range(8):
                    in_projection(k, 0, e)
                transposes(k, "ln1T", 1, xn1[1], norm1)
                x_projection(k, 0)
                tokens_first(k, 0)
                in_projection(k, 1, 0)
                in_projection(k, 1, 1)
                xd_tokens_first(k, 0)
                in_projection(k, 1, 2)
                in_projection(k, 1, 3)
                in_projection(k, 1, 4)
                step_sums(k, 0)
                in_projection(k, 1, 5)
                decayed_b(k, 0)
                in_projection(k, 1, 6)
                in_projection(k, 1, 7)
                decayed_c_and_states(k, 0)
                spread_c(k, 0)
                x_projection(k, 1)
                off_diagonal(k, 0)
                for g in range(CB):
                    ssm_output(k, 0, g)
                tokens_first(k, 1)
                xd_tokens_first(k, 1)
                out_projection(k, 0, 0)
                out_projection(k, 0, 1)
                step_sums(k, 1)
                decayed_b(k, 1)
                decayed_c_and_states(k, 1)

            def second_half(k, last=False):
                transposes(k, "ln2T", 0, xn2, norm2)
                spread_c(k, 1)
                ffn(k, 0, 0, 2)
                off_diagonal(k, 1)
                ffn(k, 0, 2, 4)
                for g in range(CB):
                    ssm_output(k, 1, g)
                ffn(k, 0, 4, 6)
                out_projection(k, 1, 0)
                out_projection(k, 1, 1)
                ffn(k, 0, 6, HB)
                transposes(k, "ln2T", 1, xn2, norm2)
                down(k, 0, HB - 2)
                down(k, 0, HB - 1)
                ffn(k, 1, 0, HB)
                if not last:
                    transposes(k + 1, "ln1T", 0, xn1[0], norm1)
                down(k, 1, HB - 2)
                down(k, 1, HB - 1)

            transposes(1, "ln1T", 0, xn1[0], norm1)
            first_half(1)
            with pe.Fori(1, TILES) as k:
                second_half(k)
                first_half(k + 1)
            second_half(TILES, last=True)

        @block.scalar
        def _(act):
            start(act, by_scalar)

            def high_part(product, target):
                act.wait_ge(made, number[product] + 1)
                act.activation(target, bank_for(product)[:, :], ACT.Copy).then_inc(highs, 1)

            for m in range(MB):
                for h in range(2):
                    high_part(("w_in", m, h), w_in[0][:, m, h * 512:(h + 1) * 512])
            act.wait_ge(s_loaded, 16 * SMALL_LOADS)
            act.activation(rates[:, :], rates[:, :], ACT.Exp).then_inc(rates_exp, 1)
            for m in range(MB):
                for h in range(2):
                    high_part(("w_up", m, h), w_up[0][:, m, h * 512:(h + 1) * 512])
            for q in range(4):
                high_part(("w_down", q, 0), w_down[0][:, 2 * q:2 * q + 2, :].rearrange(flat))
            act.wait_ge(zeroed, 1)
            act.wait_ge(prepared, 4)

            def take(k, name, i, b, out_ap, in_ap, last=True, **how):
                written(act, k, name, i, b)
                how.setdefault("func", ACT.Copy)
                ins = act.activation(out_ap, in_ap, how.pop("func"), **how)
                if last:
                    mark_read(ins, name, i, b)
                return ins

            def high_parts(k, name, b, last_use):
                written(act, k, *last_use)
                for m in range(MB):
                    take(k, name, m, b, xnT[0][:, m, :], tile_of(name, m, b)[:, :])

            def place_halo(k, b):
                act.wait_ge(convolved.handle, convolved.value(k, b, CB, ago=1))
                act.wait_ge(halo_saved.handle, halo_saved.value(k, b, 1, ago=1))
                act.activation(xi[:, :, 0:HALO], halo[b][:, :, :], ACT.Copy).then_inc(halo_moved.handle, 1)
                act.wait_ge(halo_moved.handle, halo_moved.value(k, b, 1))

            def save_halo(k, b):
                act.wait_ge(xi_copied.handle, xi_copied.value(k, b, CB))
                act.activation(halo[b][:, :, :], xi[:, :, TILE:TILE + HALO], ACT.Copy).then_inc(halo_saved.handle, 1)

            def first_tap(k, b, e):
                bank = tile_of("in", e, b)
                if e == 0:
                    act.wait_ge(gated.handle, gated.value(k, b, CB, ago=2))
                    written(act, k, "xtok", GR - 1, b, ago=2)
                take(k, "in", e, b, xi[:, e, HALO:], bank[:, :], last=False).then_inc(xi_copied.handle, 1)
                mark_read(act.activation(xc[b][:, e, :], bank[:, :], ACT.Identity, bias=tap_bias[:, e:e + 1],
                                         scale=taps[:, e, TAPS - 1:TAPS]), "in", e, b)

            def copy_z(k, b, e):
                take(k, "in", e, b, z[b][:, e - CB, :], tile_of("in", e, b)[:, :])

            def silu_x(k, b):
                act.wait_ge(convolved.handle, convolved.value(k, b, CB))
                act.activation(xc[b][:, :, :], xc[b][:, :, :], ACT.Silu).then_inc(xc_ready.handle, 1)

            def silu_z(k, b):
                read(act, k, "in", 7, b)
                act.activation(z[b][:, :, :], z[b][:, :, :], ACT.Silu).then_inc(z_ready.handle, 1)

            def take_xd(k, b):
                written(act, k, "xdtok", 0, b, ago=1)
                take(k, "xp", 0, b, xdT[0:XD, :], tile_of("xp", 0, b)[0:XD, :])

            def take_x_tok(k, b, c):
                if c == 0:
                    written(act, k, "y", CB - 1, b, ago=1)
                take(k, "xtok", c, b, x_tok[:, c, :], tile_of("xtok", c, b)[:, :])

            def exp_abs(k, b):
                act.wait_ge(abs_ready.handle, abs_ready.value(k, b, 1))
                act.activation(soft[:, 1, :], soft[:, 0, :], ACT.Exp, scale=-1.0).then_inc(exp_ready.handle, 1)

            def exp_sums(k, b):
                act.wait_ge(sums_ready.handle, sums_ready.value(k, b, 1))
                act.activation(decays[:, :, :, :].rearrange("p a c n -> p (a c n)"),
                               sums_A[:, :, :].rearrange(flat), ACT.Exp).then_inc(decays_ready.handle, 1)
                read(act, k, "u", 0, b, ago=1)
                act.activation(group_decay[:, :], group_sum[:, :], ACT.Exp).then_inc(group_decay_ready.handle, 1)

            def exp_gaps(k, b):
                written(act, k, "moff", 0, b, ago=1)
                take(k, "gap", 0, b, b_hat[:, :], tile_of("gap", 0, b)[:, :], func=ACT.Exp)

            def take_c(k, b):
                written(act, k, "y", CB - 1, b, ago=1)
                take(k, "ct", 0, b, c_startT[:, :], tile_of("ct", 0, b)[:, :])
                written(act, k, "moff", 0, b, ago=1)
                take(k, "cbd", 0, b, c_hat[:, :], tile_of("cbd", 0, b)[:, :])

            def copy_first_state(k, b):
                read(act, k, "u", 0, b, ago=2)
                written(act, k, "y", CB - 1, b, ago=2)
                act.activation(state[b][0:NS, :], state_end[b][:, :], ACT.Copy).then_inc(first_state.handle, 1)

            def exp_diagonal(k, b):
                act.wait_ge(diag_gaps.handle, diag_gaps.value(k, b, 1))
                whole = diag[:, :, :, :].rearrange("p c n u -> p (c n u)")
                act.activation(whole, whole, ACT.Exp).then_inc(diag_exp.handle, 1)

            def gelu(k, b, j):
                if j >= HRING:
                    act.wait_ge(down_steps.handle, down_steps.value(k, b, j - HRING + 1))
                elif j == HRING - 1:
                    written(act, k, "down", 0, b, ago=1)
                else:
                    act.wait_ge(down_steps.handle, down_steps.value(k, b, HB - 1, ago=1))
                take(k, "up", j, b, hid_f32[:, j % HRING, :], tile_of("up", j, b)[:, :], func=ACT.Gelu,
                     bias=bias_up[:, j:j + 1])
                read(act, k, "up", j, b)
                act.activation(hid[0][:, j % HRING, :], hid_f32[:, j % HRING, :], ACT.Copy).then_inc(hid_high.handle, 1)

            def first_half(k):
                place_halo(k, 0)
                for e in range(CB):
                    first_tap(k, 0, e)
                save_halo(k, 0)
                copy_z(k, 0, 4)
                copy_z(k, 0, 5)
                silu_x(k, 0)
                copy_z(k, 0, 6)
                copy_z(k, 0, 7)
                high_parts(k, "ln1T", 1, ("in", 7, 0))
                take_xd(k, 0)
                take_x_tok(k, 0, 0)
                take_x_tok(k, 0, 1)
                place_halo(k, 1)
                first_tap(k, 1, 0)
                exp_abs(k, 0)
                for e in range(1, CB):
                    first_tap(k, 1, e)
                save_halo(k, 1)
                copy_z(k, 1, 4)
                exp_sums(k, 0)
                copy_z(k, 1, 5)
                exp_gaps(k, 0)
                copy_z(k, 1, 6)
                copy_z(k, 1, 7)
                exp_diagonal(k, 0)
                take_c(k, 0)
                copy_first_state(k, 0)
                silu_x(k, 1)
                silu_z(k, 0)
                silu_z(k, 1)
                take_xd(k, 1)
                take_x_tok(k, 1, 0)
                take_x_tok(k, 1, 1)
                exp_abs(k, 1)
                exp_sums(k, 1)
                exp_gaps(k, 1)
                take_c(k, 1)
                copy_first_state(k, 1)

            def second_half(k, last=False):
                high_parts(k, "ln2T", 0, ("in", 7, 1))
                exp_diagonal(k, 1)
                for j in range(HB):
                    gelu(k, 0, j)
                high_parts(k, "ln2T", 1, ("up", 7, 0))
                for j in range(HB):
                    gelu(k, 1, j)
                if not last:
                    high_parts(k + 1, "ln1T", 0, ("up", 7, 0, 1))

            high_parts(1, "ln1T", 0, ("up", 7, 0, 1))
            first_half(1)
            with act.Fori(1, TILES) as k:
                second_half(k)
                first_half(k + 1)
            second_half(TILES, last=True)

        @block.vector
        def _(dve):
            done = [0]

            def link(ins):
                done[0] += 1
                ins.then_inc(vector_setup, 1)
                dve.wait_ge(vector_setup, done[0])

            def norm_stats(k, b, slot, source, var, link):
                for c in range(GR):
                    ins = dve.bn_stats(stats[:, c, :], source[:, c, :])
                link(ins)
                dve.memset(carrier[:, :], 0.0)
                for c in range(GR):
                    ins = dve.bn_aggr(mean_var[:, c, :], stats[:, c, :])
                link(ins)
                dve.tensor_scalar(var_eps[:, slot, :], mean_var[:, :, 1], EPS, None, ALU.add).then_inc(var.handle, 1)

            def normalise(k, b, slot, source, target, ready, normed):
                dve.wait_ge(ready.handle, ready.value(k, b, 1))
                for c in range(GR):
                    ins = dve.tensor_scalar(target[:, c, :], source[:, c, :], mean_var[:, c, 0:1],
                                            rstd[:, slot, c:c + 1], ALU.subtract, ALU.mult)
                ins.then_inc(normed.handle, 1)

            start(dve, by_vector)
            for banks in (WIDE, SMALL, ACC):
                for handle, total in zip(banks.read, banks.takes):
                    dve.sem_inc(handle, total)
            dve.wait_ge(masks_made, 1)
            for s in range(LOW):
                rows = 2**(s + 1)
                dve.tensor_copy(perm[0:rows, s, :].rearrange("q (r w) -> q r w", w=rows),
                                ident[0:rows, 0:rows].unsqueeze(1).to_broadcast([rows, P // rows, rows]))\
                    .then_inc(perm_made, 1)
            for b in range(BATCH):
                dve.wait_ge(x_loaded[b], 16)
                norm_stats(1, b, b, x_in[b], var1, link)
                normalise(1, b, b, x_in[b], xn1[b], rstd1, norm1)
                dve.wait_ge(norm1.handle, norm1.value(1, b, 1))
            dve.wait_ge(masks_made, 3)
            dve.wait_ge(rates_exp, 1)
            dve.tensor_reduce(row_in_block[:, :], ident[:, :].rearrange("p (j u) -> p u j", u=BL), AXIS_X, ALU.add)
            dve.tensor_tensor(m_mat[:, 0:P], block_upto[:, :], ident[:, :], ALU.subtract)
            link(dve.tensor_scalar(rates[:, :], rates[:, :], -1.0, None, ALU.mult))
            dve.tensor_reduce(later_in_block[:, :], m_mat[:, 0:P].rearrange("p (j u) -> p u j", u=BL), AXIS_X, ALU.add)
            dve.tensor_tensor(rate_before[:, :, :], before_block[:, :].unsqueeze(2).to_broadcast([P, NB, NS]),
                              rates[:, :].unsqueeze(1).to_broadcast([P, NB, NS]), ALU.mult)
            dve.tensor_tensor(bias_out[:, :], bias_raw[:, 0, :], bias_raw[:, 1, :], ALU.add)

            def receive(product, target, source, op=None, other=None):
                dve.wait_ge(made, number[product] + 1)
                if op is None:
                    ins = dve.tensor_copy(target, source)
                else:
                    ins = dve.tensor_tensor(target, other, source, op)
                ins.then_inc(taken, 1)
                dve.wait_ge(taken, number[product] + 1)

            high_count = [0]

            def low_part(product, low, high):
                high_count[0] += 1
                dve.wait_ge(highs, high_count[0])
                dve.tensor_tensor(low, bank_for(product)[:, :], high.bitcast(F32), ALU.subtract).then_inc(taken, 1)
                dve.wait_ge(taken, number[product] + 1)

            for m in range(MB):
                for h in range(2):
                    low_part(("w_in", m, h), *(w_in[part][:, m, h * 512:(h + 1) * 512] for part in (1, 0)))
            receive(("w_x", 0, 0), w_x[:, :, :].rearrange(flat), bank_for(("w_x", 0, 0))[:, 0:CB * XD])
            for h in range(2):
                receive(("w_out", h, 0), w_out[:, 2 * h:2 * h + 2, :].rearrange(flat), bank_for(("w_out", h, 0))[:, :])
            for q in range(4):
                receive(("wexpT", q, 0), wexpT[:, 2 * q:2 * q + 2, 0:DM],
                        bank_for(("wexpT", q, 0))[:, :].rearrange("p (g m) -> p g m", m=DM))
            for i in range(2):
                path = paths[i]
                for q in range(2):
                    receive(("low", i, q), path[:, 512 * q:512 * (q + 1)], bank_for(("low", i, q))[:, :])
                for s in range(1, LOW):
                    wide_as = path.rearrange("p (m w) -> p m w", w=2**s)
                    cols = HID // 2**s
                    bank = bank_for(("low", i, 2 if s == 1 else 3))
                    at = 0 if s == 1 else low_at[s] - low_at[2]
                    weights = bank[:, at:at + cols].unsqueeze(2).to_broadcast([P, cols, 2**s])
                    if s == 1:
                        receive(("low", i, 2), wide_as, weights, ALU.mult, wide_as)
                    elif s < LOW - 1:
                        if s == 2:
                            dve.wait_ge(made, number[("low", i, 3)] + 1)
                        link(dve.tensor_tensor(wide_as, wide_as, weights, ALU.mult))
                    else:
                        receive(("low", i, 3), wide_as, weights, ALU.mult, wide_as)
                if i == 0:
                    dve.sem_inc(prepared, 1)
            for h in range(2):
                receive(("pathT", h, 0), pathT[:, 4 * h:4 * h + 4, :].rearrange(flat), bank_for(("pathT", h, 0))[:, :])
            for g in range(HB):
                receive(("up_low", g, 0), mixed[:, g, :], bank_for(("up_low", g, 0))[:, 0:W1])

            def mix(weights, stage, source, target, transposed):
                span = 2**stage
                weight = lambda q, o, i: weights[:, stage, q, (2 * i + o if transposed else 2 * o + i):][:, 0:1]
                pairs = [(g // span % 2, g) for g in range(HB)]
                for o, g in pairs:
                    low = g - o * span
                    q = (low // (2 * span)) * span + low % span
                    ins = dve.tensor_scalar(target[:, g, :], source[:, low, :], weight(q, o, 0), None, ALU.mult)
                link(ins)
                for o, g in pairs:
                    low = g - o * span
                    q = (low // (2 * span)) * span + low % span
                    ins = dve.scalar_tensor_tensor(target[:, g, :], source[:, low + span, :], weight(q, o, 1),
                                                   target[:, g, :], ALU.mult, ALU.add)
                link(ins)

            dve.wait_ge(made, number[("up_low", HB - 1, 0)] + 1)
            mix(high_w[0], 0, mixed, wexpT, False)
            mix(high_w[0], 1, wexpT, mixed, False)
            mix(high_w[0], 2, mixed, wexpT, False)
            dve.tensor_tensor(bias_up[:, :], wexpT[:, :, DM], up_bias_sb[:, :], ALU.add).then_inc(prepared, 1)
            dve.wait_ge(w_loaded[3], 16)
            mix(high_w[1], 2, raw_con, con_mixed, True)
            mix(high_w[1], 1, con_mixed, raw_con, True)
            mix(high_w[1], 0, raw_con, con_mixed, True)
            dve.sem_inc(prepared, 1)
            for m in range(MB):
                for h in range(2):
                    low_part(("w_up", m, h), *(w_up[part][:, m, h * 512:(h + 1) * 512] for part in (1, 0)))
            for q in range(4):
                low_part(("w_down", q, 0), *(w_down[part][:, 2 * q:2 * q + 2, :].rearrange(flat) for part in (1, 0)))
            dve.sem_inc(prepared, 1)
            dve.memset(xdT[:, :], 0.0)
            dve.memset(dA[:, :, :], 0.0)
            dve.memset(c_start[:, :, :], 0.0)
            for b in range(BATCH):
                dve.memset(state[b][:, :], 0.0)
                dve.memset(state_end[b][:, :], 0.0)
                ins = dve.memset(halo[b][:, :, :], 0.0)
            ins.then_inc(zeroed, 1)
            dve.wait_ge(zeroed, 1)
            start(dve, [vector_steps])

            def convolve(k, b, e):
                read(dve, k, "in", e, b)
                for tap in range(TAPS - 2, -1, -1):
                    ins = dve.scalar_tensor_tensor(xc[b][:, e, :], xi[:, e, tap:tap + TILE], taps[:, e, tap:tap + 1],
                                                   xc[b][:, e, :], ALU.mult, ALU.add)
                    if tap:
                        link(ins)
                ins.then_inc(convolved.handle, 1)

            def low_parts(k, name, b):
                for m in range(MB):
                    read(dve, k, name, m, b, takes=1)
                    mark_read(dve.tensor_tensor(xnT[1][:, m, :], tile_of(name, m, b)[:, :],
                                                xnT[0][:, m, :].bitcast(F32), ALU.subtract), name, m, b)

            def low_hidden(k, b, *blocks):
                for j in blocks:
                    dve.wait_ge(hid_high.handle, hid_high.value(k, b, j + 1))
                    dve.tensor_tensor(hid[1][:, j % HRING, :], hid_f32[:, j % HRING, :],
                                      hid[0][:, j % HRING, :].bitcast(F32), ALU.subtract).then_inc(hid_ready.handle, 1)

            def take_x_tok(k, b, c):
                written(dve, k, "y", CB - 1, b, ago=1)
                written(dve, k, "xtok", c, b)
                mark_read(dve.tensor_copy(x_tok[:, c, :], tile_of("xtok", c, b)[:, :]), "xtok", c, b)

            def take_xd(k, b):
                dve.wait_ge(c_placed.handle, c_placed.value(k, b, 1, ago=1))
                written(dve, k, "xdtok", 0, b)
                mark_read(dve.tensor_copy(xd[:, :, :], tile_of("xdtok", 0, b)[:, :]
                                          .rearrange("p (c w) -> p c w", w=P)[:, :, 0:XD]), "xdtok", 0, b)
                read(dve, k, "xdtok", 0, b)
                dve.scalar_tensor_tensor(soft[:, 0, :], xd[:, :, 0], -1.0, xd[:, :, 0], ALU.mult, ALU.max)\
                    .then_inc(abs_ready.handle, 1)

            def softplus(k, b):
                den, inv, q, sq, p, log_half, relu = (soft[:, n, :] for n in range(2, 9))
                dve.wait_ge(exp_ready.handle, exp_ready.value(k, b, 1))
                link(dve.tensor_scalar(den, soft[:, 1, :], 2.0, None, ALU.add))
                link(dve.reciprocal(inv, den))
                link(dve.tensor_tensor(q, soft[:, 1, :], inv, ALU.mult))
                link(dve.tensor_tensor(sq, q, q, ALU.mult))
                link(dve.tensor_scalar(p, sq, 1 / 13, None, ALU.mult))
                for c in ATANH:
                    link(dve.scalar_tensor_tensor(p, p, c, sq, ALU.add, ALU.mult))
                dve.tensor_scalar(relu, xd[:, :, 0], 0.0, None, ALU.max)
                link(dve.scalar_tensor_tensor(log_half, p, 1.0, q, ALU.add, ALU.mult))
                written(dve, k, "sums", 0, b, ago=1)
                link(dve.scalar_tensor_tensor(delta[:, :], log_half, 2.0, relu, ALU.mult, ALU.add))
                dve.wait_ge(bd_ready.handle, bd_ready.value(k, b, 1, ago=1))
                dve.tensor_tensor(dB[:, :, :], xd[:, :, 1:1 + NS], delta[:, :].unsqueeze(2).to_broadcast([P, GR, NS]),
                                  ALU.mult).then_inc(dB_ready.handle, 1)
                dve.tensor_tensor(dA[:, :, 0:NS], rates[:, :].unsqueeze(1).to_broadcast([P, GR, NS]),
                                  delta[:, :].unsqueeze(2).to_broadcast([P, GR, NS]), ALU.mult)
                dve.tensor_tensor(d_place[:, :, :], row_in_block[:, :].unsqueeze(1).to_broadcast([P, GR, BL]),
                                  delta[:, :].unsqueeze(2).to_broadcast([P, GR, BL]), ALU.mult)\
                    .then_inc(delta_ready.handle, 1)
                written(dve, k, "gap", 0, b, ago=1)
                dve.tensor_tensor(gap_w[:, :, :, :].rearrange("p c j n -> p c (j n)"),
                                  rate_before[:, :, :].rearrange(flat).unsqueeze(1).to_broadcast([P, GR, P]),
                                  delta[:, :].unsqueeze(2).to_broadcast([P, GR, P]), ALU.mult)\
                    .then_inc(gap_w_ready.handle, 1)

            def take_sums(k, b):
                bank = tile_of("sums", 0, b)
                written(dve, k, "sums", 0, b)
                dve.wait_ge(group_decay_ready.handle, group_decay_ready.value(k, b, 1, ago=1))
                dve.tensor_copy(group_sum[:, :], bank[:, 12:13])
                dve.tensor_tensor(sums_A[:, :, :], bank[:, 0:3 * GR].unsqueeze(2).to_broadcast([P, 3 * GR, NS]),
                                  rates[:, :].unsqueeze(1).to_broadcast([P, 3 * GR, NS]), ALU.mult)\
                    .then_inc(sums_ready.handle, 1)
                mark_read(dve.tensor_tensor(d_block[:, :, :], bank[:, 16:16 + GR * BL].rearrange("p (c u) -> p c u", u=BL),
                                            later_in_block[:, :].unsqueeze(1).to_broadcast([P, GR, BL]), ALU.mult),
                          "sums", 0, b)
                read(dve, k, "sums", 0, b)
                dve.wait_ge(diag_gaps.handle, diag_gaps.value(k, b, 1, ago=1))
                dve.tensor_tensor_scan(gaps[:, :, :].rearrange(flat), restart[:, :, :].rearrange(flat),
                                       d_block[:, :, :].rearrange(flat), 0.0, ALU.mult, ALU.add)\
                    .then_inc(gaps_ready.handle, 1)

            def weigh(k, b):
                dve.wait_ge(decays_ready.handle, decays_ready.value(k, b, 1))
                c_tok = xd[:, :, 1 + NS:XD]
                written(dve, k, "ct", 0, b, ago=1)
                dve.tensor_tensor(c_start[:, :, 0:NS], c_tok, decays[:, 0, :, :], ALU.mult)\
                    .then_inc(c_start_ready.handle, 1)
                link(dve.tensor_tensor(c_block[:, :, :], c_tok, decays[:, 1, :, :], ALU.mult))
                written(dve, k, "cbd", 0, b, ago=1)
                dve.tensor_tensor(cbd_tok[:, :, :, :], c_block[:, :, :].unsqueeze(2).to_broadcast([P, GR, NB, NS]),
                                  in_block[:, :].rearrange("p (j u) -> p j u", u=BL)[:, :, 0:1].unsqueeze(1)
                                  .to_broadcast([P, GR, NB, NS]), ALU.mult).then_inc(cbd_ready.handle, 1)
                written(dve, k, "u", 0, b, ago=1)
                dve.tensor_tensor(b_end[:, :, :], dB[:, :, :], decays[:, 2, :, :], ALU.mult)\
                    .then_inc(b_end_ready.handle, 1)

            def weigh_b(k, b):
                written(dve, k, "bd", 0, b)
                read(dve, k, "gap", 0, b)
                mark_read(dve.tensor_tensor(b_hat[:, :], b_hat[:, :], tile_of("bd", 0, b)[:, :], ALU.mult), "bd", 0, b)

            def advance_state(k, b):
                bank = tile_of("u", 0, b)
                dve.wait_ge(group_decay_ready.handle, group_decay_ready.value(k, b, 1))
                written(dve, k, "u", 0, b)
                written(dve, k, "y", CB - 1, b, ago=2)
                dve.wait_ge(first_state.handle, first_state.value(k, b, 1))
                for c in range(GR):
                    at = SLOT * c
                    before = state_end[b][:, :] if c == 0 else state[b][at:at + NS, :]
                    to = state_end[b][:, :] if c == GR - 1 else state[b][at + SLOT:at + SLOT + NS, :]
                    ins = dve.scalar_tensor_tensor(to, before, group_decay[at:at + NS, :], bank[at:at + NS, :],
                                                   ALU.mult, ALU.add)
                    if c == GR - 1:
                        mark_read(ins, "u", 0, b)
                    elif c == GR - 2:
                        ins.then_inc(states_ready.handle, 1)
                        dve.wait_ge(states_ready.handle, states_ready.value(k, b, 1))
                    else:
                        link(ins)

            def weigh_diagonal(k, b):
                dve.wait_ge(diag_exp.handle, diag_exp.value(k, b, 1))
                link(dve.tensor_tensor(diag[:, :, :, :], diag[:, :, :, :],
                                       dB[:, :, :].unsqueeze(3).to_broadcast([P, GR, NS, BL]), ALU.mult))
                for h in range(2):
                    written(dve, k, "cb", h, b)
                    part = diag[:, 2 * h:2 * h + 2, :, :].rearrange("p c n u -> p (c n u)")
                    mark_read(dve.tensor_tensor(part, part, tile_of("cb", h, b)[:, :], ALU.mult), "cb", h, b)
                    read(dve, k, "cb", h, b)
                dve.tensor_reduce(diag_sum[:, :, :], diag[:, :, :, :].rearrange("p c n u -> p c u n"), AXIS_X, ALU.add)\
                    .then_inc(diag_summed.handle, 1)
                dve.wait_ge(diag_summed.handle, diag_summed.value(k, b, 1))

            def assemble(k, b):
                written(dve, k, "y", CB - 1, b, ago=1)
                link(dve.tensor_tensor(m_mat[:, :].rearrange("p (c j u) -> p c j u", j=NB, u=BL),
                                       diag_sum[:, :, :].unsqueeze(2).to_broadcast([P, GR, NB, BL]),
                                       block_upto[:, :].rearrange("p (j u) -> p j u", u=BL).unsqueeze(1)
                                       .to_broadcast([P, GR, NB, BL]), ALU.mult))
                written(dve, k, "moff", 0, b)
                mark_read(dve.tensor_tensor(m_mat[:, :], m_mat[:, :], tile_of("moff", 0, b)[:, :], ALU.add), "moff", 0, b)

            def gate(k, b, g):
                if g == 0:
                    written(dve, k, "out", 1, b, ago=1)
                    dve.wait_ge(z_ready.handle, z_ready.value(k, b, 1))
                written(dve, k, "y", g, b)
                mark_read(dve.scalar_tensor_tensor(yg[:, g, :], xc[b][:, g, :], skip[:, g:g + 1],
                                                   tile_of("y", g, b)[:, :], ALU.mult, ALU.add), "y", g, b)
                read(dve, k, "y", g, b)
                dve.tensor_tensor(yg[:, g, :], yg[:, g, :], z[b][:, g, :], ALU.mult).then_inc(gated.handle, 1)

            def first_residual(k, b):
                dve.wait_ge(x1b_ready.handle, x1b_ready.value(k, b, 1, ago=1))
                for h in range(2):
                    written(dve, k, "out", h, b)
                    mark_read(dve.tensor_tensor(x1[:, 2 * h:2 * h + 2, :],
                                                tile_of("out", h, b)[:, :].rearrange("p (c d) -> p c d", d=DM),
                                                x_in[b][:, 2 * h:2 * h + 2, :], ALU.add), "out", h, b)
                    read(dve, k, "out", h, b)

            def second_norm(k, b):
                norm_stats(k, b, BATCH + b, x1, var2, link)
                written(dve, k, "ln2T", MB - 1, b, ago=1)
                normalise(k, b, BATCH + b, x1, xn2, rstd2, norm2)

            def first_norm(k, b, loaded):
                dve.wait_ge(x_loaded[b], loaded)
                dve.wait_ge(norm2.handle, norm2.value(k, 1, 1))
                dve.wait_ge(norm1.handle, norm1.value(k + 1, b, 0))
                norm_stats(k + 1, b, b, x_in[b], var1, link)
                written(dve, k, "ln1T", MB - 1, b)
                normalise(k + 1, b, b, x_in[b], xn1[b], rstd1, norm1)

            def final(k, b):
                dve.wait_ge(x1b_ready.handle, x1b_ready.value(k, b, 1))
                written(dve, k, "down", 0, b)
                mark_read(dve.tensor_tensor(x1b, acc[:, :, :], x1b, ALU.add), "down", 0, b)

            at = [None, 0]

            def link(ins):
                at[1] += 1
                ins.then_inc(vector_steps.handle, 1)
                dve.wait_ge(vector_steps.handle, vector_steps.value(at[0], 0, at[1]))

            def first_half(k):
                at[:] = [k, 0]
                for e in range(CB):
                    convolve(k, 0, e)
                low_parts(k, "ln1T", 1)
                take_x_tok(k, 0, 2)
                take_x_tok(k, 0, 3)
                take_xd(k, 0)
                convolve(k, 1, 0)
                softplus(k, 0)
                for e in range(1, CB):
                    convolve(k, 1, e)
                take_sums(k, 0)
                weigh(k, 0)
                weigh_b(k, 0)
                advance_state(k, 0)
                weigh_diagonal(k, 0)
                assemble(k, 0)
                for g in range(CB):
                    gate(k, 0, g)
                take_x_tok(k, 1, 2)
                take_x_tok(k, 1, 3)
                take_xd(k, 1)
                softplus(k, 1)
                first_residual(k, 0)
                second_norm(k, 0)
                take_sums(k, 1)
                weigh(k, 1)
                weigh_b(k, 1)
                advance_state(k, 1)
                assert at[1] == FIRST_HALF_STEPS, at[1]

            def second_half(k, last=False):
                at[:] = [k, FIRST_HALF_STEPS]
                low_parts(k, "ln2T", 0)
                weigh_diagonal(k, 1)
                low_hidden(k, 0, 0, 1)
                assemble(k, 1)
                low_hidden(k, 0, 2, 3)
                for g in range(CB):
                    gate(k, 1, g)
                low_hidden(k, 0, 4, 5)
                first_residual(k, 1)
                low_hidden(k, 0, 6)
                second_norm(k, 1)
                low_hidden(k, 0, 7)
                low_parts(k, "ln2T", 1)
                final(k, 0)
                low_hidden(k, 1, 0, 1, 2)
                if not last:
                    first_norm(k, 0, k * 16 + 16)
                low_hidden(k, 1, 3, 4)
                if not last:
                    first_norm(k, 1, k * 16 + 16)
                low_hidden(k, 1, 5, 6, 7)
                if not last:
                    low_parts(k + 1, "ln1T", 0)
                final(k, 1)
                assert last or at[1] == VECTOR_STEPS, at[1]

            low_parts(1, "ln1T", 0)
            first_half(1)
            with dve.Fori(1, TILES) as k:
                second_half(k)
                first_half(k + 1)
            second_half(TILES, last=True)


_INS = ["L0_attn_x", "L0_attn_in_proj_w", "L0_attn_conv_w", "L0_attn_conv_b", "L0_attn_x_proj_w", "L0_attn_A_log",
        "L0_attn_D", "L0_attn_out_proj_w", "L0_ffn_W_exp", "L0_ffn_b_exp", "L0_ffn_up_weights", "L0_ffn_up_bias",
        "L0_ffn_down_weights", "L0_ffn_W_con", "L0_ffn_b_con", "L0_ffn_down_bias"]
_OUT = ((BATCH, LENGTH, DM), "float32")


def kernel(**inputs):
    import numpy as _np
    import concourse.bacc as _bacc
    from concourse import mybir as _mybir
    from concourse.bass_utils import run_bass_kernel_spmd as _run

    nc = _bacc.Bacc("TRN2", target_bir_lowering=False, num_devices=1)
    arrays, args = {}, []
    for name in _INS:
        a = _np.ascontiguousarray(inputs[name])
        arrays[f"in_{name}_dram"] = a
        args.append(nc.dram_tensor(f"in_{name}_dram", a.shape, _mybir.dt.from_np(a.dtype), kind="ExternalInput").ap())
    shape, dtype = _OUT
    args.append(nc.dram_tensor("out_dram", shape, _mybir.dt.from_np(_np.dtype(dtype)), kind="ExternalOutput").ap())
    bass_preln_ssm_butterfly_ffn(nc, *args)
    r = _run(nc, [arrays], core_ids=[0])
    return r.results[0]["out_dram"]
```

```python
from contextlib import ExitStack

import concourse.bass as bass
from concourse import mybir

F32 = mybir.dt.float32
F32R = mybir.dt.float32r
PARTS = ("high", "low")
PASSES = ((0, 0), (0, 1), (1, 0))
ALU = mybir.AluOpType
ACT = mybir.ActivationFunctionType
AXIS_X = mybir.AxisListType.X

P = 128
BATCH = 2
LENGTH = 2048
DM = 256
DI = 512
NS = 16
TAPS = 4
HID = 1024
TILE = 512
TILES = LENGTH // TILE
GR = TILE // P
MB = DM // P
CB = DI // P
HB = HID // P
BL = 16
NB = P // BL
HALO = TAPS - 1
XD = 1 + 2 * NS
SLOT = 32
LOW = 7
HIGH = 3
EPS = 1e-5
ATANH = [1 / 11, 1 / 9, 1 / 7, 1 / 5, 1 / 3]

WIDE_ORDER = (
    [("in", e, 0) for e in range(8)] + [("xp", 0, 0)] + [("in", e, 1) for e in range(7)] + [("xp", 0, 1)]
    + [("y", g, 0) for g in range(CB)] + [("out", 0, 0), ("out", 1, 0), ("in", 7, 1)]
    + [("up", j, 0) for j in range(4)] + [("y", g, 1) for g in range(CB)]
    + [("up", 4, 0), ("out", 0, 1), ("out", 1, 1)] + [("up", j, 0) for j in range(5, HB)]
    + [("up", j, 1) for j in range(HB)]
)
SMALL_ORDER = (
    [("ln1T", m, b) for b in range(BATCH) for m in range(MB)]
    + [("xtok", c, 0) for c in range(GR)] + [(name, 0, 0) for name in ("xdtok", "sums", "gap", "bd")]
    + [("ct", 0, 0), ("cb", 0, 0), ("cb", 1, 0)] + [(name, 0, 0) for name in ("cbd", "moff", "u")]
    + [("xtok", c, 1) for c in range(GR)] + [(name, 0, 1) for name in ("xdtok", "sums", "gap", "bd")]
    + [("ln2T", m, 0) for m in range(MB)]
    + [("ct", 0, 1), ("cbd", 0, 1), ("u", 0, 1), ("cb", 0, 1), ("cb", 1, 1), ("moff", 0, 1)]
    + [("ln2T", m, 1) for m in range(MB)]
)
TAKES = {"ln1T": 2, "ln2T": 2}
RING = 3
HRING = 2
FIRST_HALF_STEPS, VECTOR_STEPS = 45, 54


class Signal:

    def __init__(self, handle, count):
        self.handle, self.count, self.total = handle, count, BATCH * count

    def value(self, k, b, n, ago=0):
        return k * self.total + (b - ago) * self.count + n


class Banks:

    def __init__(self, nc, ctx, name, tiles, order):
        self.tiles, self.order = tiles, order
        self.written = [ctx.enter_context(nc.semaphore(f"{name}{i}_written")) for i in range(len(tiles))]
        self.read = [ctx.enter_context(nc.semaphore(f"{name}{i}_read")) for i in range(len(tiles))]
        self.place, self.products, self.takes = {}, [0] * len(tiles), [0] * len(tiles)
        for n, use in enumerate(order):
            bank = n % len(tiles)
            before = self.takes[bank]
            self.products[bank] += 1
            self.takes[bank] += TAKES.get(use[0], 1)
            self.place[use] = (bank, self.products[bank], before, self.takes[bank])

    def bank(self, use):
        return self.place[use][0]

    def value(self, k, use, ago, of):
        name, i, b = use
        place = self.place[(name, i, (b - ago) % BATCH)]
        total = (self.products if of == "written" else self.takes)[place[0]]
        n = place[{"written": 1, "free": 2, "read": 3}[of]]
        return place[0], (k + (b - ago) // BATCH) * total + n


def bass_preln_ssm_butterfly_ffn(
    nc, x, in_proj_w, conv_w, conv_b, x_proj_w, A_log, D, out_proj_w,
    W_exp, b_exp, up_weights, up_bias, down_weights, W_con, b_con, down_bias, out,
):
    ctx = ExitStack()
    with ctx:
        def sb(name, shape, dt=F32):
            return ctx.enter_context(nc.sbuf_tensor(name, shape, dt))

        def sem(name):
            return ctx.enter_context(nc.semaphore(name))

        with ExitStack() as under:
            low_w, paths, (wexpT, mixed) = (
                [under.enter_context(nc.sbuf_tensor(f"{name}{i}", shape, F32)) for i in range(2)]
                for name, shape in (("low_w", [P, 2 * HID]), ("paths", [P, HID]), ("mixed", [P, HB, DM + 1])))
        w_up = [sb(f"w_up_{part}", [P, MB, HID], F32R) for part in PARTS]
        hid = [sb(f"hid_{part}", [P, HRING, TILE], F32R) for part in PARTS]
        w_down = [sb(f"w_down_{part}", [P, HB, DM + 1], F32R) for part in PARTS]

        w_in = [sb(f"w_in_{part}", [P, MB, 2 * DI], F32R) for part in PARTS]
        w_x = sb("w_x", [P, CB, XD])
        w_out = sb("w_out", [P, CB, DM])
        bias_up = sb("bias_up", [P, HB])
        bias_out = sb("bias_out", [P, DM])
        taps = sb("taps", [P, CB, TAPS])
        tap_bias = sb("tap_bias", [P, CB])
        skip = sb("skip", [P, CB])
        rates = sb("rates", [P, NS])

        ident = sb("ident", [P, P])
        after = sb("after", [P, P])
        upto = sb("upto", [P, P])
        in_block = sb("in_block", [P, P])
        block_upto = sb("block_upto", [P, P])
        row_in_block = sb("row_in_block", [P, BL])
        later_in_block = sb("later_in_block", [P, BL])
        before_block = sb("before_block", [P, NB])
        restart = sb("restart", [P, GR, BL])
        ones = sb("ones", [P, P])
        minus_half = sb("minus_half", [P, GR])
        rate_before = sb("rate_before", [P, NB, NS])

        x_in = [sb(f"x_in{b}", [P, GR, DM]) for b in range(BATCH)]
        xn1 = [sb(f"xn1_{b}", [P, GR, DM]) for b in range(BATCH)]
        xnT = [sb(f"xnT_{part}", [P, MB, TILE], F32R) for part in PARTS]
        xi = sb("xi", [P, CB, HALO + TILE])
        halo = [sb(f"halo{b}", [P, CB, HALO]) for b in range(BATCH)]
        xc = [sb(f"xc{b}", [P, CB, TILE]) for b in range(BATCH)]
        z = [sb(f"z{b}", [P, CB, TILE]) for b in range(BATCH)]
        x_tok = sb("x_tok", [P, GR, DI])
        state = [sb(f"state{b}", [P, DI]) for b in range(BATCH)]
        state_end = [sb(f"state_end{b}", [NS, DI]) for b in range(BATCH)]
        xdT = sb("xdT", [P, TILE])
        xd = sb("xd", [P, GR, XD])
        soft = sb("soft", [P, 10, GR])
        delta = sb("delta", [P, GR])
        dB = sb("dB", [P, GR, NS])
        dA = sb("dA", [P, GR, SLOT])
        d_place = sb("d_place", [P, GR, BL])
        gap_w = sb("gap_w", [P, GR, NB, NS])
        bd_tok = sb("bd_tok", [P, GR, NB, NS])
        c_place = sb("c_place", [P, GR, NS, BL])
        diag = sb("diag", [P, GR, NS, BL])
        sums_A = sb("sums_A", [P, 3 * GR, NS])
        decays = sb("decays", [P, 3, GR, NS])
        group_sum = sb("group_sum", [P, 1])
        group_decay = sb("group_decay", [P, 1])
        d_block = sb("d_block", [P, GR, BL])
        gaps = sb("gaps", [P, GR, BL])
        diag_sum = sb("diag_sum", [P, GR, BL])
        c_start = sb("c_start", [P, GR, P + SLOT])
        c_block = sb("c_block", [P, GR, NS])
        cbd_tok = sb("cbd_tok", [P, GR, NB, NS])
        b_end = sb("b_end", [P, GR, NS])
        b_hat = sb("b_hat", [P, TILE])
        c_hat = sb("c_hat", [P, TILE])
        c_startT = sb("c_startT", [P, TILE])
        m_mat = sb("m_mat", [P, TILE])
        yg = sb("yg", [P, CB, TILE])
        x1 = sb("x1", [P, GR, DM])
        x1b_xn2 = sb("x1b_xn2", [P, 2, GR, DM])
        x1b, xn2 = x1b_xn2[:, 0, :, :], x1b_xn2[:, 1, :, :]
        hid_f32 = sb("hid_f32", [P, HRING, TILE])
        stats = sb("stats", [P, GR, 6])
        carrier = sb("carrier", [P, 1])
        exp_of_one = sb("exp_of_one", [P, 1])
        mean_var = sb("mean_var", [P, GR, 2])
        var_eps = sb("var_eps", [P, 2 * BATCH, GR])
        rstd = sb("rstd", [P, 2 * BATCH, GR])

        wide = [ctx.enter_context(nc.psum_tensor(f"wide{i}", [P, TILE], F32)) for i in range(RING)]
        small = [ctx.enter_context(nc.psum_tensor(f"small{i}", [P, TILE], F32)) for i in range(RING)]
        acc = ctx.enter_context(nc.psum_tensor("acc", [P, GR, DM], F32))
        WIDE = Banks(nc, ctx, "wide", wide, WIDE_ORDER)
        SMALL = Banks(nc, ctx, "small", small, SMALL_ORDER)
        ACC = Banks(nc, ctx, "acc", [acc], [("down", 0, 0), ("down", 0, 1)])
        where = {name: banks for banks in (WIDE, SMALL, ACC) for name, _, _ in banks.order}

        def tile_of(name, i, b):
            return where[name].tiles[where[name].bank((name, i, b))]

        def written(eng, k, name, i, b, ago=0):
            bank, value = where[name].value(k, (name, i, b), ago, "written")
            eng.wait_ge(where[name].written[bank], value)

        def read(eng, k, name, i, b, ago=0, takes=None):
            bank, value = where[name].value(k, (name, i, b), ago, "read" if takes is None else "free")
            eng.wait_ge(where[name].read[bank], value + (takes or 0))

        def free(eng, k, name, i, b):
            bank, value = where[name].value(k, (name, i, b), 0, "free")
            eng.wait_ge(where[name].read[bank], value)

        def mark_written(ins, name, i, b):
            ins.then_inc(where[name].written[where[name].bank((name, i, b))], 1)

        def mark_read(ins, name, i, b):
            ins.then_inc(where[name].read[where[name].bank((name, i, b))], 1)

        x_loaded = [sem(f"x_loaded{b}") for b in range(BATCH)]
        out_stored = Signal(sem("out_stored"), 16)
        var1 = Signal(sem("var1"), 1)
        rstd1 = Signal(sem("rstd1"), 1)
        norm1 = Signal(sem("norm1"), GR)
        var2 = Signal(sem("var2"), 1)
        rstd2 = Signal(sem("rstd2"), 1)
        norm2 = Signal(sem("norm2"), GR)
        halo_moved = Signal(sem("halo_moved"), 1)
        halo_saved = Signal(sem("halo_saved"), 1)
        xi_copied = Signal(sem("xi_copied"), CB)
        convolved = Signal(sem("convolved"), CB)
        xc_ready = Signal(sem("xc_ready"), CB)
        z_ready = Signal(sem("z_ready"), 1)
        abs_ready = Signal(sem("abs_ready"), 1)
        exp_ready = Signal(sem("exp_ready"), 1)
        dB_ready = Signal(sem("dB_ready"), 1)
        delta_ready = Signal(sem("delta_ready"), 1)
        gap_w_ready = Signal(sem("gap_w_ready"), 1)
        c_placed = Signal(sem("c_placed"), 1)
        bd_ready = Signal(sem("bd_ready"), 1)
        sums_ready = Signal(sem("sums_ready"), 1)
        decays_ready = Signal(sem("decays_ready"), 1)
        group_decay_ready = Signal(sem("group_decay_ready"), 1)
        gaps_ready = Signal(sem("gaps_ready"), 1)
        diag_gaps = Signal(sem("diag_gaps"), 1)
        diag_exp = Signal(sem("diag_exp"), 1)
        diag_times_b = Signal(sem("diag_times_b"), 1)
        diag_summed = Signal(sem("diag_summed"), 1)
        c_start_ready = Signal(sem("c_start_ready"), 1)
        c_block_ready = Signal(sem("c_block_ready"), 1)
        cbd_ready = Signal(sem("cbd_ready"), 1)
        b_end_ready = Signal(sem("b_end_ready"), 1)
        first_state = Signal(sem("first_state"), 1)
        states_ready = Signal(sem("states_ready"), 1)
        gated = Signal(sem("gated"), CB)
        x1b_ready = Signal(sem("x1b_ready"), 1)
        hid_high = Signal(sem("hid_high"), HB)
        hid_ready = Signal(sem("hid_ready"), HB)
        down_steps = Signal(sem("down_steps"), HB - 1)
        vector_steps = Signal(sem("vector_steps"), VECTOR_STEPS // BATCH)

        by_vector = [var1, norm1, var2, norm2, convolved, abs_ready, dB_ready, delta_ready, sums_ready,
                     gaps_ready, diag_summed, c_start_ready, c_block_ready, b_end_ready, states_ready, gated, hid_ready]
        by_scalar = [halo_moved, xi_copied, xc_ready, z_ready, exp_ready, decays_ready, group_decay_ready, diag_exp,
                     first_state, halo_saved, hid_high]
        by_pool = [rstd1, rstd2, c_placed, gap_w_ready, bd_ready, diag_gaps, cbd_ready, diag_times_b, x1b_ready]

        def start(eng, signals):
            for s in signals:
                eng.sem_inc(s.handle, s.total)

        in_loaded = [sem(f"in_loaded{h}") for h in range(2)]
        w_loaded = {name: sem(f"{name}_loaded") for name in ("x_proj", "out_proj", "exp", "con")}
        conv_loaded = sem("conv_loaded")
        s_loaded = sem("s_loaded")
        low_loaded = [sem(f"low_loaded{i}") for i in range(2)]
        CONV_LOADS, SMALL_LOADS = 4, 2 * HIGH + 4
        masks_made = sem("masks_made")
        mask_steps = sem("mask_steps")
        zeroed = sem("zeroed")
        perm_made = sem("perm_made")
        rates_exp = sem("rates_exp")
        made = sem("made")
        taken = [sem(f"taken{i}") for i in range(2)]
        highs = sem("highs")
        path_steps = sem("path_steps")
        paths_ready = sem("paths_ready")
        scaled = [sem(f"scaled{i}") for i in range(2)]
        mixed_up = [sem(f"mixed_up{i}") for i in range(2)]
        vector_setup = sem("vector_setup")

        W1 = DM + 1
        flat = "p a b -> p (a b)"
        raw_in = xc[0][:, :, :].rearrange(flat).rearrange("p (e d) -> p e d", d=DM)
        raw_exp = xc[1][:, :, :].rearrange(flat).rearrange("p (m h) -> p m h", h=HID)
        raw_out = sb("raw_out", [P, MB, DI])
        raw_x = b_hat[0:XD, :]
        perm = hid_f32[:, :, :].rearrange(flat)[:, 0:LOW * P].rearrange("p (s q) -> p s q", q=P)
        pathT = hid_f32[:, :, :].rearrange(flat).rearrange("p (g j) -> p g j", j=P)
        spread = [x1[:, :, :].rearrange(flat), xn1[0][:, :, :].rearrange(flat)]
        raw_con = low_w[1][:, :].rearrange("p (g d) -> p g d", d=DM)
        con_mixed = x1b_xn2[:, :, :, :].rearrange("p a b d -> p (a b) d")
        high_w = [sb(f"high_w{i}", [P, HIGH, HB // 2, 4]) for i in range(2)]
        bias_raw = sb("bias_raw", [P, 2, DM])
        up_bias_sb = sb("up_bias_sb", [P, HB])
        UP, DOWN = 0, 1

        low_at = [0]
        for s in range(LOW):
            low_at.append(low_at[-1] + HID // 2**s)

        steps = [
            [("w_in", m, 0) for m in range(MB)],
            [("w_in", m, 1) for m in range(MB)],
            [("w_x", 0, 0), ("low", UP, 0)],
            [("low", UP, 1), ("low", UP, 2)],
            [("low", UP, 3), ("w_out", 0, 0)],
            [("wexpT", 0, 0), ("wexpT", 1, 0)],
            [("wexpT", 2, 0), ("wexpT", 3, 0)],
            [("low", DOWN, 0), ("low", DOWN, 1)],
            [("low", DOWN, 2), ("low", DOWN, 3)],
            [("pathT", 0, 0), ("pathT", 1, 0)],
            [("up_low", 0, 0), ("up_low", 1, 0)],
            [("up_low", 2, 0), ("up_low", 3, 0)],
            [("up_low", 4, 0), ("up_low", 5, 0)],
            [("up_low", 6, 0), ("up_low", 7, 0)],
            [("w_out", 1, 0)],
            [("w_up", m, h) for m in range(MB) for h in range(2)],
            [("w_down", q, 0) for q in range(4)],
        ]
        products = [product for step in steps for product in step]
        number = {product: n for n, product in enumerate(products)}
        acc_banks = [acc[:, 2 * i:2 * i + 2, :].rearrange(flat) for i in range(2)]

        def bank_for(product):
            return acc_banks[number[product] % 2]

        def wait_taken(eng, product):
            n = number[product]
            eng.wait_ge(taken[n % 2], n // 2 + 1)

        def take_low(i, q):
            if q < 2:
                return paths[i][:, 512 * q:512 * (q + 1)]
            return spread[i][:, 0:512] if q == 2 else spread[i][:, 512:512 + low_at[LOW] - low_at[2]]

        def mixing(i, stage):
            span, transposed = 2**stage, i == DOWN
            for g in range(HB):
                o = g // span % 2
                low = g - o * span
                q = (low // (2 * span)) * span + low % span
                column = lambda i_: high_w[i][:, stage, q, (2 * i_ + o if transposed else 2 * o + i_):][:, 0:1]
                yield g, low, low + span, column(0), column(1)

        def scaled_by(i, n, g):
            return n * HB + g + 1

        def wait_mixed(eng, i, n, *blocks):
            eng.wait_ge(mixed_up[i], n * HB + max(blocks) + 1)

        MIXES = {UP: [(0, mixed, wexpT), (1, wexpT, mixed), (2, mixed, wexpT)],
                 DOWN: [(2, raw_con, con_mixed), (1, con_mixed, raw_con), (0, raw_con, con_mixed)]}

        def load_low(eng, i, weights):
            for s in range(LOW):
                half = 2**s
                for o in range(2):
                    eng.dma_start(
                        low_w[i][o * half:(o + 1) * half, low_at[s]:low_at[s + 1]].rearrange("l (c i) -> l c i", i=2),
                        weights[s, :, o, :].rearrange("(c l) i -> l c i", l=half)).then_inc(low_loaded[i], 16)

        def needed_for_first_term(i, n, g, low):
            return low, g, g ^ 2**MIXES[i][n - 1][0]

        block = ctx.enter_context(nc.Block())

        @block.sync
        def _(sp):
            def load_first(b):
                sp.dma_start(x_in[b][:, :, :], x[b, 0:TILE, :].rearrange("(c p) d -> p c d", p=P)).then_inc(x_loaded[b], 16)

            load_first(0)
            sp.dma_start(taps[:, :, :], conv_w.rearrange("(g p) o k -> p g (o k)", p=P)).then_inc(conv_loaded, 16)
            sp.dma_start(tap_bias[:, :], conv_b.rearrange("(g p) -> p g", p=P), allow_slow_non_contiguous=True).then_inc(conv_loaded, 16)
            sp.dma_start(skip[:, :], D.rearrange("(g p) -> p g", p=P), allow_slow_non_contiguous=True).then_inc(conv_loaded, 16)
            sp.dma_start(rates[:, :], A_log.partition_broadcast(P)).then_inc(conv_loaded, 16)
            load_first(1)
            sp.dma_start(raw_x, x_proj_w).then_inc(w_loaded["x_proj"], 16)
            load_low(sp, UP, up_weights)
            sp.dma_start(raw_exp, W_exp.rearrange("(m p) h -> p m h", p=P)).then_inc(w_loaded["exp"], 16)
            sp.dma_start(raw_out[:, :, :], out_proj_w.rearrange("(o p) d -> p o d", p=P)).then_inc(w_loaded["out_proj"], 16)
            sp.dma_start(up_bias_sb[:, :], up_bias.rearrange("(g p) -> p g", p=P), allow_slow_non_contiguous=True).then_inc(s_loaded, 16)
            sp.dma_start(wexpT[:, :, DM], b_exp.rearrange("(g p) -> p g", p=P), allow_slow_non_contiguous=True).then_inc(s_loaded, 16)
            for n, row in enumerate((b_con, down_bias)):
                sp.dma_start(bias_raw[:, n, :], row.partition_broadcast(P)).then_inc(s_loaded, 16)
            for i, weights in enumerate((up_weights, down_weights)):
                for s in range(HIGH):
                    sp.dma_start(high_w[i][:, s, :, :],
                                 weights[LOW + s].rearrange("(q p) o i -> p q (o i)", p=P)).then_inc(s_loaded, 16)
            load_low(sp, DOWN, down_weights)
            sp.wait_ge(made, number[("low", DOWN, 3)] + 1)
            sp.dma_start(raw_con, W_con.rearrange("(g p) d -> p g d", p=P)).then_inc(w_loaded["con"], 16)
            start(sp, [out_stored])

            def load(k, b):
                read(sp, k, "out", 1, b)
                sp.dma_start(x_in[b][:, :, :], x[b, bass.ds(k * TILE, TILE), :].rearrange("(c p) d -> p c d", p=P))\
                    .then_inc(x_loaded[b], 16)

            def store(k, b):
                read(sp, k, "down", 0, b)
                sp.dma_start(out[b, bass.ds((k - 1) * TILE, TILE), :].rearrange("(c p) d -> p c d", p=P),
                             x1b).then_inc(out_stored.handle, 16)

            with sp.Fori(1, TILES) as k:
                for b in range(BATCH):
                    load(k, b)
                for b in range(BATCH):
                    store(k, b)
            for b in range(BATCH):
                store(TILES, b)
            sp.wait_ge(out_stored.handle, out_stored.value(TILES, 1, 16))

        @block.gpsimd
        def _(pool):
            start(pool, by_pool)
            count = [0]

            def select(out_ap, in_ap, op, base, cm, pattern):
                pool.affine_select(out=out_ap, in_=in_ap, compare_op=op, fill=0.0, base=base, pattern=pattern,
                                   channel_multiplier=cm).then_inc(mask_steps, 1)
                count[0] += 1
                pool.wait_ge(mask_steps, count[0])

            pool.memset(ident[:, :], 0.0).then_inc(mask_steps, 1)
            pool.memset(minus_half[:, :], -0.5).then_inc(mask_steps, 1)
            count[0] = 2
            pool.wait_ge(mask_steps, count[0])
            pool.affine_select(out=ident[:, :], in_=ident[:, :], compare_op=ALU.not_equal, fill=1.0, base=0,
                               pattern=[[-1, P]], channel_multiplier=1).then_inc(masks_made, 1)
            pool.memset(halo[0][:, :, :], 0.0)
            pool.memset(halo[1][:, :, :], 0.0)
            pool.memset(xdT[:, :], 0.0).then_inc(zeroed, 1)

            def rstd_of(k, b, slot, var, ready):
                pool.wait_ge(var.handle, var.value(k, b, 1))
                pool.tensor_tensor(rstd[:, slot, :], var_eps[:, slot, :], minus_half[:, :], ALU.pow)\
                    .then_inc(ready.handle, 1)

            rstd_of(1, 0, 0, var1, rstd1)
            pool.wait_ge(masks_made, 1)
            for s in range(LOW):
                rows = 2**(s + 1)
                ins = pool.tensor_copy(perm[0:rows, s, :].rearrange("q (r w) -> q r w", w=rows),
                                       ident[0:rows, 0:rows].unsqueeze(1).to_broadcast([rows, P // rows, rows]))
            ins.then_inc(perm_made, 1)
            pool.memset(ones[:, :], 1.0).then_inc(mask_steps, 1)
            pool.memset(restart[:, :, :], 1.0).then_inc(mask_steps, 1)
            count[0] += 2
            pool.wait_ge(mask_steps, count[0])
            pool.memset(restart[:, :, 0], 0.0)
            select(after[:, :], ones[:, :], ALU.is_gt, 0, 1, [[-1, P]])
            select(upto[:, :], ones[:, :], ALU.is_ge, 0, -1, [[1, P]])
            in_blocks = "p (j u) -> p j u"
            blk, blk_upto = (m[:, :].rearrange(in_blocks, u=BL) for m in (in_block, block_upto))
            select(blk, ones[:, :].rearrange(in_blocks, u=BL), ALU.is_ge, 0, 1, [[-BL, NB], [0, BL]])
            select(blk, blk, ALU.is_ge, BL - 1, -1, [[BL, NB], [0, BL]])
            select(blk_upto, blk, ALU.is_ge, 0, -1, [[BL, NB], [1, BL]])
            pool.affine_select(out=before_block[:, :], in_=ones[:, 0:NB], compare_op=ALU.is_gt, fill=0.0, base=0,
                               pattern=[[BL, NB]], channel_multiplier=-1).then_inc(masks_made, 1)
            rstd_of(1, 1, 1, var1, rstd1)
            pool.memset(dA[:, :, :], 0.0)
            pool.memset(c_start[:, :, :], 0.0)
            for b in range(BATCH):
                pool.memset(state[b][:, :], 0.0)
                ins = pool.memset(state_end[b][:, :], 0.0)
            ins.then_inc(zeroed, 1)

            steps_done = [0]

            def multiply_paths(i, stages):
                for s in stages:
                    if s == 1:
                        for q in range(4):
                            wait_taken(pool, ("low", i, q))
                    cols = HID // 2**s
                    at = 0 if s == 1 else 512 + low_at[s] - low_at[2]
                    wide_as = paths[i][:, :].rearrange("p (m w) -> p m w", w=2**s)
                    ins = pool.tensor_tensor(wide_as, wide_as,
                                             spread[i][:, at:at + cols].unsqueeze(2).to_broadcast([P, cols, 2**s]), ALU.mult)
                    if s < LOW - 1:
                        steps_done[0] += 1
                        ins.then_inc(path_steps, 1)
                        pool.wait_ge(path_steps, steps_done[0])
                    else:
                        ins.then_inc(paths_ready, 1)

            def scale_down_blocks(n):
                if n == 0:
                    pool.wait_ge(w_loaded["con"], 16)
                    pool.wait_ge(s_loaded, 16 * SMALL_LOADS)
                stage, source, target = MIXES[DOWN][n]
                for g, low, _, weight, _ in mixing(DOWN, stage):
                    if n:
                        wait_mixed(pool, DOWN, n - 1, *needed_for_first_term(DOWN, n, g, low))
                    pool.tensor_tensor(target[:, g, :], source[:, low, :], weight.to_broadcast([P, DM]), ALU.mult)\
                        .then_inc(scaled[DOWN], 1)

            def place_c(k, b):
                read(pool, k, "xdtok", 0, b)
                written(pool, k, "cb", 1, b, ago=1)
                pool.tensor_tensor(c_place[:, :, :, :],
                                   xd[:, :, 1 + NS:XD].unsqueeze(3).to_broadcast([P, GR, NS, BL]),
                                   row_in_block[:, :].unsqueeze(1).unsqueeze(1).to_broadcast([P, GR, NS, BL]),
                                   ALU.mult).then_inc(c_placed.handle, 1)

            def mask_b(k, b):
                pool.wait_ge(dB_ready.handle, dB_ready.value(k, b, 1))
                written(pool, k, "bd", 0, b, ago=1)
                pool.tensor_tensor(bd_tok[:, :, :, :],
                                   dB[:, :, :].unsqueeze(2).to_broadcast([P, GR, NB, NS]),
                                   before_block[:, :].unsqueeze(1).unsqueeze(3).to_broadcast([P, GR, NB, NS]),
                                   ALU.mult).then_inc(bd_ready.handle, 1)

            def diagonal_gaps(k, b):
                pool.wait_ge(gaps_ready.handle, gaps_ready.value(k, b, 1))
                pool.wait_ge(diag_summed.handle, diag_summed.value(k, b, 1, ago=1))
                pool.tensor_tensor(diag[:, :, :, :],
                                   gaps[:, :, :].unsqueeze(2).to_broadcast([P, GR, NS, BL]),
                                   rates[:, :].unsqueeze(1).unsqueeze(3).to_broadcast([P, GR, NS, BL]),
                                   ALU.mult).then_inc(diag_gaps.handle, 1)

            def weigh_gaps(k, b):
                pool.wait_ge(dB_ready.handle, dB_ready.value(k, b, 1))
                written(pool, k, "gap", 0, b, ago=1)
                pool.tensor_tensor(gap_w[:, :, :, :].rearrange("p c j n -> p c (j n)"),
                                   rate_before[:, :, :].rearrange(flat).unsqueeze(1).to_broadcast([P, GR, P]),
                                   delta[:, :].unsqueeze(2).to_broadcast([P, GR, P]), ALU.mult)\
                    .then_inc(gap_w_ready.handle, 1)

            def place_c_block(k, b):
                pool.wait_ge(c_block_ready.handle, c_block_ready.value(k, b, 1))
                written(pool, k, "cbd", 0, b, ago=1)
                pool.tensor_tensor(cbd_tok[:, :, :, :], c_block[:, :, :].unsqueeze(2).to_broadcast([P, GR, NB, NS]),
                                   in_block[:, :].rearrange("p (j u) -> p j u", u=BL)[:, :, 0:1].unsqueeze(1)
                                   .to_broadcast([P, GR, NB, NS]), ALU.mult).then_inc(cbd_ready.handle, 1)

            def diagonal_times_b(k, b):
                pool.wait_ge(diag_exp.handle, diag_exp.value(k, b, 1))
                pool.tensor_tensor(diag[:, :, :, :], diag[:, :, :, :],
                                   dB[:, :, :].unsqueeze(3).to_broadcast([P, GR, NS, BL]), ALU.mult)\
                    .then_inc(diag_times_b.handle, 1)

            def residual_with_bias(k, b):
                read(pool, k, "out", 1, b)
                pool.wait_ge(out_stored.handle, out_stored.value(k, b, 16, ago=1))
                pool.tensor_tensor(x1b, x1[:, :, :], bias_out[:, :].unsqueeze(1).to_broadcast([P, GR, DM]),
                                   ALU.add).then_inc(x1b_ready.handle, 1)

            def first_half(k, first=False):
                place_c(k, 0)
                weigh_gaps(k, 0)
                mask_b(k, 0)
                diagonal_gaps(k, 0)
                place_c_block(k, 0)
                diagonal_times_b(k, 0)
                if first:
                    multiply_paths(DOWN, range(1, LOW))
                    for n in range(HIGH):
                        scale_down_blocks(n)
                place_c(k, 1)
                weigh_gaps(k, 1)
                mask_b(k, 1)
                rstd_of(k, 0, BATCH, var2, rstd2)
                diagonal_gaps(k, 1)
                place_c_block(k, 1)

            def second_half(k, last=False):
                residual_with_bias(k, 0)
                diagonal_times_b(k, 1)
                rstd_of(k, 1, BATCH + 1, var2, rstd2)
                residual_with_bias(k, 1)
                if not last:
                    for b in range(BATCH):
                        rstd_of(k + 1, b, b, var1, rstd1)

            multiply_paths(UP, range(1, LOW))
            first_half(1, first=True)
            pool.wait_ge(made, len(products))
            with pool.Fori(1, TILES) as k:
                second_half(k)
                first_half(k + 1)
            second_half(TILES, last=True)

        @block.tensor
        def _(pe):
            def make(product):
                name, i, h = product
                n = number[product]
                bank = bank_for(product)
                if n >= 2:
                    pe.wait_ge(taken[n % 2], n // 2)
                if name == "w_in":
                    pe.wait_ge(in_loaded[h], 16)
                    for q in range(4):
                        last = pe.transpose(bank[:, q * P:(q + 1) * P], raw_in[:, 4 * h + q, i * P:(i + 1) * P], ident[:, :])
                elif name == "w_x":
                    pe.wait_ge(w_loaded["x_proj"], 16)
                    for g in range(CB):
                        last = pe.transpose(bank[:, g * XD:(g + 1) * XD], raw_x[:, g * P:(g + 1) * P], ident[0:XD, 0:XD])
                elif name == "w_out":
                    pe.wait_ge(w_loaded["out_proj"], 16)
                    for q in range(2):
                        for o in range(MB):
                            at = (q * MB + o) * P
                            last = pe.transpose(bank[:, at:at + P], raw_out[:, o, (2 * i + q) * P:(2 * i + q + 1) * P], ident[:, :])
                elif name == "wexpT":
                    pe.wait_ge(w_loaded["exp"], 16)
                    for g in range(2):
                        for m in range(MB):
                            at = (g * MB + m) * P
                            last = pe.transpose(bank[:, at:at + P], raw_exp[:, m, (2 * i + g) * P:(2 * i + g + 1) * P], ident[:, :])
                elif name == "low":
                    pe.wait_ge(perm_made, 1)
                    pe.wait_ge(low_loaded[i], 16 * 2 * LOW)
                    if h < 2:
                        parts = [(0, 512 * h, 512 * (h + 1), 0)]
                    elif h == 2:
                        parts = [(1, low_at[1], low_at[2], 0)]
                    else:
                        parts = [(s, low_at[s], low_at[s + 1], low_at[s] - low_at[2]) for s in range(2, LOW)]
                    for s, lo, hi, at in parts:
                        rows = 2**(s + 1)
                        last = pe.matmul(bank[:, at:at + hi - lo], perm[0:rows, s, :], low_w[i][0:rows, lo:hi],
                                         start=True, stop=True)
                elif name == "pathT":
                    pe.wait_ge(paths_ready, 1)
                    for q in range(4):
                        g = 4 * i + q
                        last = pe.transpose(bank[:, q * P:(q + 1) * P], paths[UP][:, g * P:(g + 1) * P], ident[:, :])
                elif name == "up_low":
                    if i == 0:
                        pe.wait_ge(s_loaded, 16 * SMALL_LOADS)
                        wait_taken(pe, ("pathT", 0, 0))
                        wait_taken(pe, ("pathT", 1, 0))
                    last = pe.matmul(bank[:, 0:W1], pathT[:, i, :], wexpT[:, i, :], start=True, stop=True)
                elif name == "w_up":
                    wait_mixed(pe, UP, HIGH - 1, HB - 1)
                    for q in range(4):
                        last = pe.transpose(bank[:, q * P:(q + 1) * P], wexpT[:, 4 * h + q, i * P:(i + 1) * P], ident[:, :])
                else:
                    pe.wait_ge(paths_ready, 2)
                    wait_mixed(pe, DOWN, HIGH - 1, HB - 1)
                    for g in range(2):
                        last = pe.matmul(bank[:, g * DM:(g + 1) * DM], paths[DOWN][:, (2 * i + g) * P:(2 * i + g + 1) * P],
                                         con_mixed[:, 2 * i + g, :], start=True, stop=True)
                last.then_inc(made, 1)

            def prepare(step):
                for product in steps[step]:
                    make(product)
                if step == 3:
                    for m in range(MB):
                        wait_taken(pe, ("w_in", m, 1))
                elif step == 4:
                    wait_taken(pe, ("w_x", 0, 0))
                elif step == 8:
                    pe.wait_ge(masks_made, 2)
                    pe.wait_ge(zeroed, 2)
                elif step == 14:
                    for h in range(2):
                        wait_taken(pe, ("w_out", h, 0))
                elif step == 16:
                    for q in range(4):
                        wait_taken(pe, ("w_down", q, 0))

            for banks in (WIDE, SMALL, ACC):
                for handle, total in zip(banks.written, banks.products):
                    pe.sem_inc(handle, total)
            start(pe, [down_steps])
            pe.wait_ge(masks_made, 1)

            def transposes(k, name, b, source, ready):
                for m in range(MB):
                    bank = tile_of(name, m, b)
                    free(pe, k, name, m, b)
                    for c in range(GR):
                        if m == 0:
                            pe.wait_ge(ready.handle, ready.value(k, b, c + 1))
                        last = pe.transpose(bank[:, c * P:(c + 1) * P], source[:, c, m * P:(m + 1) * P], ident[:, :])
                    mark_written(last, name, m, b)

            def in_projection(k, b, e):
                bank = tile_of("in", e, b)
                free(pe, k, "in", e, b)
                if e == 0:
                    for m in range(MB):
                        read(pe, k, "ln1T", m, b)
                for n, (m, w, x) in enumerate((m, w, x) for m in range(MB) for w, x in PASSES):
                    last = pe.matmul(bank[:, :], w_in[w][:, m, e * P:(e + 1) * P], xnT[x][:, m, :],
                                     start=n == 0, stop=n == MB * len(PASSES) - 1)
                mark_written(last, "in", e, b)

            def x_projection(k, b):
                bank = tile_of("xp", 0, b)
                free(pe, k, "xp", 0, b)
                for g in range(CB):
                    pe.wait_ge(xc_ready.handle, xc_ready.value(k, b, g + 1))
                    last = pe.matmul(bank[0:XD, :], w_x[:, g, :], xc[b][:, g, :], start=g == 0, stop=g == CB - 1)
                mark_written(last, "xp", 0, b)

            def tokens_first(k, b):
                for c in range(GR):
                    bank = tile_of("xtok", c, b)
                    free(pe, k, "xtok", c, b)
                    for g in range(CB):
                        last = pe.transpose(bank[:, g * P:(g + 1) * P], xc[b][:, g, c * P:(c + 1) * P], ident[:, :])
                    mark_written(last, "xtok", c, b)

            def xd_tokens_first(k, b):
                bank = tile_of("xdtok", 0, b)
                free(pe, k, "xdtok", 0, b)
                read(pe, k, "xp", 0, b)
                for c in range(GR):
                    last = pe.transpose(bank[:, c * P:(c + 1) * P], xdT[:, c * P:(c + 1) * P], ident[:, :])
                mark_written(last, "xdtok", 0, b)

            def step_sums(k, b):
                bank = tile_of("sums", 0, b)
                free(pe, k, "sums", 0, b)
                pe.wait_ge(delta_ready.handle, delta_ready.value(k, b, 1))
                for n, mask in enumerate((upto, block_upto, after)):
                    pe.matmul(bank[:, n * GR:(n + 1) * GR], mask[:, :], delta[:, :], start=True, stop=True)
                pe.matmul(bank[:, 12:13], dA[:, :, :].rearrange(flat), ones[:, 0:1], start=True, stop=True)
                mark_written(pe.matmul(bank[:, 16:16 + GR * BL], in_block[:, :], d_place[:, :, :].rearrange(flat),
                                       start=True, stop=True), "sums", 0, b)

            def gap_products(k, b):
                bank = tile_of("gap", 0, b)
                free(pe, k, "gap", 0, b)
                pe.wait_ge(gap_w_ready.handle, gap_w_ready.value(k, b, 1))
                for c in range(GR):
                    last = pe.matmul(bank[:, c * P:(c + 1) * P], gap_w[:, c, :, :].rearrange(flat), after[:, :],
                                     start=True, stop=True)
                mark_written(last, "gap", 0, b)

            def transpose_groups(k, name, b, source, ready):
                bank = tile_of(name, 0, b)
                free(pe, k, name, 0, b)
                pe.wait_ge(ready.handle, ready.value(k, b, 1))
                for c in range(GR):
                    last = pe.transpose(bank[:, c * P:(c + 1) * P], source(c), ident[:, :])
                mark_written(last, name, 0, b)

            def state_inputs(k, b):
                bank = tile_of("u", 0, b)
                free(pe, k, "u", 0, b)
                pe.wait_ge(b_end_ready.handle, b_end_ready.value(k, b, 1))
                for c in range(GR):
                    read(pe, k, "xtok", c, b)
                for c in range(GR):
                    last = pe.matmul(bank[SLOT * c:SLOT * c + NS, :], b_end[:, c, :], x_tok[:, c, :],
                                     start=True, stop=True)
                mark_written(last, "u", 0, b)

            def spread_c(k, b):
                for h in range(2):
                    bank = tile_of("cb", h, b)
                    free(pe, k, "cb", h, b)
                    if h == 0:
                        pe.wait_ge(c_placed.handle, c_placed.value(k, b, 1))
                    mark_written(pe.matmul(bank[:, :], in_block[:, :],
                                           c_place[:, 2 * h:2 * h + 2, :, :].rearrange("p c n u -> p (c n u)"),
                                           start=True, stop=True), "cb", h, b)

            def off_diagonal(k, b):
                bank = tile_of("moff", 0, b)
                free(pe, k, "moff", 0, b)
                read(pe, k, "bd", 0, b)
                read(pe, k, "cbd", 0, b)
                for c in range(GR):
                    last = pe.matmul(bank[:, c * P:(c + 1) * P], b_hat[:, c * P:(c + 1) * P], c_hat[:, c * P:(c + 1) * P],
                                     start=True, stop=True)
                mark_written(last, "moff", 0, b)

            def ssm_output(k, b):
                for pair in ((0, 1), (2, 3)):
                    for g in pair:
                        bank = tile_of("y", g, b)
                        free(pe, k, "y", g, b)
                        if g == 0:
                            read(pe, k, "moff", 0, b)
                        for c in range(GR):
                            pe.matmul(bank[:, c * P:(c + 1) * P], x_tok[:, c, g * P:(g + 1) * P],
                                      m_mat[:, c * P:(c + 1) * P], start=c == 0, stop=False, skip_group_check=True)
                    for g in pair:
                        if g == 0:
                            read(pe, k, "ct", 0, b)
                            pe.wait_ge(first_state.handle, first_state.value(k, b, 1))
                            pe.wait_ge(states_ready.handle, states_ready.value(k, b, 1))
                        mark_written(pe.matmul(tile_of("y", g, b)[:, :], state[b][:, g * P:(g + 1) * P], c_startT[:, :],
                                               start=False, stop=True, skip_group_check=True), "y", g, b)

            def out_projection(k, b, h):
                bank = tile_of("out", h, b)
                free(pe, k, "out", h, b)
                if h == 0:
                    pe.wait_ge(gated.handle, gated.value(k, b, CB))
                for q in range(2):
                    c = 2 * h + q
                    for g in range(CB):
                        last = pe.matmul(bank[:, q * DM:(q + 1) * DM], yg[:, g, c * P:(c + 1) * P], w_out[:, g, :],
                                         start=g == 0, stop=g == CB - 1)
                mark_written(last, "out", h, b)

            def up(k, b, j):
                bank = tile_of("up", j, b)
                free(pe, k, "up", j, b)
                if j == 0:
                    for m in range(MB):
                        read(pe, k, "ln2T", m, b)
                for n, (m, w, x) in enumerate((m, w, x) for m in range(MB) for w, x in PASSES):
                    last = pe.matmul(bank[:, :], w_up[w][:, m, j * P:(j + 1) * P], xnT[x][:, m, :],
                                     start=n == 0, stop=n == MB * len(PASSES) - 1)
                mark_written(last, "up", j, b)

            def down(k, b, j):
                if j == 0:
                    free(pe, k, "down", 0, b)
                pe.wait_ge(hid_ready.handle, hid_ready.value(k, b, j + 1))
                for c in range(GR):
                    for n, (h, w) in enumerate(PASSES):
                        last = pe.matmul(acc[:, c, :], hid[h][:, j % HRING, c * P:(c + 1) * P], w_down[w][:, j, 0:DM],
                                         start=j == 0 and c % 2 == 0 and n == 0,
                                         stop=j == HB - 1 and n == len(PASSES) - 1, skip_group_check=True)
                if j == HB - 1:
                    mark_written(last, "down", 0, b)
                else:
                    last.then_inc(down_steps.handle, 1)

            def decayed_b(k, b):
                gap_products(k, b)
                transpose_groups(k, "bd", b, lambda c: bd_tok[:, c, :, :].rearrange(flat), bd_ready)

            def decayed_c_start(k, b):
                transpose_groups(k, "ct", b, lambda c: c_start[:, :, :].rearrange(flat)[:, c * P:(c + 1) * P], c_start_ready)

            def decayed_c_block(k, b):
                transpose_groups(k, "cbd", b, lambda c: cbd_tok[:, c, :, :].rearrange(flat), cbd_ready)

            def ffn(k, b, first, last):
                for j in range(first, last):
                    up(k, b, j)
                    if j >= HRING:
                        down(k, b, j - HRING)

            def first_half(k, beside=lambda step: None):
                for e in range(8):
                    in_projection(k, 0, e)
                    if e % 2:
                        beside(2 + e // 2)
                transposes(k, "ln1T", 1, xn1[1], norm1)
                x_projection(k, 0)
                tokens_first(k, 0)
                xd_tokens_first(k, 0)
                beside(6)
                in_projection(k, 1, 0)
                in_projection(k, 1, 1)
                beside(7)
                in_projection(k, 1, 2)
                in_projection(k, 1, 3)
                beside(8)
                step_sums(k, 0)
                beside(9)
                in_projection(k, 1, 4)
                decayed_b(k, 0)
                beside(10)
                in_projection(k, 1, 5)
                decayed_c_start(k, 0)
                spread_c(k, 0)
                beside(11)
                decayed_c_block(k, 0)
                in_projection(k, 1, 6)
                off_diagonal(k, 0)
                state_inputs(k, 0)
                beside(12)
                x_projection(k, 1)
                beside(13)
                beside(14)
                ssm_output(k, 0)
                tokens_first(k, 1)
                xd_tokens_first(k, 1)
                out_projection(k, 0, 0)
                out_projection(k, 0, 1)
                beside(15)
                step_sums(k, 1)
                beside(16)
                decayed_b(k, 1)
                in_projection(k, 1, 7)
                transposes(k, "ln2T", 0, xn2, norm2)
                decayed_c_start(k, 1)
                decayed_c_block(k, 1)
                state_inputs(k, 1)

            def second_half(k, last=False):
                ffn(k, 0, 0, 2)
                spread_c(k, 1)
                off_diagonal(k, 1)
                ffn(k, 0, 2, 4)
                ssm_output(k, 1)
                ffn(k, 0, 4, 5)
                out_projection(k, 1, 0)
                out_projection(k, 1, 1)
                ffn(k, 0, 5, HB)
                transposes(k, "ln2T", 1, xn2, norm2)
                down(k, 0, HB - 2)
                down(k, 0, HB - 1)
                ffn(k, 1, 0, HB)
                if not last:
                    transposes(k + 1, "ln1T", 0, xn1[0], norm1)
                down(k, 1, HB - 2)
                down(k, 1, HB - 1)

            prepare(0)
            transposes(1, "ln1T", 0, xn1[0], norm1)
            prepare(1)
            for m in range(MB):
                wait_taken(pe, ("w_in", m, 0))
            first_half(1, prepare)
            with pe.Fori(1, TILES) as k:
                second_half(k)
                first_half(k + 1)
            second_half(TILES, last=True)

        @block.scalar
        def _(act):
            act.dma_start(raw_in[:, 0:4, :], in_proj_w[0:DI, :].rearrange("(e p) d -> p e d", p=P)).then_inc(in_loaded[0], 16)
            act.dma_start(raw_in[:, 4:8, :], in_proj_w[DI:2 * DI, :].rearrange("(e p) d -> p e d", p=P)).then_inc(in_loaded[1], 16)
            start(act, by_scalar)

            def receive(product):
                name, i, h = product
                bank = bank_for(product)
                act.wait_ge(made, number[product] + 1)
                if name in ("w_in", "w_up", "w_down"):
                    if name == "w_in":
                        target = w_in[0][:, i, h * 512:(h + 1) * 512]
                    elif name == "w_up":
                        target = w_up[0][:, i, h * 512:(h + 1) * 512]
                    else:
                        target = w_down[0][:, 2 * i:2 * i + 2, 0:DM]
                    act.activation(target, bank, ACT.Copy).then_inc(highs, 1)
                    return
                if name == "w_x":
                    ins = act.activation(w_x[:, :, :].rearrange(flat), bank[:, 0:CB * XD], ACT.Copy)
                elif name == "w_out":
                    ins = act.activation(w_out[:, 2 * i:2 * i + 2, :].rearrange(flat), bank, ACT.Copy)
                elif name == "wexpT":
                    ins = act.activation(wexpT[:, 2 * i:2 * i + 2, 0:DM], bank.rearrange("p (g m) -> p g m", m=DM), ACT.Copy)
                elif name == "low":
                    target = take_low(i, h)
                    width = 512 if h < 3 else low_at[LOW] - low_at[2]
                    ins = act.activation(target, bank[:, 0:width], ACT.Copy)
                elif name == "pathT":
                    ins = act.activation(pathT[:, 4 * i:4 * i + 4, :].rearrange(flat), bank, ACT.Copy)
                else:
                    ins = act.activation(mixed[:, i, :], bank[:, 0:W1], ACT.Copy)
                ins.then_inc(taken[number[product] % 2], 1)

            def scale_blocks(n):
                if n == 0:
                    for g in range(HB - 2, HB):
                        wait_taken(act, ("up_low", g, 0))
                stage, source, target = MIXES[UP][n]
                for g, low, _, weight, _ in mixing(UP, stage):
                    if n:
                        wait_mixed(act, UP, n - 1, *needed_for_first_term(UP, n, g, low))
                    act.activation(target[:, g, :], source[:, low, :], ACT.Copy, scale=weight).then_inc(scaled[UP], 1)

            def prepare(step):
                for product in steps[step]:
                    receive(product)

            def take(k, name, i, b, out_ap, in_ap, last=True, **how):
                written(act, k, name, i, b)
                how.setdefault("func", ACT.Copy)
                ins = act.activation(out_ap, in_ap, how.pop("func"), **how)
                if last:
                    mark_read(ins, name, i, b)
                return ins

            def high_parts(k, name, b, last_use):
                written(act, k, *last_use)
                for m in range(MB):
                    take(k, name, m, b, xnT[0][:, m, :], tile_of(name, m, b)[:, :])

            def place_halo(k, b):
                act.wait_ge(convolved.handle, convolved.value(k, b, CB, ago=1))
                act.wait_ge(halo_saved.handle, halo_saved.value(k, b, 1, ago=1))
                act.activation(xi[:, :, 0:HALO], halo[b][:, :, :], ACT.Copy).then_inc(halo_moved.handle, 1)
                act.wait_ge(halo_moved.handle, halo_moved.value(k, b, 1))

            def save_halo(k, b):
                act.wait_ge(xi_copied.handle, xi_copied.value(k, b, CB))
                act.activation(halo[b][:, :, :], xi[:, :, TILE:TILE + HALO], ACT.Copy).then_inc(halo_saved.handle, 1)

            def first_tap(k, b, e):
                bank = tile_of("in", e, b)
                if e == 0:
                    act.wait_ge(gated.handle, gated.value(k, b, CB, ago=2))
                    written(act, k, "xtok", GR - 1, b, ago=2)
                take(k, "in", e, b, xi[:, e, HALO:], bank[:, :], last=False).then_inc(xi_copied.handle, 1)
                mark_read(act.activation(xc[b][:, e, :], bank[:, :], ACT.Identity, bias=tap_bias[:, e:e + 1],
                                         scale=taps[:, e, TAPS - 1:TAPS]), "in", e, b)

            def copy_z(k, b, e):
                take(k, "in", e, b, z[b][:, e - CB, :], tile_of("in", e, b)[:, :])

            def silu_x(k, b):
                for e in range(CB):
                    act.wait_ge(convolved.handle, convolved.value(k, b, e + 1))
                    act.activation(xc[b][:, e, :], xc[b][:, e, :], ACT.Silu).then_inc(xc_ready.handle, 1)

            def silu_z(k, b):
                read(act, k, "in", 7, b)
                act.activation(z[b][:, :, :], z[b][:, :, :], ACT.Silu).then_inc(z_ready.handle, 1)

            def take_xd(k, b):
                written(act, k, "xdtok", 0, b, ago=1)
                take(k, "xp", 0, b, xdT[0:XD, :], tile_of("xp", 0, b)[0:XD, :])

            def take_x_tok(k, b, c):
                if c == 0:
                    written(act, k, "y", CB - 1, b, ago=1)
                take(k, "xtok", c, b, x_tok[:, c, :], tile_of("xtok", c, b)[:, :])

            def load_exp_table():
                act.activation(exp_of_one[:, :], ones[:, 0:1], ACT.Exp)

            def exp_abs(k, b):
                act.wait_ge(abs_ready.handle, abs_ready.value(k, b, 1))
                act.activation(soft[:, 1, :], soft[:, 0, :], ACT.Exp, scale=-1.0).then_inc(exp_ready.handle, 1)

            def exp_sums(k, b):
                act.wait_ge(sums_ready.handle, sums_ready.value(k, b, 1))
                act.activation(decays[:, :, :, :].rearrange("p a c n -> p (a c n)"),
                               sums_A[:, :, :].rearrange(flat), ACT.Exp).then_inc(decays_ready.handle, 1)
                read(act, k, "u", 0, b, ago=1)
                act.activation(group_decay[:, :], group_sum[:, :], ACT.Exp).then_inc(group_decay_ready.handle, 1)

            def exp_gaps(k, b):
                written(act, k, "moff", 0, b, ago=1)
                take(k, "gap", 0, b, b_hat[:, :], tile_of("gap", 0, b)[:, :], func=ACT.Exp)

            def take_c_start(k, b):
                written(act, k, "y", CB - 1, b, ago=1)
                take(k, "ct", 0, b, c_startT[:, :], tile_of("ct", 0, b)[:, :])

            def take_c_block(k, b):
                written(act, k, "moff", 0, b, ago=1)
                take(k, "cbd", 0, b, c_hat[:, :], tile_of("cbd", 0, b)[:, :])

            def copy_first_state(k, b):
                read(act, k, "u", 0, b, ago=2)
                written(act, k, "y", CB - 1, b, ago=2)
                act.activation(state[b][0:NS, :], state_end[b][:, :], ACT.Copy).then_inc(first_state.handle, 1)

            def exp_diagonal(k, b):
                act.wait_ge(diag_gaps.handle, diag_gaps.value(k, b, 1))
                whole = diag[:, :, :, :].rearrange("p c n u -> p (c n u)")
                act.activation(whole, whole, ACT.Exp).then_inc(diag_exp.handle, 1)

            def gelu(k, b, j):
                if j >= HRING:
                    act.wait_ge(down_steps.handle, down_steps.value(k, b, j - HRING + 1))
                elif j == HRING - 1:
                    written(act, k, "down", 0, b, ago=1)
                else:
                    act.wait_ge(down_steps.handle, down_steps.value(k, b, HB - 1, ago=1))
                take(k, "up", j, b, hid_f32[:, j % HRING, :], tile_of("up", j, b)[:, :], func=ACT.Gelu,
                     bias=bias_up[:, j:j + 1])
                read(act, k, "up", j, b)
                act.activation(hid[0][:, j % HRING, :], hid_f32[:, j % HRING, :], ACT.Copy).then_inc(hid_high.handle, 1)

            def first_half(k, beside=lambda step: None, scale=lambda n: None):
                place_halo(k, 0)
                first_tap(k, 0, 0)
                first_tap(k, 0, 1)
                beside(2)
                first_tap(k, 0, 2)
                first_tap(k, 0, 3)
                save_halo(k, 0)
                beside(3)
                copy_z(k, 0, 4)
                copy_z(k, 0, 5)
                beside(4)
                silu_x(k, 0)
                copy_z(k, 0, 6)
                copy_z(k, 0, 7)
                beside(5)
                high_parts(k, "ln1T", 1, ("in", 7, 0))
                take_xd(k, 0)
                take_x_tok(k, 0, 0)
                take_x_tok(k, 0, 1)
                load_exp_table()
                beside(6)
                exp_abs(k, 0)
                place_halo(k, 1)
                first_tap(k, 1, 0)
                first_tap(k, 1, 1)
                beside(7)
                first_tap(k, 1, 2)
                first_tap(k, 1, 3)
                save_halo(k, 1)
                beside(8)
                exp_sums(k, 0)
                beside(9)
                copy_z(k, 1, 4)
                exp_gaps(k, 0)
                beside(10)
                copy_z(k, 1, 5)
                exp_diagonal(k, 0)
                beside(11)
                take_c_start(k, 0)
                take_c_block(k, 0)
                copy_z(k, 1, 6)
                copy_first_state(k, 0)
                beside(12)
                silu_x(k, 1)
                silu_z(k, 0)
                beside(13)
                beside(14)
                scale(0)
                scale(1)
                take_xd(k, 1)
                scale(2)
                load_exp_table()
                take_x_tok(k, 1, 0)
                take_x_tok(k, 1, 1)
                exp_abs(k, 1)
                beside(15)
                exp_sums(k, 1)
                beside(16)
                exp_gaps(k, 1)
                copy_z(k, 1, 7)
                high_parts(k, "ln2T", 0, ("in", 7, 1))
                exp_diagonal(k, 1)
                take_c_start(k, 1)
                take_c_block(k, 1)
                copy_first_state(k, 1)

            def second_half(k, last=False):
                silu_z(k, 1)
                for j in range(HB):
                    gelu(k, 0, j)
                high_parts(k, "ln2T", 1, ("up", 7, 0))
                for j in range(HB):
                    gelu(k, 1, j)
                if not last:
                    high_parts(k + 1, "ln1T", 0, ("up", 7, 0, 1))

            prepare(0)
            high_parts(1, "ln1T", 0, ("up", 7, 0, 1))
            prepare(1)
            act.wait_ge(conv_loaded, 16 * CONV_LOADS)
            act.activation(rates[:, :], rates[:, :], ACT.Exp).then_inc(rates_exp, 1)
            act.wait_ge(zeroed, 1)
            act.wait_ge(masks_made, 2)
            first_half(1, prepare, scale_blocks)
            with act.Fori(1, TILES) as k:
                second_half(k)
                first_half(k + 1)
            second_half(TILES, last=True)

        @block.vector
        def _(dve):
            done = [0]

            def link_setup(ins):
                done[0] += 1
                ins.then_inc(vector_setup, 1)
                dve.wait_ge(vector_setup, done[0])

            def group_stats(source, groups):
                for c in groups:
                    ins = dve.bn_stats(stats[:, c, :], source[:, c, :])
                return ins

            def norm_stats(k, b, slot, source, var, link, groups=range(GR)):
                link(group_stats(source, groups))
                dve.memset(carrier[:, :], 0.0)
                for c in range(GR):
                    ins = dve.bn_aggr(mean_var[:, c, :], stats[:, c, :])
                link(ins)
                dve.tensor_scalar(var_eps[:, slot, :], mean_var[:, :, 1], EPS, None, ALU.add).then_inc(var.handle, 1)

            def normalise(k, b, slot, source, target, ready, normed):
                dve.wait_ge(ready.handle, ready.value(k, b, 1))
                for c in range(GR):
                    dve.tensor_scalar(target[:, c, :], source[:, c, :], mean_var[:, c, 0:1],
                                      rstd[:, slot, c:c + 1], ALU.subtract, ALU.mult).then_inc(normed.handle, 1)

            start(dve, by_vector)
            for banks in (WIDE, SMALL, ACC):
                for handle, total in zip(banks.read, banks.takes):
                    dve.sem_inc(handle, total)

            high_count = [0]

            def low_part(product, low, high):
                high_count[0] += 1
                dve.wait_ge(highs, high_count[0])
                dve.tensor_tensor(low, bank_for(product), high.bitcast(F32), ALU.subtract)\
                    .then_inc(taken[number[product] % 2], 1)

            def low_of_in(h):
                for m in range(MB):
                    low_part(("w_in", m, h), *(w_in[part][:, m, h * 512:(h + 1) * 512] for part in (1, 0)))

            def constants():
                dve.wait_ge(masks_made, 2)
                dve.wait_ge(rates_exp, 1)
                dve.tensor_reduce(row_in_block[:, :], ident[:, :].rearrange("p (j u) -> p u j", u=BL), AXIS_X, ALU.add)
                dve.tensor_tensor(m_mat[:, 0:P], block_upto[:, :], ident[:, :], ALU.subtract)
                link_setup(dve.tensor_scalar(rates[:, :], rates[:, :], -1.0, None, ALU.mult))
                dve.tensor_reduce(later_in_block[:, :], m_mat[:, 0:P].rearrange("p (j u) -> p u j", u=BL), AXIS_X, ALU.add)
                dve.wait_ge(s_loaded, 16 * SMALL_LOADS)
                dve.tensor_tensor(bias_out[:, :], bias_raw[:, 0, :], bias_raw[:, 1, :], ALU.add)
                link_setup(dve.tensor_tensor(rate_before[:, :, :], before_block[:, :].unsqueeze(2).to_broadcast([P, NB, NS]),
                                       rates[:, :].unsqueeze(1).to_broadcast([P, NB, NS]), ALU.mult))
                dve.wait_ge(zeroed, 2)

            def add_blocks(i, n):
                stage, source, target = MIXES[i][n]
                for g, _, high, _, weight in mixing(i, stage):
                    dve.wait_ge(scaled[i], scaled_by(i, n, g))
                    if n:
                        wait_mixed(dve, i, n - 1, high)
                    dve.scalar_tensor_tensor(target[:, g, :], source[:, high, :], weight, target[:, g, :],
                                             ALU.mult, ALU.add).then_inc(mixed_up[i], 1)
                if n == HIGH - 1:
                    wait_mixed(dve, i, n, HB - 1)
                if (i, n) == (UP, HIGH - 1):
                    dve.tensor_tensor(bias_up[:, :], wexpT[:, :, DM], up_bias_sb[:, :], ALU.add)

            def low_of_ffn(*chosen):
                for name, i, h in chosen:
                    if name == "w_up":
                        low_part((name, i, h), *(w_up[part][:, i, h * 512:(h + 1) * 512] for part in (1, 0)))
                    else:
                        low_part((name, i, h), *(w_down[part][:, 2 * i:2 * i + 2, 0:DM] for part in (1, 0)))

            start(dve, [vector_steps])

            def convolve(k, b, e, chosen=range(TAPS - 2, -1, -1)):
                read(dve, k, "in", e, b)
                for tap in chosen:
                    ins = dve.scalar_tensor_tensor(xc[b][:, e, :], xi[:, e, tap:tap + TILE], taps[:, e, tap:tap + 1],
                                                   xc[b][:, e, :], ALU.mult, ALU.add)
                    if tap:
                        link(ins)
                    else:
                        ins.then_inc(convolved.handle, 1)

            def low_parts(k, name, b):
                for m in range(MB):
                    read(dve, k, name, m, b, takes=1)
                    mark_read(dve.tensor_tensor(xnT[1][:, m, :], tile_of(name, m, b)[:, :],
                                                xnT[0][:, m, :].bitcast(F32), ALU.subtract), name, m, b)

            def low_hidden(k, b, *blocks):
                for j in blocks:
                    dve.wait_ge(hid_high.handle, hid_high.value(k, b, j + 1))
                    dve.tensor_tensor(hid[1][:, j % HRING, :], hid_f32[:, j % HRING, :],
                                      hid[0][:, j % HRING, :].bitcast(F32), ALU.subtract).then_inc(hid_ready.handle, 1)

            def take_x_tok(k, b, c):
                written(dve, k, "y", CB - 1, b, ago=1)
                written(dve, k, "xtok", c, b)
                mark_read(dve.tensor_copy(x_tok[:, c, :], tile_of("xtok", c, b)[:, :]), "xtok", c, b)

            def take_xd(k, b):
                dve.wait_ge(c_placed.handle, c_placed.value(k, b, 1, ago=1))
                written(dve, k, "xdtok", 0, b)
                mark_read(dve.tensor_copy(xd[:, :, :], tile_of("xdtok", 0, b)[:, :]
                                          .rearrange("p (c w) -> p c w", w=P)[:, :, 0:XD]), "xdtok", 0, b)
                read(dve, k, "xdtok", 0, b)
                dve.scalar_tensor_tensor(soft[:, 0, :], xd[:, :, 0], -1.0, xd[:, :, 0], ALU.mult, ALU.max)\
                    .then_inc(abs_ready.handle, 1)

            def softplus(k, b):
                den, inv, q, sq, p, log_half, relu = (soft[:, n, :] for n in range(2, 9))
                dve.wait_ge(exp_ready.handle, exp_ready.value(k, b, 1))
                link(dve.tensor_scalar(den, soft[:, 1, :], 2.0, None, ALU.add))
                link(dve.reciprocal(inv, den))
                link(dve.tensor_tensor(q, soft[:, 1, :], inv, ALU.mult))
                link(dve.tensor_tensor(sq, q, q, ALU.mult))
                link(dve.tensor_scalar(p, sq, 1 / 13, None, ALU.mult))
                for c in ATANH:
                    link(dve.scalar_tensor_tensor(p, p, c, sq, ALU.add, ALU.mult))
                dve.tensor_scalar(relu, xd[:, :, 0], 0.0, None, ALU.max)
                link(dve.scalar_tensor_tensor(log_half, p, 1.0, q, ALU.add, ALU.mult))
                written(dve, k, "sums", 0, b, ago=1)
                dve.wait_ge(gap_w_ready.handle, gap_w_ready.value(k, b, 1, ago=1))
                link(dve.scalar_tensor_tensor(delta[:, :], log_half, 2.0, relu, ALU.mult, ALU.add))
                dve.wait_ge(diag_times_b.handle, diag_times_b.value(k, b, 1, ago=1))
                dve.tensor_tensor(dB[:, :, :], xd[:, :, 1:1 + NS], delta[:, :].unsqueeze(2).to_broadcast([P, GR, NS]),
                                  ALU.mult).then_inc(dB_ready.handle, 1)
                dve.tensor_tensor(dA[:, :, 0:NS], rates[:, :].unsqueeze(1).to_broadcast([P, GR, NS]),
                                  delta[:, :].unsqueeze(2).to_broadcast([P, GR, NS]), ALU.mult)
                dve.tensor_tensor(d_place[:, :, :], row_in_block[:, :].unsqueeze(1).to_broadcast([P, GR, BL]),
                                  delta[:, :].unsqueeze(2).to_broadcast([P, GR, BL]), ALU.mult)\
                    .then_inc(delta_ready.handle, 1)

            def take_sums(k, b):
                bank = tile_of("sums", 0, b)
                written(dve, k, "sums", 0, b)
                dve.wait_ge(group_decay_ready.handle, group_decay_ready.value(k, b, 1, ago=1))
                dve.tensor_copy(group_sum[:, :], bank[:, 12:13])
                dve.tensor_tensor(sums_A[:, :, :], bank[:, 0:3 * GR].unsqueeze(2).to_broadcast([P, 3 * GR, NS]),
                                  rates[:, :].unsqueeze(1).to_broadcast([P, 3 * GR, NS]), ALU.mult)\
                    .then_inc(sums_ready.handle, 1)
                mark_read(dve.tensor_tensor(d_block[:, :, :], bank[:, 16:16 + GR * BL].rearrange("p (c u) -> p c u", u=BL),
                                            later_in_block[:, :].unsqueeze(1).to_broadcast([P, GR, BL]), ALU.mult),
                          "sums", 0, b)
                read(dve, k, "sums", 0, b)
                dve.wait_ge(diag_gaps.handle, diag_gaps.value(k, b, 1, ago=1))
                dve.tensor_tensor_scan(gaps[:, :, :].rearrange(flat), restart[:, :, :].rearrange(flat),
                                       d_block[:, :, :].rearrange(flat), 0.0, ALU.mult, ALU.add)\
                    .then_inc(gaps_ready.handle, 1)

            def weigh(k, b):
                dve.wait_ge(decays_ready.handle, decays_ready.value(k, b, 1))
                c_tok = xd[:, :, 1 + NS:XD]
                written(dve, k, "ct", 0, b, ago=1)
                dve.tensor_tensor(c_start[:, :, 0:NS], c_tok, decays[:, 0, :, :], ALU.mult)\
                    .then_inc(c_start_ready.handle, 1)
                dve.wait_ge(cbd_ready.handle, cbd_ready.value(k, b, 1, ago=1))
                dve.tensor_tensor(c_block[:, :, :], c_tok, decays[:, 1, :, :], ALU.mult).then_inc(c_block_ready.handle, 1)
                written(dve, k, "u", 0, b, ago=1)
                dve.tensor_tensor(b_end[:, :, :], dB[:, :, :], decays[:, 2, :, :], ALU.mult)\
                    .then_inc(b_end_ready.handle, 1)

            def weigh_b(k, b):
                written(dve, k, "bd", 0, b)
                read(dve, k, "gap", 0, b)
                mark_read(dve.tensor_tensor(b_hat[:, :], b_hat[:, :], tile_of("bd", 0, b)[:, :], ALU.mult), "bd", 0, b)

            def advance_state(k, b):
                bank = tile_of("u", 0, b)
                dve.wait_ge(group_decay_ready.handle, group_decay_ready.value(k, b, 1))
                written(dve, k, "u", 0, b)
                written(dve, k, "y", CB - 1, b, ago=2)
                dve.wait_ge(first_state.handle, first_state.value(k, b, 1))
                for c in range(GR):
                    at = SLOT * c
                    before = state_end[b][:, :] if c == 0 else state[b][at:at + NS, :]
                    to = state_end[b][:, :] if c == GR - 1 else state[b][at + SLOT:at + SLOT + NS, :]
                    ins = dve.scalar_tensor_tensor(to, before, group_decay[at:at + NS, :], bank[at:at + NS, :],
                                                   ALU.mult, ALU.add)
                    if c == GR - 1:
                        mark_read(ins, "u", 0, b)
                    elif c == GR - 2:
                        ins.then_inc(states_ready.handle, 1)
                        dve.wait_ge(states_ready.handle, states_ready.value(k, b, 1))
                    else:
                        link(ins)

            def diagonal_times_c(k, b, h):
                if h == 0:
                    dve.wait_ge(diag_times_b.handle, diag_times_b.value(k, b, 1))
                written(dve, k, "cb", h, b)
                part = diag[:, 2 * h:2 * h + 2, :, :].rearrange("p c n u -> p (c n u)")
                mark_read(dve.tensor_tensor(part, part, tile_of("cb", h, b)[:, :], ALU.mult), "cb", h, b)

            def sum_diagonal(k, b):
                for h in range(2):
                    read(dve, k, "cb", h, b)
                dve.tensor_reduce(diag_sum[:, :, :], diag[:, :, :, :].rearrange("p c n u -> p c u n"), AXIS_X, ALU.add)\
                    .then_inc(diag_summed.handle, 1)
                dve.wait_ge(diag_summed.handle, diag_summed.value(k, b, 1))

            def assemble(k, b):
                written(dve, k, "y", CB - 1, b, ago=1)
                link(dve.tensor_tensor(m_mat[:, :].rearrange("p (c j u) -> p c j u", j=NB, u=BL),
                                       diag_sum[:, :, :].unsqueeze(2).to_broadcast([P, GR, NB, BL]),
                                       block_upto[:, :].rearrange("p (j u) -> p j u", u=BL).unsqueeze(1)
                                       .to_broadcast([P, GR, NB, BL]), ALU.mult))
                written(dve, k, "moff", 0, b)
                mark_read(dve.tensor_tensor(m_mat[:, :], m_mat[:, :], tile_of("moff", 0, b)[:, :], ALU.add), "moff", 0, b)

            def gate(k, b, g):
                if g == 0:
                    written(dve, k, "out", 1, b, ago=1)
                    dve.wait_ge(z_ready.handle, z_ready.value(k, b, 1))
                written(dve, k, "y", g, b)
                mark_read(dve.scalar_tensor_tensor(yg[:, g, :], xc[b][:, g, :], skip[:, g:g + 1],
                                                   tile_of("y", g, b)[:, :], ALU.mult, ALU.add), "y", g, b)
                read(dve, k, "y", g, b)
                dve.tensor_tensor(yg[:, g, :], yg[:, g, :], z[b][:, g, :], ALU.mult).then_inc(gated.handle, 1)

            def first_residual(k, b, h):
                if h == 0:
                    dve.wait_ge(x1b_ready.handle, x1b_ready.value(k, b, 1, ago=1))
                written(dve, k, "out", h, b)
                mark_read(dve.tensor_tensor(x1[:, 2 * h:2 * h + 2, :],
                                            tile_of("out", h, b)[:, :].rearrange("p (c d) -> p c d", d=DM),
                                            x_in[b][:, 2 * h:2 * h + 2, :], ALU.add), "out", h, b)
                read(dve, k, "out", h, b)
                if h == 0:
                    group_stats(x1, range(2))

            def second_stats(k, b):
                norm_stats(k, b, BATCH + b, x1, var2, link, range(2, GR))

            def second_normalise(k, b):
                written(dve, k, "ln2T", MB - 1, b, ago=1)
                normalise(k, b, BATCH + b, x1, xn2, rstd2, norm2)

            def first_stats(k, b, loaded):
                dve.wait_ge(x_loaded[b], loaded)
                dve.wait_ge(norm2.handle, norm2.value(k, 1, GR))
                dve.wait_ge(norm1.handle, norm1.value(k + 1, b, 0))
                norm_stats(k + 1, b, b, x_in[b], var1, link)

            def first_normalise(k, b):
                written(dve, k, "ln1T", MB - 1, b)
                normalise(k + 1, b, b, x_in[b], xn1[b], rstd1, norm1)

            def final(k, b):
                dve.wait_ge(x1b_ready.handle, x1b_ready.value(k, b, 1))
                written(dve, k, "down", 0, b)
                mark_read(dve.tensor_tensor(x1b, acc[:, :, :], x1b, ALU.add), "down", 0, b)

            at = [None, 0]

            def link(ins):
                at[1] += 1
                ins.then_inc(vector_steps.handle, 1)
                dve.wait_ge(vector_steps.handle, vector_steps.value(at[0], 0, at[1]))

            def first_half(k, add=lambda i, n: None, weights_in_parts=lambda *products: None):
                at[:] = [k, 0]
                for e in range(CB):
                    convolve(k, 0, e)
                low_parts(k, "ln1T", 1)
                take_x_tok(k, 0, 2)
                take_x_tok(k, 0, 3)
                take_xd(k, 0)
                softplus(k, 0)
                convolve(k, 1, 0)
                take_sums(k, 0)
                convolve(k, 1, 1)
                weigh(k, 0)
                weigh_b(k, 0)
                convolve(k, 1, 2)
                diagonal_times_c(k, 0, 0)
                diagonal_times_c(k, 0, 1)
                convolve(k, 1, 3)
                sum_diagonal(k, 0)
                assemble(k, 0)
                advance_state(k, 0)
                add(DOWN, 0)
                add(UP, 0)
                for g in range(CB):
                    gate(k, 0, g)
                    if g == 1:
                        add(UP, 1)
                        add(DOWN, 1)
                add(UP, 2)
                take_x_tok(k, 1, 2)
                take_x_tok(k, 1, 3)
                take_xd(k, 1)
                add(DOWN, 2)
                softplus(k, 1)
                weights_in_parts(("w_up", 0, 0), ("w_up", 0, 1), ("w_up", 1, 0), ("w_up", 1, 1))
                first_residual(k, 0, 0)
                first_residual(k, 0, 1)
                second_stats(k, 0)
                take_sums(k, 1)
                weights_in_parts(*(("w_down", q, 0) for q in range(4)))
                weigh(k, 1)
                second_normalise(k, 0)
                weigh_b(k, 1)
                low_parts(k, "ln2T", 0)
                assert at[1] == FIRST_HALF_STEPS, at[1]

            def second_half(k, last=False):
                at[:] = [k, FIRST_HALF_STEPS]
                advance_state(k, 1)
                diagonal_times_c(k, 1, 0)
                low_hidden(k, 0, 0)
                diagonal_times_c(k, 1, 1)
                sum_diagonal(k, 1)
                low_hidden(k, 0, 1)
                assemble(k, 1)
                low_hidden(k, 0, 2, 3)
                for g in range(CB):
                    gate(k, 1, g)
                low_hidden(k, 0, 4)
                first_residual(k, 1, 0)
                first_residual(k, 1, 1)
                second_stats(k, 1)
                second_normalise(k, 1)
                low_hidden(k, 0, 5, 6, 7)
                low_parts(k, "ln2T", 1)
                final(k, 0)
                low_hidden(k, 1, 0, 1)
                for b in range(BATCH):
                    if not last:
                        first_stats(k, b, k * 16 + 16)
                    low_hidden(k, 1, 2 * b + 2)
                    if not last:
                        first_normalise(k, b)
                    low_hidden(k, 1, 2 * b + 3)
                low_hidden(k, 1, 6, 7)
                if not last:
                    low_parts(k + 1, "ln1T", 0)
                final(k, 1)
                assert last or at[1] == VECTOR_STEPS, at[1]

            def norm_of_first(b):
                dve.wait_ge(x_loaded[b], 16)
                norm_stats(1, b, b, x_in[b], var1, link_setup)
                normalise(1, b, b, x_in[b], xn1[b], rstd1, norm1)
                dve.wait_ge(norm1.handle, norm1.value(1, b, GR))

            norm_of_first(0)
            low_of_in(0)
            low_parts(1, "ln1T", 0)
            low_of_in(1)
            norm_of_first(1)
            constants()
            first_half(1, add_blocks, low_of_ffn)
            with dve.Fori(1, TILES) as k:
                second_half(k)
                first_half(k + 1)
            second_half(TILES, last=True)


_INS = ["L0_attn_x", "L0_attn_in_proj_w", "L0_attn_conv_w", "L0_attn_conv_b", "L0_attn_x_proj_w", "L0_attn_A_log",
        "L0_attn_D", "L0_attn_out_proj_w", "L0_ffn_W_exp", "L0_ffn_b_exp", "L0_ffn_up_weights", "L0_ffn_up_bias",
        "L0_ffn_down_weights", "L0_ffn_W_con", "L0_ffn_b_con", "L0_ffn_down_bias"]
_OUT = ((BATCH, LENGTH, DM), "float32")


def kernel(**inputs):
    import numpy as _np
    import concourse.bacc as _bacc
    from concourse import mybir as _mybir
    from concourse.bass_utils import run_bass_kernel_spmd as _run

    nc = _bacc.Bacc("TRN2", target_bir_lowering=False, num_devices=1)
    arrays, args = {}, []
    for name in _INS:
        a = _np.ascontiguousarray(inputs[name])
        arrays[f"in_{name}_dram"] = a
        args.append(nc.dram_tensor(f"in_{name}_dram", a.shape, _mybir.dt.from_np(a.dtype), kind="ExternalInput").ap())
    shape, dtype = _OUT
    args.append(nc.dram_tensor("out_dram", shape, _mybir.dt.from_np(_np.dtype(dtype)), kind="ExternalOutput").ap())
    bass_preln_ssm_butterfly_ffn(nc, *args)
    r = _run(nc, [arrays], core_ids=[0])
    return r.results[0]["out_dram"]
```
